# Optimizing a Trainium2 kernel written in Bass

```python
import numpy as np
import jax
import jax.numpy as jnp

def _softmax(x, axis=-1):
    return jax.nn.softmax(x, axis=axis)

def _gelu(x):
    return jax.nn.gelu(x, approximate=True)

def _silu(x):
    return jax.nn.silu(x)

def _sigmoid(x):
    return jax.nn.sigmoid(x)

def _layernorm(x, axis=-1, eps=1e-05):
    m = jnp.mean(x, axis=axis, keepdims=True)
    v = jnp.var(x, axis=axis, keepdims=True)
    return (x - m) / jnp.sqrt(v + eps)

def _scatter_add(tgt, idx, src, axis=0):
    return tgt.at[idx].add(src)

def _segment_sum(src, seg, n):
    return jax.ops.segment_sum(src, seg, n)
kernel_name = 'mk_seq_preln_d2_jaxref_r8_a40d96'

def setup_inputs(seed: int=0):
    np.random.seed(seed)
    _w = jnp.asarray

    def _L0_attn_setup():
        import jax, jax.numpy as jnp
        import numpy as np
        D = 128
        H = 16
        HD = D // H
        EPS = 1e-06

        def _rmsnorm(x, w):
            xf = x.astype(jnp.float32)
            var = jnp.mean(xf * xf, axis=-1, keepdims=True)
            return (w * (xf * jax.lax.rsqrt(var + EPS))).astype(x.dtype)
        key = jax.random.key(seed)
        ks = jax.random.split(key, 10)
        B, N = (2, 256)
        s = 0.02
        return {'x': jax.random.normal(ks[0], (B, N, D), jnp.float32), 'Wq': jax.random.normal(ks[1], (D, D + H), jnp.float32) * s, 'bq': jnp.zeros((D + H,), jnp.float32), 'Wk': jax.random.normal(ks[2], (D, D), jnp.float32) * s, 'bk': jnp.zeros((D,), jnp.float32), 'Wv': jax.random.normal(ks[3], (D, D), jnp.float32) * s, 'bv': jnp.zeros((D,), jnp.float32), 'Wo': jax.random.normal(ks[4], (D, D), jnp.float32) * s, 'bo': jnp.zeros((D,), jnp.float32), 'qn_w': jnp.ones((HD,), jnp.float32), 'kn_w': jnp.ones((HD,), jnp.float32)}
    _L0_attn_in = _L0_attn_setup()

    def _L0_ffn_setup():
        import jax, jax.numpy as jnp
        import numpy as np
        from jax import lax
        T, B, I, M, O = (32, 64, 128, 128, 128)

        def _xavier(key, shape):
            fan_out, fan_in = shape
            limit = float(np.sqrt(6.0 / (fan_in + fan_out)))
            return jax.random.uniform(key, shape, jnp.float32, -limit, limit)
        key = jax.random.key(seed)
        ks = jax.random.split(key, 9)
        x = jax.random.normal(ks[0], (T, B, I), jnp.float32)
        return {'x': x, 'wf': _xavier(ks[1], (M, I)), 'uf': _xavier(ks[2], (M, M)), 'bf': jnp.zeros((M,), jnp.float32), 'wi': _xavier(ks[3], (M, I)), 'ui': _xavier(ks[4], (M, M)), 'bi': jnp.zeros((M,), jnp.float32), 'wc': _xavier(ks[5], (M, I)), 'uc': _xavier(ks[6], (M, M)), 'bc': jnp.zeros((M,), jnp.float32), 'wo': _xavier(ks[7], (O, I)), 'uo': _xavier(ks[8], (O, M)), 'bo': jnp.zeros((O,), jnp.float32), 'in_c': jnp.zeros((M,), jnp.float32)}
    _L0_ffn_in = _L0_ffn_setup()

    def _L1_attn_setup():
        import jax, jax.numpy as jnp
        import numpy as np
        B, N, D = (4, 256, 128)
        H = 8
        DK = D // H
        DV = D // H
        DF = 2 * DK
        CHUNK = 64
        RMS_EPS = 1e-05

        def _hedgehog(x, w, b):
            y = jnp.einsum('bhnd,ed->bhne', x, w) + b
            return jnp.concatenate([jnp.exp(y), jnp.exp(-y)], axis=-1)

        def _fused_chunk_linear_attn(q, k, v):
            b, h, n, df = q.shape
            dv = v.shape[-1]
            nc = n // CHUNK

            def to_chunks(t):
                d = t.shape[-1]
                return t.reshape(b, h, nc, CHUNK, d).transpose(2, 0, 1, 3, 4)
            qc, kc, vc = (to_chunks(q), to_chunks(k), to_chunks(v))
            mask = jnp.tril(jnp.ones((CHUNK, CHUNK), dtype=bool))

            def step(S, inp):
                qi, ki, vi = inp
                attn = jnp.einsum('bhcd,bhed->bhce', qi, ki)
                attn = jnp.where(mask, attn, 0.0)
                intra = jnp.einsum('bhce,bhev->bhcv', attn, vi)
                inter = jnp.einsum('bhcd,bhdv->bhcv', qi, S)
                S = S + jnp.einsum('bhcd,bhcv->bhdv', ki, vi)
                return (S, intra + inter)
            S0 = jnp.zeros((b, h, df, dv), dtype=q.dtype)
            _, oc = jax.lax.scan(step, S0, (qc, kc, vc))
            return oc.transpose(1, 2, 0, 3, 4).reshape(b, h, n, dv)
        key = jax.random.key(seed)
        ks = jax.random.split(key, 10)
        s = D ** (-0.5)
        x = jax.random.normal(ks[0], (B, N, D), dtype=jnp.float32)
        Wq = jax.random.normal(ks[1], (D, D), dtype=jnp.float32) * s
        Wk = jax.random.normal(ks[2], (D, D), dtype=jnp.float32) * s
        Wv = jax.random.normal(ks[3], (D, D), dtype=jnp.float32) * s
        Wo = jax.random.normal(ks[4], (D, D), dtype=jnp.float32) * s
        eye = jnp.eye(DK, dtype=jnp.float32)
        fmq_w = eye + 0.02 * jax.random.normal(ks[5], (DK, DK), dtype=jnp.float32)
        fmq_b = 0.02 * jax.random.normal(ks[6], (DK,), dtype=jnp.float32)
        fmk_w = eye + 0.02 * jax.random.normal(ks[7], (DK, DK), dtype=jnp.float32)
        fmk_b = 0.02 * jax.random.normal(ks[8], (DK,), dtype=jnp.float32)
        rms_w = 1.0 + 0.1 * jax.random.normal(ks[9], (DV,), dtype=jnp.float32)
        return {'x': x, 'Wq': Wq, 'Wk': Wk, 'Wv': Wv, 'Wo': Wo, 'fmq_w': fmq_w, 'fmq_b': fmq_b, 'fmk_w': fmk_w, 'fmk_b': fmk_b, 'rms_w': rms_w}
    _L1_attn_in = _L1_attn_setup()

    def _L1_ffn_setup():
        import jax, jax.numpy as jnp
        import numpy as np
        TOP_K = 2
        key = jax.random.key(seed)
        ks = jax.random.split(key, 6)
        B, L, D, E, F = (2, 256, 128, 8, 512)
        x = jax.random.normal(ks[0], (B, L, D), dtype=jnp.float32)
        Wg = jax.random.normal(ks[1], (D, E), dtype=jnp.float32) * D ** (-0.5)
        W1 = jax.random.normal(ks[2], (E, D, F), dtype=jnp.float32) * D ** (-0.5)
        b1 = jnp.zeros((E, F), dtype=jnp.float32)
        W2 = jax.random.normal(ks[3], (E, F, D), dtype=jnp.float32) * F ** (-0.5)
        b2 = jnp.zeros((E, D), dtype=jnp.float32)
        return {'x': x, 'Wg': Wg, 'W1': W1, 'b1': b1, 'W2': W2, 'b2': b2}
    _L1_ffn_in = _L1_ffn_setup()
    _d = {'L0_attn_x': _L0_attn_in['x'], 'L0_attn_Wq': _L0_attn_in['Wq'], 'L0_attn_bq': _L0_attn_in['bq'], 'L0_attn_Wk': _L0_attn_in['Wk'], 'L0_attn_bk': _L0_attn_in['bk'], 'L0_attn_Wv': _L0_attn_in['Wv'], 'L0_attn_bv': _L0_attn_in['bv'], 'L0_attn_Wo': _L0_attn_in['Wo'], 'L0_attn_bo': _L0_attn_in['bo'], 'L0_attn_qn_w': _L0_attn_in['qn_w'], 'L0_attn_kn_w': _L0_attn_in['kn_w'], 'L0_ffn_wf': _L0_ffn_in['wf'], 'L0_ffn_uf': _L0_ffn_in['uf'], 'L0_ffn_bf': _L0_ffn_in['bf'], 'L0_ffn_wi': _L0_ffn_in['wi'], 'L0_ffn_ui': _L0_ffn_in['ui'], 'L0_ffn_bi': _L0_ffn_in['bi'], 'L0_ffn_wc': _L0_ffn_in['wc'], 'L0_ffn_uc': _L0_ffn_in['uc'], 'L0_ffn_bc': _L0_ffn_in['bc'], 'L0_ffn_wo': _L0_ffn_in['wo'], 'L0_ffn_uo': _L0_ffn_in['uo'], 'L0_ffn_bo': _L0_ffn_in['bo'], 'L0_ffn_in_c': _L0_ffn_in['in_c'], 'L1_attn_Wq': _L1_attn_in['Wq'], 'L1_attn_Wk': _L1_attn_in['Wk'], 'L1_attn_Wv': _L1_attn_in['Wv'], 'L1_attn_Wo': _L1_attn_in['Wo'], 'L1_attn_fmq_w': _L1_attn_in['fmq_w'], 'L1_attn_fmq_b': _L1_attn_in['fmq_b'], 'L1_attn_fmk_w': _L1_attn_in['fmk_w'], 'L1_attn_fmk_b': _L1_attn_in['fmk_b'], 'L1_attn_rms_w': _L1_attn_in['rms_w'], 'L1_ffn_Wg': _L1_ffn_in['Wg'], 'L1_ffn_W1': _L1_ffn_in['W1'], 'L1_ffn_b1': _L1_ffn_in['b1'], 'L1_ffn_W2': _L1_ffn_in['W2'], 'L1_ffn_b2': _L1_ffn_in['b2']}
    _x0 = _d['L0_attn_x']
    _d['L0_attn_x'] = jax.random.normal(jax.random.fold_in(jax.random.key(seed), 1), (4, 1024, 128), dtype=_x0.dtype)
    del _x0
    return _d

def reference(L0_attn_x, L0_attn_Wq, L0_attn_bq, L0_attn_Wk, L0_attn_bk, L0_attn_Wv, L0_attn_bv, L0_attn_Wo, L0_attn_bo, L0_attn_qn_w, L0_attn_kn_w, L0_ffn_wf, L0_ffn_uf, L0_ffn_bf, L0_ffn_wi, L0_ffn_ui, L0_ffn_bi, L0_ffn_wc, L0_ffn_uc, L0_ffn_bc, L0_ffn_wo, L0_ffn_uo, L0_ffn_bo, L0_ffn_in_c, L1_attn_Wq, L1_attn_Wk, L1_attn_Wv, L1_attn_Wo, L1_attn_fmq_w, L1_attn_fmq_b, L1_attn_fmk_w, L1_attn_fmk_b, L1_attn_rms_w, L1_ffn_Wg, L1_ffn_W1, L1_ffn_b1, L1_ffn_W2, L1_ffn_b2):

    def _L0_attn_ref(x, Wq, bq, Wk, bk, Wv, bv, Wo, bo, qn_w, kn_w):
        import jax, jax.numpy as jnp
        import numpy as np
        D = 128
        H = 16
        HD = D // H
        EPS = 1e-06

        def _rmsnorm(x, w):
            xf = x.astype(jnp.float32)
            var = jnp.mean(xf * xf, axis=-1, keepdims=True)
            return (w * (xf * jax.lax.rsqrt(var + EPS))).astype(x.dtype)
        B, N, _ = x.shape
        qg = x @ Wq + bq
        Q, gate = (qg[..., :D], qg[..., D:])
        K = x @ Wk + bk
        V = x @ Wv + bv
        Q = Q.reshape(B, N, H, HD).transpose(0, 2, 1, 3)
        K = K.reshape(B, N, H, HD).transpose(0, 2, 1, 3)
        V = V.reshape(B, N, H, HD).transpose(0, 2, 1, 3)
        Q = _rmsnorm(Q, qn_w)
        K = _rmsnorm(K, kn_w)
        scores = jnp.einsum('bhqd,bhkd->bhqk', Q, K) / jnp.sqrt(jnp.float32(HD))
        attn = jax.nn.softmax(scores.astype(jnp.float32), axis=-1).astype(Q.dtype)
        out = jnp.einsum('bhqk,bhkd->bhqd', attn, V)
        out = out.transpose(0, 2, 1, 3)
        out = out * jax.nn.sigmoid(gate)[..., None]
        out = out.reshape(B, N, D)
        return out @ Wo + bo

    def _L0_ffn_ref(x, wf, uf, bf, wi, ui, bi, wc, uc, bc, wo, uo, bo, in_c):
        import jax, jax.numpy as jnp
        import numpy as np
        from jax import lax
        T, B, I, M, O = (32, 64, 128, 128, 128)

        def _xavier(key, shape):
            fan_out, fan_in = shape
            limit = float(np.sqrt(6.0 / (fan_in + fan_out)))
            return jax.random.uniform(key, shape, jnp.float32, -limit, limit)
        batch = x.shape[1]
        c0 = jnp.broadcast_to(in_c, (batch, in_c.shape[0]))

        def step(c, xt):
            ft = jax.nn.sigmoid(xt @ wf.T + c @ uf.T + bf)
            it = jax.nn.sigmoid(xt @ wi.T + c @ ui.T + bi)
            gt = jnp.tanh(xt @ wc.T + c @ uc.T + bc)
            c = ft * c + it * gt
            return (c, None)
        c_final, _ = lax.scan(step, c0, x)
        h = jnp.tanh(jnp.einsum('tbi,oi->tbo', x, wo) + c_final @ uo.T + bo)
        return h

    def _L1_attn_ref(x, Wq, Wk, Wv, Wo, fmq_w, fmq_b, fmk_w, fmk_b, rms_w):
        import jax, jax.numpy as jnp
        import numpy as np
        B, N, D = (4, 256, 128)
        H = 8
        DK = D // H
        DV = D // H
        DF = 2 * DK
        CHUNK = 64
        RMS_EPS = 1e-05

        def _hedgehog(x, w, b):
            y = jnp.einsum('bhnd,ed->bhne', x, w) + b
            return jnp.concatenate([jnp.exp(y), jnp.exp(-y)], axis=-1)

        def _fused_chunk_linear_attn(q, k, v):
            b, h, n, df = q.shape
            dv = v.shape[-1]
            nc = n // CHUNK

            def to_chunks(t):
                d = t.shape[-1]
                return t.reshape(b, h, nc, CHUNK, d).transpose(2, 0, 1, 3, 4)
            qc, kc, vc = (to_chunks(q), to_chunks(k), to_chunks(v))
            mask = jnp.tril(jnp.ones((CHUNK, CHUNK), dtype=bool))

            def step(S, inp):
                qi, ki, vi = inp
                attn = jnp.einsum('bhcd,bhed->bhce', qi, ki)
                attn = jnp.where(mask, attn, 0.0)
                intra = jnp.einsum('bhce,bhev->bhcv', attn, vi)
                inter = jnp.einsum('bhcd,bhdv->bhcv', qi, S)
                S = S + jnp.einsum('bhcd,bhcv->bhdv', ki, vi)
                return (S, intra + inter)
            S0 = jnp.zeros((b, h, df, dv), dtype=q.dtype)
            _, oc = jax.lax.scan(step, S0, (qc, kc, vc))
            return oc.transpose(1, 2, 0, 3, 4).reshape(b, h, n, dv)
        b, n, d = x.shape
        split = lambda t: t.reshape(b, n, H, -1).transpose(0, 2, 1, 3)
        q = split(x @ Wq.T)
        k = split(x @ Wk.T)
        v = split(x @ Wv.T)
        q = _hedgehog(q, fmq_w, fmq_b)
        k = _hedgehog(k, fmk_w, fmk_b)
        scale = q.shape[-1] ** (-0.5)
        o = _fused_chunk_linear_attn(q * scale, k, v)
        o = o * jax.lax.rsqrt(jnp.mean(o * o, axis=-1, keepdims=True) + RMS_EPS) * rms_w
        o = o.transpose(0, 2, 1, 3).reshape(b, n, H * DV)
        return o @ Wo.T

    def _L1_ffn_ref(x, Wg, W1, b1, W2, b2):
        import jax, jax.numpy as jnp
        import numpy as np
        TOP_K = 2
        b, l, d = x.shape
        E = Wg.shape[1]
        xt = x.reshape(b * l, d)
        N = xt.shape[0]
        S = jax.nn.sigmoid(xt @ Wg)
        G, I = jax.lax.top_k(S, TOP_K)
        h = jax.nn.gelu(jnp.einsum('nd,edf->enf', xt, W1) + b1[:, None, :])
        y = jnp.einsum('enf,efd->end', h, W2) + b2[:, None, :]
        combine = jnp.zeros((N, E), dtype=x.dtype).at[jnp.arange(N)[:, None], I].add(G)
        out = jnp.einsum('ne,end->nd', combine, y)
        return out.reshape(b, l, d)
    x = L0_attn_x
    x = x + _L0_attn_ref(_layernorm(x, axis=-1), L0_attn_Wq, L0_attn_bq, L0_attn_Wk, L0_attn_bk, L0_attn_Wv, L0_attn_bv, L0_attn_Wo, L0_attn_bo, L0_attn_qn_w, L0_attn_kn_w)
    x = x + _L0_ffn_ref(_layernorm(x, axis=-1), L0_ffn_wf, L0_ffn_uf, L0_ffn_bf, L0_ffn_wi, L0_ffn_ui, L0_ffn_bi, L0_ffn_wc, L0_ffn_uc, L0_ffn_bc, L0_ffn_wo, L0_ffn_uo, L0_ffn_bo, L0_ffn_in_c)
    x = x + _L1_attn_ref(_layernorm(x, axis=-1), L1_attn_Wq, L1_attn_Wk, L1_attn_Wv, L1_attn_Wo, L1_attn_fmq_w, L1_attn_fmq_b, L1_attn_fmk_w, L1_attn_fmk_b, L1_attn_rms_w)
    x = x + _L1_ffn_ref(_layernorm(x, axis=-1), L1_ffn_Wg, L1_ffn_W1, L1_ffn_b1, L1_ffn_W2, L1_ffn_b2)
    return x

_drawn_inputs = setup_inputs


def setup_inputs(seed=0):
    import zlib

    import numpy as np

    out = dict(_drawn_inputs(seed))
    spreads = {'L0_attn_bq': (0.0, 0.271),
     'L0_attn_bk': (0.0, 2.0),
     'L0_attn_bv': (0.0, 0.1),
     'L0_attn_bo': (0.0, 0.1),
     'L0_attn_qn_w': (1.0, 0.6),
     'L0_attn_kn_w': (1.0, 0.6),
     'L0_ffn_bf': (0.0, 0.1),
     'L0_ffn_bi': (0.0, 0.1),
     'L0_ffn_bc': (0.0, 0.1),
     'L0_ffn_bo': (0.0, 0.1),
     'L0_ffn_in_c': (0.0, 0.1),
     'L1_ffn_b1': (0.0, 0.1),
     'L1_ffn_b2': (0.0, 0.1)}
    factors = {'L0_attn_Wq': 11.565,
     'L0_attn_Wk': 7.733,
     'L1_attn_fmq_b': 3.564,
     'L1_attn_fmk_b': 3.245,
     'L0_attn_Wv': 2.693}
    for name, (base, spread) in spreads.items():
        noise = np.random.default_rng([zlib.crc32(name.encode()), seed]).standard_normal(out[name].shape)
        drawn = base * np.exp(spread * noise) if base else spread * noise
        out[name] = jnp.asarray(drawn.astype(out[name].dtype))
    for name, factor in factors.items():
        out[name] = (out[name] * factor).astype(out[name].dtype)
    return out
```

```python
import math
from contextlib import ExitStack

import concourse.bass as bass
from concourse import mybir

F32 = mybir.dt.float32
BF16 = mybir.dt.bfloat16
I32 = mybir.dt.int32
ALU = mybir.AluOpType
ACT = mybir.ActivationFunctionType
AX_X = mybir.AxisListType.X

P = 128
D = 128
B, N = 4, 1024
TB = N // P
NT = B * TB
HT = TB // 2
HN = N // 2
LN_EPS = 1e-5

H0, HD = 16, 8
HG = 4
NG = H0 // HG
VW = 32
SPLITS = 3
COMBOS = SPLITS * SPLITS
KROWS = 96
W0 = 3 * D + H0
RMS0_EPS = 1e-6
SLOTS = 2 * 2 * TB
PROBS = 8
LOADS = 16 * 2 * COMBOS

H1, DK = 8, 16
DF = 2 * DK
G1 = 2
RMS1_EPS = 1e-5

E, F = 8, 512
FT = F // P
GATES_AT, TANH_AT = 10, (18, 23, 26)
NCONST = 5 * P + E * E + 1
RSQRT_MAGIC = float(0x5F3759DF)


class Steps:

    def __init__(self, eng, sem, base, per):
        self.eng, self.sem, self.base, self.per, self.n = eng, sem, base, per, 0

    def go(self, ins):
        self.n += 1
        ins.then_inc(self.sem, 1)

    def wait(self):
        self.eng.wait_ge(self.sem, self.base + self.n)

    def did(self, ins):
        self.go(ins)
        self.wait()

    def end(self):
        assert self.n == self.per, self.n


class Banks:

    def __init__(self, n):
        self.used, self.phases = [0] * n, {}

    def phase(self, name, first, count, jobs):
        base, place = list(self.used), {}
        for job, bank in jobs:
            self.used[bank] += 1
            place[job] = (bank, self.used[bank])
        per = [u - b for u, b in zip(self.used, base)]
        self.phases[name] = (first, per, place)
        self.used = [b + count * p for b, p in zip(base, per)]

    def at(self, name, job, i):
        first, per, place = self.phases[name]
        bank, n = place[job]
        return bank, (i - first) * per[bank] + n


RSQRT_STEPS = 11
LN_STEPS = 4 + 3 + 3 + 1 + RSQRT_STEPS


def rsqrt(v, s, out, x, t, half):
    s.did(v.tensor_scalar(half.bitcast(I32), x.bitcast(I32), 1, None, ALU.logical_shift_right))
    s.did(v.tensor_scalar(out.bitcast(I32), half.bitcast(I32), -1.0, RSQRT_MAGIC, ALU.mult, ALU.add))
    for _ in range(3):
        s.did(v.tensor_tensor(t, out, out, ALU.mult))
        s.did(v.scalar_tensor_tensor(t, t, -0.5, x, ALU.mult, ALU.mult))
        s.did(v.scalar_tensor_tensor(out, t, 1.5, out, ALU.add, ALU.mult))


def layernorm(v, s, out, x, st, w, ready):
    v.memset(w[:, 6], 0.0)
    for u in range(HT):
        s.go(v.bn_stats(st[:, u], x[:, u]))
    s.wait()
    s.go(v.tensor_tensor(w[:, 0], st[:, :, 1], st[:, :, 4], ALU.add))
    s.go(v.tensor_tensor(w[:, 1], st[:, :, 1], st[:, :, 4], ALU.subtract))
    s.go(v.tensor_tensor(w[:, 2], st[:, :, 2], st[:, :, 5], ALU.add))
    s.wait()
    s.go(v.tensor_scalar(w[:, 6], w[:, 0], 0.5, None, ALU.mult))
    s.go(v.scalar_tensor_tensor(w[:, 3], w[:, 1], 0.25, w[:, 1], ALU.mult, ALU.mult))
    s.go(v.tensor_scalar(w[:, 4], w[:, 2], 1.0 / D, LN_EPS, ALU.mult, ALU.add))
    s.wait()
    s.did(v.tensor_tensor(w[:, 0], w[:, 3], w[:, 4], ALU.add))
    rsqrt(v, s, w[:, 5], w[:, 0], w[:, 1], w[:, 2])
    for u in range(HT):
        ins = v.tensor_scalar(out[:, u], x[:, u], w[:, 6, u:u + 1], w[:, 5, u:u + 1], ALU.subtract, ALU.mult)
    ins.then_inc(ready, 1)


def build(nc, x, w_qkvg, b_qkvg, qn_w, kn_w, w_o0, b_o0, w_gates, u_gates, b_gates, w_h, u_h, b_h, c_in,
          w_q1, w_k1, w_v1, w_o1, fm_q, fm_k, fb_q, fb_k, rms_w, w_g, w_1, b_1, w_2, b_2, consts, out):
    with ExitStack() as ctx:
        def sb(name, shape, dt=F32):
            return ctx.enter_context(nc.sbuf_tensor(name, shape, dt))

        def sem(name):
            return ctx.enter_context(nc.semaphore(name))

        qk_dram = nc.dram_tensor("qk_splits", (B, SPLITS, 2, P, N), BF16, kind="Internal").ap()
        X = sb("X", [P, NT, D])
        xn1T = sb("xn1T", [D, NT * P])
        C2 = sb("C2", [D, N])
        const_sb = sb("const_sb", [P, NCONST])
        ident = const_sb[:, 0:P]
        causal = const_sb[:, P:2 * P]
        blocks = const_sb[:, 2 * P:3 * P]
        signs = const_sb[:, 3 * P:5 * P]
        before = const_sb[:, 5 * P:5 * P + E * E].rearrange("p (e f) -> p e f", e=E)
        sign_col = const_sb[:, 5 * P + E * E:NCONST]
        work = sb("work", [P, 7, HT])
        st = sb("st", [P, HT, 6])

        ps = ctx.enter_context(nc.psum_tensor("ps", [P, 8, 512], F32))
        S = ps[:, 0:4, :].rearrange("p (s j) q -> p s j q", s=2)
        O = ps[:, 4:6, :]
        SIDE = 6

        banks = Banks(8)
        full = [sem(f"bank{i}_full") for i in range(8)]
        free = [sem(f"bank{i}_free") for i in range(8)]

        front_jobs = {"xT": 1, "m0": 1, "m1": 0, "m2": 1, "m3": 0, "q": 1, "k": 0}
        post_jobs = {"attT": 0, "wo": 0, "x1T": 1, "f": 1, "i": 1, "g": 0}
        att_jobs = {"oT0": 0, "oT1": 0, "oT2": 1, "oT3": 0}
        order = ["attT", "xT", "wo", "m0", "m1", "m2", "m3", "x1T", "oT0", "q", "k", "f", "oT1", "i", "g", "oT2", "oT3"]
        PHASES = [("lead", -1, 0, 1, 0, 0), ("grow", 0, 1, 1, 1, 0), ("steady", 1, B - 1, 1, 1, 1),
                  ("shrink", B - 1, B, 0, 1, 1), ("tail", B, B + 1, 0, 0, 1)]
        for name, b0, b1, has_front, has_att, has_post in PHASES:
            jobs = {**(front_jobs if has_front else {}), **(att_jobs if has_att else {}), **(post_jobs if has_post else {})}
            banks.phase(name, 2 * b0, 2 * (b1 - b0), [(j, SIDE + jobs[j]) for j in order if j in jobs])
        l1 = []
        for hf in range(2):
            l1 += [("h", 0), ("hT", 1), ("x2T", 0), ("qf0", 1), ("qf1", 0), ("kf0", 1), ("kf1", 0), ("v", 1), ("kt0", 0), ("kt1", 1)]
            l1 += [(f"A{c}{g}", 2 + g) for c in range(HT) for g in range(G1)]
            l1 += [(f"S{c}{g}", 6 + g) for c in range(HT) for g in range(G1)]
            l1 += [("O0", 4), ("O1", 5), ("on0", 0), ("on1", 1), ("onT", 0), ("wo1", 1), ("x3T", 0), ("gate", 1)]
        l1 = [(f"{j}h{0 if n < len(l1) // 2 else 1}", b) for n, (j, b) in enumerate(l1)]
        banks.phase("linear", 0, B, l1)
        moe = [(f"up{e}{f}", (FT * e + f) % 4) for e in range(E) for f in range(FT)] + [(f"down{e}", 4 + e % 2) for e in range(E)] + [("cT", 6), ("b2", 7)]
        banks.phase("experts", 0, 2 * B, moe)

        s_const = sem("s_const"); s_x = sem("s_x"); s_prep = sem("s_prep"); s_prep_pe = sem("s_prep_pe")
        s_zero = sem("s_zero"); s_pool = sem("s_pool")
        front_steps = sem("front_steps"); post_steps = sem("post_steps"); att_steps = sem("att_steps")
        xn_ready = sem("xn_ready"); qkn_ready = sem("qkn_ready"); x1n_ready = sem("x1n_ready")
        split_ready = sem("split_ready"); split_stored = sem("split_stored"); gate_exp = sem("gate_exp")
        loaded = [sem("loaded0"), sem("loaded1")]
        v_staged = [sem("v_staged0"), sem("v_staged1")]
        scores_ready = sem("scores_ready"); probs_ready = sem("probs_ready"); probs_used = sem("probs_used")
        o_copied = sem("o_copied"); c_ready = sem("c_ready")
        w_loaded = sem("w_loaded"); l1_steps = sem("l1_steps"); act1 = sem("act1")
        xn2_ready = sem("xn2_ready"); qbd_ready = sem("qbd_ready"); state_ready = sem("state_ready")
        on_ready = sem("on_ready"); xn3_ready = sem("xn3_ready"); state_sum = sem("state_sum")
        squared1 = sem("squared1"); x3_static = sem("x3_static")
        hid_ready = sem("hid_ready"); hid_used = sem("hid_used"); moe_steps = sem("moe_steps")
        combT_ready = sem("combT_ready"); stored = sem("stored")
        combT_ps = sem("combT_ps")

        FRONT_STEPS = LN_STEPS + 3 + RSQRT_STEPS + 1 + 3 + 2
        POST_STEPS = 1 + LN_STEPS + 1 + 2
        L1_STEPS = 2 * LN_STEPS + 2 + RSQRT_STEPS + 1 + 2 + 2 * HT + 4
        MOE_STEPS = 3 + 3 * E
        CONST_LOADS = 11
        LATE_LOADS = 13
        s_prep2 = sem("s_prep2"); we_loaded = sem("we_loaded")

        with ExitStack() as part:
            def pb(name, shape, dt=F32):
                return part.enter_context(nc.sbuf_tensor(name, shape, dt))

            wqkvg = pb("wqkvg", [D, W0])
            bqkvg = pb("bqkvg", [P, W0])
            qnw = pb("qnw", [P, D])
            kscale = pb("kscale", [P, D])
            wo0 = pb("wo0", [D, D])
            bo0 = pb("bo0", [P, D])
            wg3 = pb("wg3", [D, 3, D])
            ug3 = pb("ug3", [D, 3, D])
            bg3 = pb("bg3", [D, 3])
            c0 = pb("c0", [D, 1])
            stF = pb("stF", [P, HT, 6])
            wF = pb("wF", [P, 7, HT])
            rr = pb("rr", [P, 4, 2 * H0 * HT])
            xn = pb("xn", [P, HT, D])
            xnT = pb("xnT", [D, HN])
            qk = pb("qk", [P, HT, 2 * D])
            sq = pb("sq", [P, HT, 2 * D])
            rest = pb("rest", [P, 2, HN])
            split = pb("split", [P, SPLITS, 2, HN], BF16)
            VG = pb("VG", [P, NT, D + H0])
            G = pb("G", [P, NT, H0])
            gexp = pb("gexp", [P, HT, H0])
            Q_st = pb("Q_st", [KROWS, 2, HG, N], BF16)
            K_st = pb("K_st", [KROWS, 2, HG, N], BF16)
            V_st = pb("V_st", [P, 2, TB, HG, VW])
            prob = pb("prob", [P, PROBS, 2, HN])
            OT = pb("OT", [P, 2, HN])
            rden = pb("rden", [P, 2, HG * HT])
            att = pb("att", [P, NT, D])
            att_static = pb("att_static", [P, HT, D])
            attT = pb("attT", [D, HN])
            x1n = pb("x1n", [P, HT, D])
            tg = pb("tg", [D, 3, HN])
            block = part.enter_context(nc.Block())

            def phases(eng, body):
                for name, b0, b1, has_front, has_att, has_post in PHASES:
                    if b1 - b0 == 1:
                        with eng.Fori(0, 2) as hp:
                            body(name, b0, hp, has_front, has_att, has_post)
                    else:
                        with eng.Fori(b0, b1) as b:
                            with eng.Fori(0, 2) as hp:
                                body(name, b, hp, has_front, has_att, has_post)

            @block.sync
            def _(sp):
                sp.dma_start(X[:, 0:TB], x[0:N].rearrange("(t p) d -> p t d", p=P)).then_inc(s_x, 16)
                loads = ((wqkvg, w_qkvg), (bqkvg, b_qkvg.partition_broadcast(P)), (qnw, qn_w.partition_broadcast(P)),
                         (kscale, kn_w.partition_broadcast(P)), (const_sb, consts), (wo0, w_o0), (bo0, b_o0.partition_broadcast(P)),
                         (wg3, w_gates), (ug3, u_gates), (bg3, b_gates), (c0, c_in))
                assert len(loads) == CONST_LOADS
                for dst, src in loads:
                    sp.dma_start(dst[:], src).then_inc(s_const, 16)
                sp.dma_start(X[:, TB:], x[N:].rearrange("(t p) d -> p t d", p=P)).then_inc(s_x, 16)

                def store_splits(b, hp):
                    sp.wait_ge(split_ready, 2 * b + hp + 1)
                    sp.dma_start(qk_dram[b, :, :, :, hp * HN:(hp + 1) * HN].rearrange("s a p t -> p (s a) t"),
                                 split[:].rearrange("p s a t -> p (s a) t")).then_inc(split_stored, 16)

                def load_group(b, hp, i, before_it=True):
                    if i == 0 and hp == 0:
                        sp.wait_ge(split_stored, 32 * (b + 1))
                    if before_it:
                        sp.wait_ge(scores_ready, 2 * SLOTS * (2 * b + hp - 1) + SLOTS * (i + 1))
                    heads = (2 * hp + i) * HG * HD
                    for c in range(SPLITS):
                        for s in range(SPLITS):
                            row = HD * (SPLITS * c + s)
                            for a, dst, which in ((0, Q_st, c), (1, K_st, s)):
                                sp.dma_start(dst[row:row + HD, i],
                                             qk_dram[b, which, a, heads:heads + HG * HD, :].rearrange("(j d) t -> d j t", d=HD)
                                             ).then_inc(loaded[i], 16)

                sp.wait_ge(s_zero, 2)
                store_splits(0, 0)
                store_splits(0, 1)
                load_group(0, 0, 0, False)
                load_group(0, 0, 1, False)
                with sp.Fori(0, B - 1) as b:
                    for hp in range(2):
                        store_splits(b + 1, hp)
                        load_group(b + hp, 1 - hp, 0)
                        load_group(b + hp, 1 - hp, 1)
                load_group(B - 1, 1, 0)
                load_group(B - 1, 1, 1)

            @block.gpsimd
            def _(pool):
                pool.memset(V_st[:], 0.0).then_inc(s_pool, 1)
                pool.wait_ge(s_pool, 1)
                pool.memset(V_st[:, :, :, :, HD:HD + 1], 1.0).then_inc(s_pool, 1)
                pool.wait_ge(s_pool, 2)

                def stage(b, hp, i, phase):
                    if i == 0 and hp == 0:
                        k, n = banks.at(phase, "m3", 2 * b - 1)
                        pool.wait_ge(free[k], n)
                    if phase != "lead":
                        pool.wait_ge(probs_used, SLOTS * (2 * b + hp - 1) + SLOTS // 2 * (i + 1))
                    heads = (2 * hp + i) * HG * HD
                    pool.tensor_copy(V_st[:, i, :, :, 0:HD],
                                     VG[:, bass.ds(b * TB, TB), heads:heads + HG * HD].rearrange("p k (j d) -> p k j d", d=HD)
                                     ).then_inc(v_staged[i], 1)

                stage(0, 0, 0, "lead")
                stage(0, 0, 1, "lead")
                for hp in range(2):
                    for i in range(2):
                        stage(hp, 1 - hp, i, "grow")
                with pool.Fori(1, B - 1) as b:
                    for hp in range(2):
                        for i in range(2):
                            stage(b + hp, 1 - hp, i, "steady")
                for i in range(2):
                    stage(B - 1, 1, i, "shrink")

            @block.vector
            def _(v):
                v.memset(Q_st[64:KROWS], 0.0).then_inc(s_zero, 1)
                v.memset(K_st[64:KROWS], 0.0).then_inc(s_zero, 1)
                v.wait_ge(s_const, 16 * CONST_LOADS)
                v.scalar_tensor_tensor(kscale[:], qnw[:], float(HD) ** -0.5, kscale[:], ALU.mult, ALU.mult).then_inc(s_prep, 1)
                v.tensor_scalar(ug3[:], ug3[:], 0.5, None, ALU.mult).then_inc(s_prep, 1)
                v.tensor_scalar(bg3[:, 0:2], bg3[:, 0:2], 0.5, None, ALU.mult).then_inc(s_prep, 1)
                v.tensor_scalar(C2[:], c0[:].to_broadcast([D, N]), 2.0, None, ALU.mult).then_inc(c_ready, 1)
                v.wait_ge(s_prep, 3)
                v.wait_ge(s_x, 32)

                def body(name, b, hp, has_front, has_att, has_post):
                    it = 2 * b + hp
                    f = Steps(v, front_steps, (it + 2) * FRONT_STEPS, FRONT_STEPS)
                    q = Steps(v, post_steps, (it - 2) * POST_STEPS, POST_STEPS)
                    TF = (b + 1) * TB + hp * HT
                    TP = (b - 1) * TB + hp * HT
                    XP = X[:, bass.ds(TP, HT)] if has_post else None

                    def product(job):
                        k, n = banks.at(name, job, it)
                        v.wait_ge(full[k], n)
                        return k

                    def was_read(job):
                        k, n = banks.at(name, job, it)
                        v.wait_ge(free[k], n)

                    def output(unit):
                        qh, g = unit % 2, 2 * hp + unit // 2
                        T4 = bass.ds(b * TB + HT * qh, HT)
                        v.wait_ge(probs_used, it * SLOTS + (unit + 1) * TB)
                        v.tensor_copy(OT[:, qh], O[:, qh]).then_inc(o_copied, 1)
                        k = product(f"oT{unit}")
                        oT = ps[:, k].rearrange("p (t j c) -> p t j c", t=HT, j=HG)
                        r = rden[:].rearrange("p a (t j) -> p a t j", t=HT)
                        a = Steps(v, att_steps, (4 * it + unit) * 2, 2)
                        a.did(v.reciprocal(r[:, 0], oT[:, :, :, HD]))
                        a.did(v.tensor_tensor(r[:, 1], r[:, 0], G[:, T4, bass.ds(g * HG, HG)], ALU.mult))
                        a.end()
                        v.tensor_tensor(att[:, T4, bass.ds(g * HG * HD, HG * HD)].rearrange("p t (j d) -> p t j d", d=HD),
                                        oT[:, :, :, 0:HD], r[:, 1].unsqueeze(3).to_broadcast([P, HT, HG, HD]), ALU.mult).then_inc(free[k], 1)

                    if has_post:
                        q.go(v.tensor_copy(att_static[:], att[:, bass.ds(TP, HT)]))
                    if has_front:
                        layernorm(v, f, xn[:], X[:, bass.ds(TF, HT)], stF, wF, xn_ready)
                    if has_post:
                        k = product("attT")
                        v.tensor_copy(attT[:], ps[:, k]).then_inc(free[k], 1)
                    if has_front:
                        k = product("xT")
                        v.tensor_copy(xnT[:], ps[:, k]).then_inc(free[k], 1)
                    if has_post:
                        k = product("wo")
                        v.tensor_tensor(XP, ps[:, k].rearrange("p (t d) -> p t d", t=HT), XP, ALU.add).then_inc(free[k], 1)
                        was_read("wo")
                        q.did(v.tensor_tensor(XP, XP, bo0[:].unsqueeze(1).to_broadcast([P, HT, D]), ALU.add))
                    if has_front:
                        for u in range(HT):
                            k = product(f"m{u}")
                            v.tensor_tensor(qk[:, u], ps[:, k, 0:2 * D], bqkvg[:, 0:2 * D], ALU.add)
                            v.tensor_tensor(VG[:, TF + u], ps[:, k, 2 * D:W0], bqkvg[:, 2 * D:W0], ALU.add).then_inc(free[k], 1)
                    if has_post:
                        layernorm(v, q, x1n[:], XP, st, work, x1n_ready)
                    if has_front:
                        was_read("m3")
                        f.did(v.tensor_tensor(sq[:], qk[:], qk[:], ALU.mult))
                        f.did(v.tensor_reduce(rr[:, 1], sq[:].rearrange("p t (h d) -> p (t h) d", d=HD), AX_X, ALU.add))
                        f.did(v.tensor_scalar(rr[:, 0], rr[:, 1], 1.0 / HD, RMS0_EPS, ALU.mult, ALU.add))
                        rsqrt(v, f, rr[:, 3], rr[:, 0], rr[:, 1], rr[:, 2])
                        qk_heads = qk[:].rearrange("p t (h d) -> p (t h) d", d=HD)
                        f.did(v.tensor_tensor(qk_heads, qk_heads, rr[:, 3].unsqueeze(2).to_broadcast([P, HT * 2 * H0, HD]), ALU.mult))
                        v.tensor_tensor(qk[:, :, D:], qk[:, :, D:], kscale[:].unsqueeze(1).to_broadcast([P, HT, D]), ALU.mult).then_inc(qkn_ready, 1)
                    if has_post:
                        k = product("x1T")
                        v.tensor_copy(xn1T[:, bass.ds(TP * P, HN)], ps[:, k]).then_inc(free[k], 1)
                    if has_att:
                        output(0)
                    if has_front:
                        v.wait_ge(split_stored, 16 * (it + 2))
                        for a, job in ((0, "q"), (1, "k")):
                            k = product(job)
                            f.did(v.tensor_copy(split[:, 0, a], ps[:, k]))
                            v.tensor_tensor(rest[:, a], ps[:, k], split[:, 0, a], ALU.subtract).then_inc(free[k], 1)
                        was_read("q")
                        was_read("k")
                        f.did(v.tensor_copy(split[:, 1], rest[:]))
                        v.tensor_tensor(split[:, 2], rest[:], split[:, 1], ALU.subtract).then_inc(split_ready, 1)
                        v.wait_ge(gate_exp, it + 3)
                        f.did(v.tensor_scalar(gexp[:], gexp[:], 1.0, None, ALU.add))
                        f.go(v.reciprocal(G[:, bass.ds(TF, HT)], gexp[:]))
                        f.end()
                    if has_att:
                        output(1)
                        output(2)
                    if has_post:
                        for job in "fig":
                            was_read(job)
                        CP = C2[:, bass.ds(hp * HN, HN)]
                        q.go(v.scalar_tensor_tensor(tg[:, 0], tg[:, 0], 1.0, CP, ALU.add, ALU.mult))
                        q.did(v.scalar_tensor_tensor(tg[:, 1], tg[:, 1], 1.0, tg[:, 2], ALU.add, ALU.mult))
                        v.scalar_tensor_tensor(CP, tg[:, 0], 0.5, tg[:, 1], ALU.mult, ALU.add).then_inc(c_ready, 1)
                        q.end()
                    if has_att:
                        output(3)

                phases(v, body)

            @block.scalar
            def _(act):
                act.wait_ge(s_const, 16 * CONST_LOADS)
                act.wait_ge(s_prep, 3)

                def body(name, b, hp, has_front, has_att, has_post):
                    it = 2 * b + hp

                    def gates():
                        k, n = banks.at(name, "m3", it)
                        act.wait_ge(free[k], n)
                        act.activation(gexp[:], VG[:, bass.ds((b + 1) * TB + hp * HT, HT), D:], ACT.Exp, scale=-1.0).then_inc(gate_exp, 1)

                    def tanh(n_gate, job):
                        k, n = banks.at(name, job, it)
                        act.wait_ge(full[k], n)
                        act.wait_ge(c_ready, it - 1)
                        act.activation(tg[:, n_gate], ps[:, k], ACT.Tanh, bias=bg3[:, n_gate:n_gate + 1],
                                       scale=(0.5 if n_gate < 2 else 1.0)).then_inc(free[k], 1)

                    for slot in range(SLOTS if has_att else 1):
                        if has_att:
                            for pair in range(2):
                                n = 2 * slot + pair
                                act.wait_ge(scores_ready, 2 * SLOTS * it + n + 1)
                                if pair == 0 and n >= PROBS:
                                    act.wait_ge(probs_used, SLOTS * it + (n - PROBS) // 2 + 1)
                                act.activation(prob[:, n % PROBS], S[:, n % 2], ACT.Exp).then_inc(probs_ready, 1)
                        if has_front and slot == (GATES_AT if has_att else 0):
                            gates()
                        for g, job in enumerate("fig"):
                            if has_post and slot == (TANH_AT[g] if has_att else 0):
                                tanh(g, job)

                phases(act, body)

            @block.tensor
            def _(pe):
                pe.wait_ge(s_const, 16 * CONST_LOADS)
                pe.wait_ge(s_prep, 3)

                def body(name, b, hp, has_front, has_att, has_post):
                    it = 2 * b + hp

                    def bank(job):
                        k, n = banks.at(name, job, it)
                        pe.wait_ge(free[k], n - 1)
                        return k

                    def transposed(job, src):
                        k = bank(job)
                        for t in range(HT):
                            mm = pe.transpose(ps[:, k, t * P:(t + 1) * P], src(t), ident)
                        mm.then_inc(full[k], 1)

                    def was_read(job):
                        k, n = banks.at(name, job, it)
                        pe.wait_ge(free[k], n)

                    def x_transpose():
                        pe.wait_ge(xn_ready, it + 3)
                        transposed("xT", lambda t: xn[:, t])

                    def project(u):
                        if u == 0:
                            was_read("xT")
                        k = bank(f"m{u}")
                        pe.matmul(ps[:, k, 0:W0], xnT[:, u * P:(u + 1) * P], wqkvg[:], start=True, stop=True).then_inc(full[k], 1)

                    def qk_transpose(a):
                        pe.wait_ge(qkn_ready, it + 3)
                        transposed("qk"[a], lambda t: qk[:, t, a * D:(a + 1) * D])

                    def att_transpose():
                        pe.wait_ge(post_steps, (it - 2) * POST_STEPS + 1)
                        transposed("attT", lambda t: att_static[:, t])

                    def project_out():
                        was_read("attT")
                        k = bank("wo")
                        for t in range(HT):
                            mm = pe.matmul(ps[:, k, t * P:(t + 1) * P], attT[:, t * P:(t + 1) * P], wo0[:], start=True, stop=True)
                        mm.then_inc(full[k], 1)

                    def x1_transpose():
                        pe.wait_ge(x1n_ready, it - 1)
                        transposed("x1T", lambda t: x1n[:, t])

                    def gate_x(g):
                        if g == 0:
                            was_read("x1T")
                            pe.wait_ge(c_ready, it - 2)
                        k = bank("fig"[g])
                        pe.matmul(ps[:, k], wg3[:, g], xn1T[:, bass.ds(((b - 1) * 2 + hp) * HN, HN)], start=True, stop=False)

                    def gate_c(g):
                        k, _ = banks.at(name, "fig"[g], it)
                        pe.matmul(ps[:, k], ug3[:, g], C2[:, bass.ds(hp * HN, HN)], start=False, stop=True).then_inc(full[k], 1)

                    def out_transpose(unit):
                        pe.wait_ge(o_copied, 4 * it + unit + 1)
                        qh = unit % 2
                        k = bank(f"oT{unit}")
                        for t in range(HT):
                            mm = pe.transpose(ps[:, k, t * P:(t + 1) * P], OT[:, qh, t * P:(t + 1) * P], ident)
                        mm.then_inc(full[k], 1)

                    pieces = []
                    if has_post:
                        pieces += [(0, att_transpose, ()), (3, project_out, ()), (9, x1_transpose, ()),
                                   (15, gate_x, (0,)), (16, gate_c, (0,)), (20, gate_x, (1,)), (21, gate_c, (1,)),
                                   (23, gate_x, (2,)), (24, gate_c, (2,))]
                    if has_front:
                        pieces += [(2, x_transpose, ())] + [(4 + u, project, (u,)) for u in range(HT)]
                        pieces += [(12, qk_transpose, (0,)), (13, qk_transpose, (1,))]
                    if has_att:
                        pieces += [(10, out_transpose, (0,)), (18, out_transpose, (1,)), (26, out_transpose, (2,))]
                    pieces.sort(key=lambda piece: piece[0])

                    def scores(n):
                        i, m = n // (2 * 2 * TB), n % (2 * 2 * TB)
                        qh, kt, pair = m // (2 * TB), (m // 2) % TB, m % 2
                        if m == 0:
                            pe.wait_ge(loaded[i], LOADS * (it + 1))
                        if n >= 2:
                            pe.wait_ge(probs_ready, 2 * SLOTS * it + n - 1)
                        for j in range(2):
                            mm = pe.matmul(S[:, n % 2, j], K_st[:, i, 2 * pair + j, kt * P:(kt + 1) * P],
                                           Q_st[:, i, 2 * pair + j, qh * HN:(qh + 1) * HN], start=True, stop=True)
                        mm.then_inc(scores_ready, 1)

                    def values(slot):
                        i, qh, kt = slot // (2 * TB), (slot // TB) % 2, slot % TB
                        if slot % (2 * TB) == 0:
                            pe.wait_ge(v_staged[i], it + 1)
                        if kt == 0 and slot >= 2 * TB:
                            pe.wait_ge(o_copied, 4 * it + slot // TB - 1)
                        pe.wait_ge(probs_ready, 2 * SLOTS * it + 2 * slot + 2)
                        for j in range(HG):
                            mm = pe.matmul(O[VW * j:VW * (j + 1), qh], V_st[:, i, kt, j], prob[:, (2 * slot + j // 2) % PROBS, j % 2],
                                           start=(kt == 0), stop=(kt == TB - 1))
                        mm.then_inc(probs_used, 1)

                    if has_att:
                        pe.wait_ge(probs_ready, 2 * SLOTS * it)
                        scores(0)
                        scores(1)
                    for slot in range(SLOTS if has_att else 1):
                        if has_att:
                            if slot < SLOTS - 1:
                                scores(2 * slot + 2)
                            if slot:
                                values(slot - 1)
                        while pieces and (pieces[0][0] <= slot or not has_att):
                            _, piece, args = pieces.pop(0)
                            piece(*args)
                        if has_att and slot < SLOTS - 1:
                            scores(2 * slot + 3)
                    if has_att:
                        values(SLOTS - 1)
                        out_transpose(3)

                phases(pe, body)

        with ExitStack() as part:
            def pb(name, shape, dt=F32):
                return part.enter_context(nc.sbuf_tensor(name, shape, dt))

            wh = pb("wh", [D, D])
            uh = pb("uh", [D, D])
            bh = pb("bh", [D, 1])
            wq1 = pb("wq1", [D, D])
            wk1 = pb("wk1", [D, D])
            wv1 = pb("wv1", [D, D])
            wo1 = pb("wo1", [D, D])
            fmq = pb("fmq", [D, 2 * D])
            fmk = pb("fmk", [D, 2 * D])
            fb = pb("fb", [D, 2])
            rmsw = pb("rmsw", [D, 1])
            wqf = pb("wqf", [D, 2 * D])
            wkf = pb("wkf", [D, 2 * D])
            wg = pb("wg", [D, E])
            w1 = pb("w1", [D, E, F])
            w2 = pb("w2", [P, E, FT, D])
            b1 = pb("b1", [P, E, FT])
            b2 = pb("b2", [E, D])
            hT = pb("hT", [D, HN])
            xn2 = pb("xn2", [P, HT, D])
            xn2T = pb("xn2T", [D, HN])
            Qf = pb("Qf", [P, G1, HN])
            Kf = pb("Kf", [P, G1, HN])
            Qbd = pb("Qbd", [P, G1, HG, HN])
            V1 = pb("V1", [P, HT, H1, VW])
            Kt = pb("Kt", [P, G1, HT, P])
            Am = pb("Am", [P, G1, HG, P])
            state = pb("state", [P, 2, G1, P])
            oT1 = pb("oT1", [P, G1, HN])
            sq1 = pb("sq1", [P, HT, H1, DK])
            rr1 = pb("rr1", [P, 4, HT * H1])
            on = pb("on", [P, HT, D])
            onT = pb("onT", [D, HN])
            xn3 = pb("xn3", [P, HT, D])
            x3s = pb("x3s", [D, HN])
            sg = pb("sg", [P, HT, E])
            pairs = pb("pairs", [P, 2, HT * E, E])
            comb = pb("comb", [P, NT, E])
            combT = pb("combT", [E, HN])
            comb_static = pb("comb_static", [P, HT, E])
            hid = pb("hid", [P, 2, FT, HN])
            block = part.enter_context(nc.Block())

            def wait_full(eng, phase, job, i):
                k, n = banks.at(phase, job, i)
                eng.wait_ge(full[k], n)
                return k

            def wait_free(eng, phase, job, i, before=0):
                k, n = banks.at(phase, job, i)
                eng.wait_ge(free[k], n - before)
                return k

            @block.sync
            def _(sp):
                loads = ((wh, w_h), (uh, u_h), (bh, b_h), (wq1, w_q1), (wk1, w_k1), (wv1, w_v1), (wo1, w_o1), (fmq, fm_q), (fmk, fm_k),
                         (rmsw, rms_w), (wg, w_g))
                assert len(loads) + 2 == LATE_LOADS
                for dst, src in loads:
                    sp.dma_start(dst[:], src).then_inc(w_loaded, 16)
                sp.dma_start(fb[:, 0:1], fb_q).then_inc(w_loaded, 16)
                sp.dma_start(fb[:, 1:2], fb_k).then_inc(w_loaded, 16)
                for dst, src in ((w1, w_1), (w2, w_2), (b1, b_1), (b2, b_2)):
                    sp.dma_start(dst[:], src).then_inc(we_loaded, 16)
                with sp.Fori(0, 2 * B) as h:
                    wait_free(sp, "experts", f"down{E - 1}", h)
                    sp.dma_start(out[bass.ds(h * HN, HN), :].rearrange("(t p) d -> p t d", p=P), X[:, bass.ds(h * HT, HT)]).then_inc(stored, 16)
                sp.wait_ge(stored, 16 * 2 * B)

            @block.vector
            def _(v):
                v.memset(Qbd[:], 0.0).then_inc(s_prep2, 1)
                v.memset(V1[:], 0.0).then_inc(s_prep2, 1)
                v.wait_ge(w_loaded, 16 * LATE_LOADS)
                v.tensor_scalar(uh[:], uh[:], 0.5, None, ALU.mult).then_inc(s_prep2, 1)
                v.tensor_scalar(wo1[:], wo1[:], rmsw[:], None, ALU.mult).then_inc(s_prep2, 1)
                v.tensor_tensor(fmq[:], fmq[:], signs, ALU.mult).then_inc(s_prep2, 1)
                v.tensor_tensor(fmk[:], fmk[:], signs, ALU.mult).then_inc(s_prep2, 1)
                v.tensor_tensor(fb[:], fb[:], sign_col.to_broadcast([D, 2]), ALU.mult).then_inc(s_prep2, 1)
                v.wait_ge(s_prep2, 7)
                v.tensor_scalar(fb[:, 0:1], fb[:, 0:1], -0.5 * math.log(DF), None, ALU.add).then_inc(s_prep2, 1)
                v.wait_ge(s_prep_pe, 2)
                v.tensor_copy(wqf[:], ps[:, 0, 0:2 * D]).then_inc(s_prep2, 1)
                v.tensor_copy(wkf[:], ps[:, 1, 0:2 * D]).then_inc(s_prep2, 1)
                with v.Fori(0, B) as b:
                    for hf in range(2):
                        h = 2 * b + hf
                        s = Steps(v, l1_steps, h * L1_STEPS, L1_STEPS)
                        T4 = bass.ds(b * TB + hf * HT, HT)

                        def product(job):
                            return wait_full(v, "linear", f"{job}h{hf}", b)

                        def was_read(job):
                            wait_free(v, "linear", f"{job}h{hf}", b)

                        X4 = X[:, T4]
                        k = product("hT")
                        v.tensor_tensor(X4, ps[:, k].rearrange("p (t d) -> p t d", t=HT), X4, ALU.add).then_inc(free[k], 1)
                        was_read("hT")
                        layernorm(v, s, xn2[:], X4, st, work, xn2_ready)
                        k = product("x2T")
                        v.tensor_copy(xn2T[:], ps[:, k]).then_inc(free[k], 1)
                        was_read("qf0")
                        was_read("qf1")
                        for j in range(HG):
                            rows = slice(DF * j, DF * (j + 1))
                            ins = v.tensor_copy(Qbd[rows, :, j], Qf[rows])
                        ins.then_inc(qbd_ready, 1)
                        k = product("v")
                        v.tensor_copy(V1[:, :, :, 0:DK], ps[:, k].rearrange("p (t h d) -> p t h d", t=HT, h=H1)).then_inc(free[k], 1)

                        def mask(n):
                            c, g = n // G1, n % G1
                            k = product(f"A{c}{g}")
                            v.tensor_tensor(Am[:, g], ps[:, k].rearrange("p (j q) -> p j q", j=HG), causal.unsqueeze(1).to_broadcast([P, HG, P]),
                                            ALU.mult).then_inc(free[k], 1)

                        def keep_state(n):
                            c, g = n // G1, n % G1
                            k = product(f"S{c}{g}")
                            v.tensor_tensor(state[:, (c + 1) % 2, g], ps[:, k, 0:P], blocks, ALU.mult).then_inc(free[k], 1)

                        for n in range(HT * G1 + 2):
                            if n >= 2:
                                keep_state(n - 2)
                            if n < HT * G1:
                                mask(n)
                        v.wait_ge(squared1, 2 * h + 2)
                        s.did(v.tensor_reduce(rr1[:, 1], sq1[:].rearrange("p t h d -> p (t h) d"), AX_X, ALU.add))
                        s.did(v.tensor_scalar(rr1[:, 0], rr1[:, 1], 1.0 / DK, RMS1_EPS, ALU.mult, ALU.add))
                        rsqrt(v, s, rr1[:, 3], rr1[:, 0], rr1[:, 1], rr1[:, 2])
                        for a in range(2):
                            k = product(f"on{a}")
                            for c in range(2):
                                ins = v.tensor_tensor(on[:, 2 * a + c].rearrange("p (h d) -> p h d", h=H1),
                                                ps[:, k, 2 * c * P:2 * (c + 1) * P].rearrange("p (h d) -> p h d", h=H1)[:, :, 0:DK],
                                                rr1[:, 3, (2 * a + c) * H1:(2 * a + c + 1) * H1].unsqueeze(2).to_broadcast([P, H1, DK]), ALU.mult)
                            ins.then_inc(free[k], 1)
                        k = product("onT")
                        v.tensor_copy(onT[:], ps[:, k]).then_inc(free[k], 1)
                        k = product("wo1")
                        v.tensor_tensor(X4, ps[:, k].rearrange("p (t d) -> p t d", t=HT), X4, ALU.add).then_inc(free[k], 1)
                        was_read("wo1")
                        layernorm(v, s, xn3[:], X4, st, work, xn3_ready)
                        k = product("x3T")
                        s.did(v.tensor_copy(x3s[:], ps[:, k]))
                        v.tensor_copy(xn1T[:, bass.ds(h * HN, HN)], x3s[:]).then_inc(free[k], 1)
                        was_read("gate")
                        s.did(v.tensor_scalar(sg[:], sg[:], 1.0, None, ALU.add))
                        s.did(v.reciprocal(sg[:], sg[:]))
                        rows = sg[:].rearrange("p t e -> p (t e)").unsqueeze(2).to_broadcast([P, HT * E, E])
                        for t in range(HT):
                            mine = sg[:, t].unsqueeze(2).to_broadcast([P, E, E])
                            other = sg[:, t].unsqueeze(1).to_broadcast([P, E, E])
                            s.go(v.tensor_tensor(pairs[:, 0, t * E:(t + 1) * E], other, mine, ALU.is_gt))
                            s.go(v.tensor_tensor(pairs[:, 1, t * E:(t + 1) * E], other, mine, ALU.is_equal))
                        s.wait()
                        p4 = pairs[:, 1].rearrange("p (t e) f -> p t e f", t=HT)
                        s.did(v.tensor_tensor(p4, p4, before.unsqueeze(1).to_broadcast([P, HT, E, E]), ALU.mult))
                        s.did(v.tensor_tensor(pairs[:, 0], pairs[:, 0], pairs[:, 1], ALU.add))
                        s.did(v.tensor_reduce(rr1[:, 0], pairs[:, 0], AX_X, ALU.add))
                        s.go(v.scalar_tensor_tensor(comb[:, T4].rearrange("p t e -> p (t e)"), rr1[:, 0], 2.0, sg[:].rearrange("p t e -> p (t e)"), ALU.is_lt, ALU.mult))
                        s.end()
                v.wait_ge(l1_steps, L1_STEPS * 2 * B)
                with v.Fori(0, 2 * B) as h:
                    m = Steps(v, moe_steps, h * MOE_STEPS, MOE_STEPS)
                    m.go(v.tensor_copy(comb_static[:], comb[:, bass.ds(h * HT, HT)]))
                    X4 = X[:, bass.ds(h * HT, HT)]
                    k = wait_full(v, "experts", "cT", h)
                    m.go(v.tensor_copy(combT[:], ps[0:E, k]))
                    ins_k = wait_full(v, "experts", "b2", h)
                    m.did(v.tensor_tensor(X4, ps[:, ins_k].rearrange("p (t d) -> p t d", t=HT), X4, ALU.add))
                    for e in range(E):
                        k = wait_full(v, "experts", f"down{e}", h)
                        if e:
                            m.wait()
                        for t in range(HT):
                            ins = v.scalar_tensor_tensor(X[:, h * HT + t], ps[:, k, t * D:(t + 1) * D], comb_static[:, t, e:e + 1], X[:, h * HT + t], ALU.mult, ALU.add)
                            if t < HT - 1:
                                m.go(ins)
                        ins.then_inc(free[k], 1)
                        wait_free(v, "experts", f"down{e}", h)
                    m.end()

            @block.scalar
            def _(act):
                act.wait_ge(s_prep2, 10)
                with act.Fori(0, B) as b:
                    for hf in range(2):
                        h = 2 * b + hf
                        k = wait_full(act, "linear", f"hh{hf}", b)
                        act.activation(hT[:], ps[:, k], ACT.Tanh, bias=bh[:]).then_inc(free[k], 1)
                        for a, dst in ((0, Qf), (1, Kf)):
                            for g in range(G1):
                                k = wait_full(act, "linear", f"{'qk'[a]}f{g}h{hf}", b)
                                act.activation(dst[:, g], ps[:, k], ACT.Exp, bias=fb[:, a:a + 1]).then_inc(free[k], 1)
                        for g in range(G1):
                            k = wait_full(act, "linear", f"kt{g}h{hf}", b)
                            act.activation(Kt[:, g].rearrange("p c f -> p (c f)"), ps[:, k], ACT.Copy).then_inc(free[k], 1)
                        for g in range(G1):
                            k = wait_full(act, "linear", f"O{g}h{hf}", b)
                            act.activation(oT1[:, g], ps[:, k], ACT.Copy).then_inc(free[k], 1)
                        for a in range(2):
                            k = wait_full(act, "linear", f"on{a}h{hf}", b)
                            for c in range(2):
                                ins = act.activation(sq1[:, 2 * a + c], ps[:, k, 2 * c * P:2 * (c + 1) * P].rearrange("p (h d) -> p h d", h=H1)[:, :, 0:DK], ACT.Square)
                            ins.then_inc(squared1, 1)
                        k = wait_full(act, "linear", f"gateh{hf}", b)
                        act.activation(sg[:].rearrange("p t e -> p (t e)"), ps[:, k, 0:HT * E], ACT.Exp, scale=-1.0).then_inc(free[k], 1)
                act.wait_ge(we_loaded, 64)
                with act.Fori(0, 2 * B) as h:
                    for e in range(E):
                        for f in range(FT):
                            k = wait_full(act, "experts", f"up{e}{f}", h)
                            if e >= 2 and f == 0:
                                wait_full(act, "experts", f"down{e - 2}", h)
                            act.activation(hid[:, e % 2, f], ps[:, k], ACT.Gelu_apprx_tanh, bias=b1[:, e, f:f + 1]).then_inc(free[k], 1)

            @block.tensor
            def _(pe):
                pe.wait_ge(s_prep2, 6)
                pe.matmul(ps[:, 0, 0:2 * D], wq1[:], fmq[:], start=True, stop=True).then_inc(s_prep_pe, 1)
                pe.matmul(ps[:, 1, 0:2 * D], wk1[:], fmk[:], start=True, stop=True).then_inc(s_prep_pe, 1)
                pe.wait_ge(s_prep2, 10)
                with pe.Fori(0, B) as b:
                    for hf in range(2):
                        h = 2 * b + hf

                        def bank(job):
                            return wait_free(pe, "linear", f"{job}h{hf}", b, 1)

                        def was_read(job):
                            wait_free(pe, "linear", f"{job}h{hf}", b)

                        def transposed(job, src):
                            k = bank(job)
                            for t in range(HT):
                                mm = pe.transpose(ps[:, k, t * P:(t + 1) * P], src(t), ident)
                            mm.then_inc(full[k], 1)

                        def by_tile(job, src, w, width=D):
                            k = bank(job)
                            for t in range(HT):
                                mm = pe.matmul(ps[:, k, t * width:(t + 1) * width], src[:, t * P:(t + 1) * P], w[:], start=True, stop=True)
                            mm.then_inc(full[k], 1)

                        k = bank("h")
                        pe.matmul(ps[:, k], wh[:], xn1T[:, bass.ds(h * HN, HN)], start=True, stop=False)
                        pe.matmul(ps[:, k], uh[:], C2[:, hf * HN:(hf + 1) * HN], start=False, stop=True).then_inc(full[k], 1)
                        was_read("h")
                        transposed("hT", lambda t: hT[:, t * P:(t + 1) * P])
                        pe.wait_ge(xn2_ready, h + 1)
                        transposed("x2T", lambda t: xn2[:, t])
                        was_read("x2T")
                        for a, w in ((0, wqf), (1, wkf)):
                            for g in range(G1):
                                k = bank(f"{'qk'[a]}f{g}")
                                pe.matmul(ps[:, k], w[:, g * P:(g + 1) * P], xn2T[:], start=True, stop=True).then_inc(full[k], 1)
                        by_tile("v", xn2T, wv1)
                        for g in range(G1):
                            was_read(f"kf{g}")
                            transposed(f"kt{g}", lambda t: Kf[:, g, t * P:(t + 1) * P])
                        pe.wait_ge(qbd_ready, h + 1)
                        was_read("v")
                        was_read("kt0")
                        was_read("kt1")

                        def inner(n):
                            c, g = n // G1, n % G1
                            k = bank(f"A{c}{g}")
                            pe.matmul(ps[:, k], Kf[:, g, c * P:(c + 1) * P], Qbd[:, g, :, c * P:(c + 1) * P], start=True, stop=True).then_inc(full[k], 1)

                        def outer(n):
                            c, g = n // G1, n % G1
                            first = hf == 0 and c == 0
                            cols = slice(c * P, (c + 1) * P)
                            k = banks.at("linear", f"O{g}h{hf}", b)[0]
                            if c == 0:
                                bank(f"O{g}")
                            if not first:
                                if c:
                                    was_read(f"S{c - 1}{g}")
                                pe.matmul(ps[:, k, cols], state[:, c % 2, g], Qf[:, g, cols], start=True, stop=False, skip_group_check=True)
                            was_read(f"A{c}{g}")
                            for j in range(HG):
                                mm = pe.matmul(ps[VW * j:VW * (j + 1), k, cols], V1[:, c, HG * g + j], Am[:, g, j], start=first, stop=True, skip_group_check=True)
                            if c == HT - 1:
                                mm.then_inc(full[k], 1)
                            k = bank(f"S{c}{g}")
                            pe.matmul(ps[:, k, 0:P], Kt[:, g, c], V1[:, c, HG * g:HG * (g + 1)].rearrange("p j v -> p (j v)"),
                                      start=first, stop=True, skip_group_check=True).then_inc(full[k], 1)

                        inner(0)
                        inner(1)
                        for n in range(HT * G1):
                            outer(n)
                            if n + 2 < HT * G1:
                                inner(n + 2)
                        was_read("O0")
                        was_read("O1")
                        for a in range(2):
                            k = bank(f"on{a}")
                            for c in range(2):
                                for g in range(G1):
                                    mm = pe.transpose(ps[:, k, (2 * c + g) * P:(2 * c + g + 1) * P], oT1[:, g, (2 * a + c) * P:(2 * a + c + 1) * P], ident)
                            mm.then_inc(full[k], 1)
                        was_read("on0")
                        was_read("on1")
                        transposed("onT", lambda t: on[:, t])
                        was_read("onT")
                        by_tile("wo1", onT, wo1)
                        pe.wait_ge(xn3_ready, h + 1)
                        transposed("x3T", lambda t: xn3[:, t])
                        was_read("x3T")
                        by_tile("gate", x3s, wg, E)
                pe.wait_ge(we_loaded, 64)
                pe.wait_ge(l1_steps, L1_STEPS * 2 * B)
                with pe.Fori(0, 2 * B) as h:
                    def bank(job):
                        return wait_free(pe, "experts", job, h, 1)

                    pe.wait_ge(moe_steps, h * MOE_STEPS + 1)
                    k = banks.at("experts", "cT", h)[0]
                    for t in range(HT):
                        mm = pe.transpose(ps[0:E, k, t * P:(t + 1) * P], comb_static[:, t], ident)
                    mm.then_inc(full[k], 1)
                    pe.wait_ge(moe_steps, h * MOE_STEPS + 2)
                    k = banks.at("experts", "b2", h)[0]
                    for t in range(HT):
                        mm = pe.matmul(ps[:, k, t * D:(t + 1) * D], combT[:, t * P:(t + 1) * P], b2[:], start=True, stop=True)
                    mm.then_inc(full[k], 1)

                    def up(e):
                        for f in range(FT):
                            k = bank(f"up{e}{f}")
                            pe.matmul(ps[:, k], w1[:, e, f * P:(f + 1) * P], xn1T[:, bass.ds(h * HN, HN)], start=True, stop=True).then_inc(full[k], 1)

                    def down(e):
                        if e >= 2:
                            k = wait_free(pe, "experts", f"down{e - 2}", h)
                        k = banks.at("experts", f"down{e}", h)[0]
                        wait_free(pe, "experts", f"up{e}{FT - 1}", h)
                        for t in range(HT):
                            for f in range(FT):
                                mm = pe.matmul(ps[:, k, t * D:(t + 1) * D], hid[:, e % 2, f, t * P:(t + 1) * P], w2[:, e, f], start=(f == 0), stop=(f == FT - 1))
                        mm.then_inc(full[k], 1)

                    up(0)
                    for e in range(1, E + 1):
                        if e < E:
                            up(e)
                        down(e - 1)


def _layout(np, a):
    def diagonal(w):
        o = np.zeros((H1, DK, H1, 2, DK), w.dtype)
        for h in range(H1):
            for sign in range(2):
                o[h, :, h, sign, :] = w.T
        return o.reshape(D, 2 * D)

    wq, bq = a["L0_attn_Wq"], a["L0_attn_bq"]
    consts = np.zeros((P, NCONST), np.float32)
    consts[:, 0:P] = np.eye(P)
    consts[:, P:2 * P] = np.triu(np.ones((P, P)))
    consts[:, 2 * P:3 * P] = np.kron(np.eye(HG), np.ones((VW, VW)))
    consts[:, 3 * P:5 * P] = np.tile(np.repeat([1.0, -1.0], DK), 2 * HG)
    consts[:, 5 * P:5 * P + E * E] = np.tril(np.ones((E, E)), -1).reshape(E * E)
    consts[:, 5 * P + E * E] = np.tile(np.repeat([1.0, -1.0], DK), HG)
    return dict(
        x=a["L0_attn_x"].reshape(NT * P, D),
        w_qkvg=np.concatenate([wq[:, :D], a["L0_attn_Wk"], a["L0_attn_Wv"], wq[:, D:]], 1),
        b_qkvg=np.concatenate([bq[:D], a["L0_attn_bk"], a["L0_attn_bv"], bq[D:]]),
        qn_w=np.tile(a["L0_attn_qn_w"], H0), kn_w=np.tile(a["L0_attn_kn_w"], H0),
        w_o0=a["L0_attn_Wo"], b_o0=a["L0_attn_bo"],
        w_gates=np.stack([a["L0_ffn_w" + c].T for c in "fic"], 1),
        u_gates=np.stack([a["L0_ffn_u" + c].T for c in "fic"], 1),
        b_gates=np.stack([a["L0_ffn_b" + c] for c in "fic"], 1),
        w_h=a["L0_ffn_wo"].T, u_h=a["L0_ffn_uo"].T, b_h=a["L0_ffn_bo"].reshape(D, 1), c_in=a["L0_ffn_in_c"].reshape(D, 1),
        w_q1=a["L1_attn_Wq"], w_k1=a["L1_attn_Wk"], w_v1=a["L1_attn_Wv"].T, w_o1=a["L1_attn_Wo"].T,
        fm_q=diagonal(a["L1_attn_fmq_w"]), fm_k=diagonal(a["L1_attn_fmk_w"]),
        fb_q=np.tile(a["L1_attn_fmq_b"], H1).reshape(D, 1), fb_k=np.tile(a["L1_attn_fmk_b"], H1).reshape(D, 1),
        rms_w=np.tile(a["L1_attn_rms_w"], H1).reshape(D, 1),
        w_g=a["L1_ffn_Wg"], w_1=a["L1_ffn_W1"].transpose(1, 0, 2), b_1=a["L1_ffn_b1"].reshape(E, FT, P).transpose(2, 0, 1),
        w_2=a["L1_ffn_W2"].reshape(E, FT, P, D).transpose(2, 0, 1, 3), b_2=a["L1_ffn_b2"],
        consts=consts,
    )


def kernel(**inputs):
    import numpy as _np
    import concourse.bacc as _bacc
    from concourse import mybir as _mybir
    from concourse.bass_utils import run_bass_kernel_spmd as _run

    nc = _bacc.Bacc("TRN2", target_bir_lowering=False, num_devices=1)
    laid = _layout(_np, {k: _np.asarray(v) for k, v in inputs.items()})
    arrays, args = {}, {}
    for name, a in laid.items():
        a = _np.ascontiguousarray(a)
        arrays[f"in_{name}"] = a
        args[name] = nc.dram_tensor(f"in_{name}", a.shape, _mybir.dt.from_np(a.dtype), kind="ExternalInput").ap()
    out = nc.dram_tensor("out_rows", (NT * P, D), _mybir.dt.float32, kind="ExternalOutput").ap()
    build(nc, out=out, **args)
    r = _run(nc, [arrays], core_ids=[0])
    return r.results[0]["out_rows"].reshape(B, N, D)
```

```python
import math
from contextlib import ExitStack

import concourse.bass as bass
from concourse import mybir

F32 = mybir.dt.float32
BF16 = mybir.dt.bfloat16
I32 = mybir.dt.int32
ALU = mybir.AluOpType
ACT = mybir.ActivationFunctionType
AX_X = mybir.AxisListType.X
AX_XY = mybir.AxisListType.XY

P = 128
D = 128
B, N = 4, 1024
TB = N // P
NT = B * TB
HT = TB // 2
HN = N // 2
LN_EPS = 1e-5

H0, HD = 16, 8
HG = 4
NG = H0 // HG
VW = 32
SPLITS = 3
COMBOS = SPLITS * SPLITS
KROWS = 96
W0 = 3 * D + H0
RMS0_EPS = 1e-6
SLOTS = 2 * 2 * TB
SHIFT_ROW = COMBOS * HD
SHIFT_ABOVE = 40.0
PROBS = 8
LOADS = 16 * 2 * COMBOS

H1, DK = 8, 16
DF = 2 * DK
G1 = 2
RMS1_EPS = 1e-5

E, F = 8, 512
FT = F // P
GATES_AT, TANH_AT = 10, (18, 23, 26)
NCONST = 5 * P + E * E + 1
RSQRT_MAGIC = float(0x5F3759DF)


class Steps:

    def __init__(self, eng, sem, base, per):
        self.eng, self.sem, self.base, self.per, self.n = eng, sem, base, per, 0

    def go(self, ins):
        self.n += 1
        ins.then_inc(self.sem, 1)

    def wait(self):
        self.eng.wait_ge(self.sem, self.base + self.n)

    def did(self, ins):
        self.go(ins)
        self.wait()

    def end(self):
        assert self.n == self.per, self.n


LATE = (("h", 4), ("hT", 9), ("x2T", 2), ("qf0", 0), ("qf1", 0), ("kf0", 1), ("kf1", 1), ("v", 1), ("kt0", 0), ("kt1", 4),
        ("A00", 1), ("A01", 1), ("A10", 1), ("A11", 1), ("O0", 0), ("outer0", 0), ("S0", 1), ("A20", 1), ("A21", 1), ("outer1", 0), ("S1", 1),
        ("A30", 1), ("A31", 1), ("O1", 0), ("outer2", 0), ("S2", 2), ("on0", 0), ("outer3", 0), ("S3", 2),
        ("on1", 6), ("onT", 2), ("wo1", 8), ("x3T", 2), ("gate", 0))
LATE_PHASES = (("start", 0, 1, (("", 0, True, False),)),
               ("middle", 0, B - 1, (("'", 1, True, True), ("", 0, True, True))),
               ("last", B - 1, 1, (("'", 1, True, True),)),
               ("end", B, 1, (("", 0, False, True),)))


def late_order(has_linear, has_experts):
    experts = []
    if has_experts:
        def up(e):
            return [f"up{e}{f}" for f in range(FT)]

        experts = ["cT", "b2"] + up(0)
        for e in range(E):
            experts += (up(e + 1) if e + 1 < E else []) + [f"down{e}{t}" for t in range(HT)]
    order = []
    for job, fill in LATE if has_linear else ():
        order += [job] + experts[:fill]
        experts = experts[fill:]
    return order + experts


class Banks:

    def __init__(self, n):
        self.used, self.phases = [0] * n, {}

    def phase(self, name, first, count, jobs):
        base, place = list(self.used), {}
        for job, bank in jobs:
            self.used[bank] += 1
            place[job] = (bank, self.used[bank])
        per = [u - b for u, b in zip(self.used, base)]
        self.phases[name] = (first, per, place)
        self.used = [b + count * p for b, p in zip(base, per)]

    def at(self, name, job, i):
        first, per, place = self.phases[name]
        bank, n = place[job]
        return bank, (i - first) * per[bank] + n


RSQRT_STEPS = 11
LN_STEPS = 4 + 3 + 3 + 1 + RSQRT_STEPS


def rsqrt(v, s, out, x, t, half):
    s.did(v.tensor_scalar(half.bitcast(I32), x.bitcast(I32), 1, None, ALU.logical_shift_right))
    s.did(v.tensor_scalar(out.bitcast(I32), half.bitcast(I32), -1.0, RSQRT_MAGIC, ALU.mult, ALU.add))
    for _ in range(3):
        s.did(v.tensor_tensor(t, out, out, ALU.mult))
        s.did(v.scalar_tensor_tensor(t, t, -0.5, x, ALU.mult, ALU.mult))
        s.did(v.scalar_tensor_tensor(out, t, 1.5, out, ALU.add, ALU.mult))


def layernorm(v, s, out, x, st, w, ready):
    v.memset(w[:, 6], 0.0)
    for u in range(HT):
        s.go(v.bn_stats(st[:, u], x[:, u]))
    s.wait()
    s.go(v.tensor_tensor(w[:, 0], st[:, :, 1], st[:, :, 4], ALU.add))
    s.go(v.tensor_tensor(w[:, 1], st[:, :, 1], st[:, :, 4], ALU.subtract))
    s.go(v.tensor_tensor(w[:, 2], st[:, :, 2], st[:, :, 5], ALU.add))
    s.wait()
    s.go(v.tensor_scalar(w[:, 6], w[:, 0], 0.5, None, ALU.mult))
    s.go(v.scalar_tensor_tensor(w[:, 3], w[:, 1], 0.25, w[:, 1], ALU.mult, ALU.mult))
    s.go(v.tensor_scalar(w[:, 4], w[:, 2], 1.0 / D, LN_EPS, ALU.mult, ALU.add))
    s.wait()
    s.did(v.tensor_tensor(w[:, 0], w[:, 3], w[:, 4], ALU.add))
    rsqrt(v, s, w[:, 5], w[:, 0], w[:, 1], w[:, 2])
    for u in range(HT):
        ins = v.tensor_scalar(out[:, u], x[:, u], w[:, 6, u:u + 1], w[:, 5, u:u + 1], ALU.subtract, ALU.mult)
    ins.then_inc(ready, 1)


def build(nc, x, w_qkvg, b_qkvg, qn_w, kn_w, w_o0, b_o0, w_gates, u_gates, b_gates, w_h, u_h, b_h, c_in,
          w_q1, w_k1, w_v1, w_o1, fm_q, fm_k, fb_q, fb_k, rms_w, w_g, w_1, b_1, w_2, b_2, consts, out):
    with ExitStack() as ctx:
        def sb(name, shape, dt=F32):
            return ctx.enter_context(nc.sbuf_tensor(name, shape, dt))

        def sem(name):
            return ctx.enter_context(nc.semaphore(name))

        qk_dram = nc.dram_tensor("qk_splits", (B, SPLITS, 2, P, N), BF16, kind="Internal").ap()
        shift_dram = nc.dram_tensor("shift_splits", (SPLITS, HG * TB, P), BF16, kind="Internal").ap()
        X = sb("X", [P, NT, D])
        xn1T = sb("xn1T", [D, NT * P])
        C2 = sb("C2", [D, N])
        const_sb = sb("const_sb", [P, NCONST])
        ident = const_sb[:, 0:P]
        causal = const_sb[:, P:2 * P]
        blocks = const_sb[:, 2 * P:3 * P]
        signs = const_sb[:, 3 * P:5 * P]
        before = const_sb[:, 5 * P:5 * P + E * E].rearrange("p (e f) -> p e f", e=E)
        sign_col = const_sb[:, 5 * P + E * E:NCONST]
        work = sb("work", [P, 7, HT])
        st = sb("st", [P, HT, 6])

        ps = ctx.enter_context(nc.psum_tensor("ps", [P, 8, 512], F32))
        S = ps[:, 0:4, :].rearrange("p (s j) q -> p s j q", s=2)
        O = ps[:, 4:6, :]
        SIDE = 6

        banks = Banks(8)
        full = [sem(f"bank{i}_full") for i in range(8)]
        free = [sem(f"bank{i}_free") for i in range(8)]

        front_jobs = {"xT": 1, "m0": 1, "m1": 0, "m2": 1, "m3": 0, "q": 1, "k": 0}
        post_jobs = {"attT": 0, "wo": 0, "x1T": 1, "f": 1, "i": 1, "g": 0}
        att_jobs = {"oT0": 0, "oT1": 0, "oT2": 1, "oT3": 0}
        order = ["attT", "xT", "wo", "m0", "m1", "m2", "m3", "x1T", "oT0", "q", "k", "f", "oT1", "i", "g", "oT2", "oT3"]
        PHASES = [("lead", -1, 0, 1, 0, 0), ("grow", 0, 1, 1, 1, 0), ("steady", 1, B - 1, 1, 1, 1),
                  ("shrink", B - 1, B, 0, 1, 1), ("tail", B, B + 1, 0, 0, 1)]
        for name, b0, b1, has_front, has_att, has_post in PHASES:
            jobs = {**(front_jobs if has_front else {}), **(att_jobs if has_att else {}), **(post_jobs if has_post else {})}
            banks.phase(name, 2 * b0, 2 * (b1 - b0), [(j, SIDE + jobs[j]) for j in order if j in jobs])
        late_banks = {"h": 0, "hT": 1, "x2T": 0, "qf0": 1, "qf1": 0, "kf0": 1, "kf1": 0, "v": 1, "kt0": 0, "kt1": 1, "A": 2, "O": 3, "S": 4,
                      "on0": 0, "on1": 1, "onT": 0, "wo1": 1, "x3T": 0, "gate": 1, "cT": 7, "b2": 7, "up": 5, "down": 7}

        def late_jobs(has_linear, has_experts, tag):
            for job in late_order(has_linear, has_experts):
                kind = "down" if job[:4] == "down" else "up" if job[:2] == "up" else job[0] if job[0] in "AOS" else job
                if job[:4] == "down" and job[-1] != "0" or job[:5] == "outer":
                    continue
                yield (job[:5] if kind == "down" else job) + tag, late_banks[kind] + (int(job[-1]) % 2 if kind == "up" else 0)

        for name, first, count, halves in LATE_PHASES:
            banks.phase(name, first, count, [pair for tag, hf, has_linear, has_experts in halves for pair in late_jobs(has_linear, has_experts, tag)])

        s_const = sem("s_const"); s_x = sem("s_x"); s_prep = sem("s_prep"); s_prep_pe = sem("s_prep_pe")
        s_zero = sem("s_zero"); s_pool = sem("s_pool")
        front_steps = sem("front_steps"); post_steps = sem("post_steps"); att_steps = sem("att_steps")
        xn_ready = sem("xn_ready"); qkn_ready = sem("qkn_ready"); x1n_ready = sem("x1n_ready")
        split_ready = sem("split_ready"); split_stored = sem("split_stored"); gate_exp = sem("gate_exp")
        loaded = [sem("loaded0"), sem("loaded1")]
        v_staged = [sem("v_staged0"), sem("v_staged1")]
        scores_ready = sem("scores_ready"); probs_ready = sem("probs_ready"); probs_used = sem("probs_used")
        o_copied = sem("o_copied"); c_ready = sem("c_ready")
        w_loaded = sem("w_loaded"); l1_steps = sem("l1_steps"); act1 = sem("act1")
        xn2_ready = sem("xn2_ready"); qbd_ready = sem("qbd_ready"); state_ready = sem("state_ready")
        on_ready = sem("on_ready"); xn3_ready = sem("xn3_ready"); state_sum = sem("state_sum")
        squared1 = sem("squared1"); x3_static = sem("x3_static")
        hid_ready = sem("hid_ready"); hid_used = sem("hid_used"); moe_steps = sem("moe_steps")
        combT_ready = sem("combT_ready"); stored = sem("stored")
        combT_ps = sem("combT_ps")

        FRONT_STEPS = LN_STEPS + 3 + RSQRT_STEPS + 1 + 3 + 2
        POST_STEPS = 1 + LN_STEPS + 1 + 2
        L1_STEPS = 2 * LN_STEPS + 2 + RSQRT_STEPS + 1 + 2 + 2 * HT + 4
        MOE_STEPS = 3 * E
        CONST_LOADS = 11
        LATE_LOADS = 13
        ones_loaded = sem("ones_loaded"); shift_ready = sem("shift_ready"); shift_loaded = sem("shift_loaded"); shift_stored = sem("shift_stored")
        max_scores = sem("max_scores"); max_taken = sem("max_taken"); max_turned = sem("max_turned"); shift_steps = sem("shift_steps")
        s_prep2 = sem("s_prep2"); we_loaded = sem("we_loaded")

        with ExitStack() as part:
            def pb(name, shape, dt=F32):
                return part.enter_context(nc.sbuf_tensor(name, shape, dt))

            wqkvg = pb("wqkvg", [D, W0])
            bqkvg = pb("bqkvg", [P, W0])
            qnw = pb("qnw", [P, D])
            kscale = pb("kscale", [P, D])
            wo0 = pb("wo0", [D, D])
            bo0 = pb("bo0", [P, D])
            wg3 = pb("wg3", [D, 3, D])
            ug3 = pb("ug3", [D, 3, D])
            bg3 = pb("bg3", [D, 3])
            c0 = pb("c0", [D, 1])
            stF = pb("stF", [P, HT, 6])
            wF = pb("wF", [P, 7, HT])
            rr = pb("rr", [P, 4, 2 * H0 * HT])
            xn = pb("xn", [P, HT, D])
            xnT = pb("xnT", [D, HN])
            qk = pb("qk", [P, HT, 2 * D])
            sq = pb("sq", [P, HT, 2 * D])
            rest = pb("rest", [P, 2, HN])
            split = pb("split", [P, SPLITS, 2, HN], BF16)
            VG = pb("VG", [P, NT, D + H0])
            G = pb("G", [P, NT, H0])
            gexp = pb("gexp", [P, HT, H0])
            Q_st = pb("Q_st", [KROWS, 2, HG, N], BF16)
            K_st = pb("K_st", [KROWS, 2, HG, N], BF16)
            V_st = pb("V_st", [P, 2, TB, HG, VW])
            prob = pb("prob", [P, PROBS, 2, HN])
            OT = pb("OT", [P, 2, HN])
            rden = pb("rden", [P, 2, HG * HT])
            att = pb("att", [P, NT, D])
            att_static = pb("att_static", [P, HT, D])
            attT = pb("attT", [D, HN])
            x1n = pb("x1n", [P, HT, D])
            tg = pb("tg", [D, 3, HN])
            bound = pb("bound", [P, 1])
            shift_flag = pb("shift_flag", [1, 1], I32)
            row_max = pb("row_max", [P, HG * TB])
            shift = pb("shift", [HG * TB, P])
            shift_split = pb("shift_split", [HG * TB, SPLITS, P], BF16)
            block = part.enter_context(nc.Block())

            def phases(eng, body):
                for name, b0, b1, has_front, has_att, has_post in PHASES:
                    if b1 - b0 == 1:
                        with eng.Fori(0, 2) as hp:
                            body(name, b0, hp, has_front, has_att, has_post)
                    else:
                        with eng.Fori(b0, b1) as b:
                            with eng.Fori(0, 2) as hp:
                                body(name, b, hp, has_front, has_att, has_post)

            @block.sync
            def _(sp):
                sp.dma_start(X[:, 0:TB], x[0:N].rearrange("(t p) d -> p t d", p=P)).then_inc(s_x, 16)
                loads = ((wqkvg, w_qkvg), (bqkvg, b_qkvg.partition_broadcast(P)), (qnw, qn_w.partition_broadcast(P)),
                         (kscale, kn_w.partition_broadcast(P)), (const_sb, consts), (wo0, w_o0), (bo0, b_o0.partition_broadcast(P)),
                         (wg3, w_gates), (ug3, u_gates), (bg3, b_gates), (c0, c_in))
                assert len(loads) == CONST_LOADS
                for dst, src in loads:
                    sp.dma_start(dst[:], src).then_inc(s_const, 16)
                sp.dma_start(X[:, TB:], x[N:].rearrange("(t p) d -> p t d", p=P)).then_inc(s_x, 16)

                def store_splits(b, hp):
                    sp.wait_ge(split_ready, 2 * b + hp + 1)
                    sp.dma_start(qk_dram[b, :, :, :, hp * HN:(hp + 1) * HN].rearrange("s a p t -> p (s a) t"),
                                 split[:].rearrange("p s a t -> p (s a) t")).then_inc(split_stored, 16)

                def load_group(b, hp, i, before_it=True):
                    if i == 0 and hp == 0:
                        sp.wait_ge(split_stored, 32 * (b + 1))
                    if before_it:
                        sp.wait_ge(scores_ready, 2 * SLOTS * (2 * b + hp - 1) + SLOTS * (i + 1))
                    heads = (2 * hp + i) * HG * HD
                    for c in range(SPLITS):
                        for s in range(SPLITS):
                            row = HD * (SPLITS * c + s)
                            for a, dst, which in ((0, Q_st, c), (1, K_st, s)):
                                sp.dma_start(dst[row:row + HD, i],
                                             qk_dram[b, which, a, heads:heads + HG * HD, :].rearrange("(j d) t -> d j t", d=HD)
                                             ).then_inc(loaded[i], 16)

                sp.wait_ge(s_zero, 3)
                sp.dma_start(K_st[SHIFT_ROW:SHIFT_ROW + SPLITS], Q_st[0:SPLITS]).then_inc(ones_loaded, 16)
                sp.wait_ge(ones_loaded, 16)
                store_splits(0, 0)
                store_splits(0, 1)
                load_group(0, 0, 0, False)
                load_group(0, 0, 1, False)
                sp.wait_ge(s_prep, 5)
                shifted = sp.value_load(shift_flag[0:1, 0:1], min_val=0, max_val=1)

                def load_shift(it, i):
                    with sp.If(shifted != 0):
                        sp.wait_ge(shift_ready, 2 * it + i + 1)
                        sp.dma_start(shift_dram.rearrange("s r q -> r s q"), shift_split[:]).then_inc(shift_stored, 16)
                        sp.wait_ge(shift_stored, 16 * (2 * it + i + 1))
                        sp.dma_start(Q_st[SHIFT_ROW:SHIFT_ROW + SPLITS, i].rearrange("p j t -> p (j t)"),
                                     shift_dram.rearrange("s r q -> s (r q)")).then_inc(shift_loaded, 16)

                with sp.Fori(0, B - 1) as b:
                    for hp in range(2):
                        load_shift(2 * b + hp, 0)
                        store_splits(b + 1, hp)
                        load_shift(2 * b + hp, 1)
                        load_group(b + hp, 1 - hp, 0)
                        load_group(b + hp, 1 - hp, 1)
                load_shift(2 * B - 2, 0)
                load_shift(2 * B - 2, 1)
                load_group(B - 1, 1, 0)
                load_group(B - 1, 1, 1)
                load_shift(2 * B - 1, 0)
                load_shift(2 * B - 1, 1)

            @block.gpsimd
            def _(pool):
                pool.memset(V_st[:], 0.0).then_inc(s_pool, 1)
                pool.wait_ge(s_pool, 1)
                pool.memset(V_st[:, :, :, :, HD:HD + 1], 1.0).then_inc(s_pool, 1)
                pool.wait_ge(s_pool, 2)

                def stage(b, hp, i, phase):
                    if i == 0 and hp == 0:
                        k, n = banks.at(phase, "m3", 2 * b - 1)
                        pool.wait_ge(free[k], n)
                    if phase != "lead":
                        pool.wait_ge(probs_used, SLOTS * (2 * b + hp - 1) + SLOTS // 2 * (i + 1))
                    heads = (2 * hp + i) * HG * HD
                    pool.tensor_copy(V_st[:, i, :, :, 0:HD],
                                     VG[:, bass.ds(b * TB, TB), heads:heads + HG * HD].rearrange("p k (j d) -> p k j d", d=HD)
                                     ).then_inc(v_staged[i], 1)

                stage(0, 0, 0, "lead")
                stage(0, 0, 1, "lead")
                for hp in range(2):
                    for i in range(2):
                        stage(hp, 1 - hp, i, "grow")
                with pool.Fori(1, B - 1) as b:
                    for hp in range(2):
                        for i in range(2):
                            stage(b + hp, 1 - hp, i, "steady")
                for i in range(2):
                    stage(B - 1, 1, i, "shrink")

            @block.vector
            def _(v):
                v.memset(Q_st[64:KROWS], 0.0).then_inc(s_zero, 1)
                v.memset(K_st[64:KROWS], 0.0).then_inc(s_zero, 1)
                v.memset(Q_st[0:SPLITS], 1.0).then_inc(s_zero, 1)
                v.wait_ge(s_const, 16 * CONST_LOADS)
                v.scalar_tensor_tensor(kscale[:], qnw[:], float(HD) ** -0.5, kscale[:], ALU.mult, ALU.mult).then_inc(s_prep, 1)
                v.tensor_scalar(ug3[:], ug3[:], 0.5, None, ALU.mult).then_inc(s_prep, 1)
                v.tensor_scalar(bg3[:, 0:2], bg3[:, 0:2], 0.5, None, ALU.mult).then_inc(s_prep, 1)
                v.tensor_scalar(C2[:], c0[:].to_broadcast([D, N]), 2.0, None, ALU.mult).then_inc(c_ready, 1)
                v.wait_ge(s_prep, 3)
                v.tensor_reduce(bound[:], kscale[:], AX_X, ALU.max, apply_absolute_value=True).then_inc(s_prep, 1)
                v.wait_ge(s_prep, 4)
                v.tensor_scalar(shift_flag[:], bound[0:1], float(HD), SHIFT_ABOVE, ALU.mult, ALU.is_gt).then_inc(s_prep, 1)
                v.wait_ge(s_prep, 5)
                shifted = v.value_load(shift_flag[0:1, 0:1], min_val=0, max_val=1)
                v.wait_ge(s_x, 32)

                def body(name, b, hp, has_front, has_att, has_post):
                    it = 2 * b + hp
                    f = Steps(v, front_steps, (it + 2) * FRONT_STEPS, FRONT_STEPS)
                    q = Steps(v, post_steps, (it - 2) * POST_STEPS, POST_STEPS)
                    TF = (b + 1) * TB + hp * HT
                    TP = (b - 1) * TB + hp * HT
                    XP = X[:, bass.ds(TP, HT)] if has_post else None

                    def product(job):
                        k, n = banks.at(name, job, it)
                        v.wait_ge(full[k], n)
                        return k

                    def was_read(job):
                        k, n = banks.at(name, job, it)
                        v.wait_ge(free[k], n)

                    def output(unit):
                        qh, g = unit % 2, 2 * hp + unit // 2
                        T4 = bass.ds(b * TB + HT * qh, HT)
                        v.wait_ge(probs_used, it * SLOTS + (unit + 1) * TB)
                        v.tensor_copy(OT[:, qh], O[:, qh]).then_inc(o_copied, 1)
                        k = product(f"oT{unit}")
                        oT = ps[:, k].rearrange("p (t j c) -> p t j c", t=HT, j=HG)
                        r = rden[:].rearrange("p a (t j) -> p a t j", t=HT)
                        a = Steps(v, att_steps, (4 * it + unit) * 2, 2)
                        a.did(v.reciprocal(r[:, 0], oT[:, :, :, HD]))
                        a.did(v.tensor_tensor(r[:, 1], r[:, 0], G[:, T4, bass.ds(g * HG, HG)], ALU.mult))
                        a.end()
                        v.tensor_tensor(att[:, T4, bass.ds(g * HG * HD, HG * HD)].rearrange("p t (j d) -> p t j d", d=HD),
                                        oT[:, :, :, 0:HD], r[:, 1].unsqueeze(3).to_broadcast([P, HT, HG, HD]), ALU.mult).then_inc(free[k], 1)

                    def largest_scores(i):
                        with v.If(shifted != 0):
                            with v.Fori(0, HG) as j:
                                with v.Fori(0, TB // 2) as t:
                                    for u in range(2):
                                        n = j * TB + 2 * t + u
                                        v.wait_ge(max_scores, (2 * it + i) * HG * TB + n + 1)
                                        v.tensor_reduce(row_max[:, bass.ds(n, 1)], S[:, u], AX_XY, ALU.max).then_inc(max_taken, 1)
                            v.wait_ge(max_turned, 2 * it + i + 1)
                            e = Steps(v, shift_steps, (2 * it + i) * 5, 5)
                            e.did(v.tensor_scalar(shift[:], ps[0:HG * TB, 0, 0:P], -1.0, None, ALU.mult))
                            for s in range(2):
                                e.did(v.tensor_copy(shift_split[:, s], shift[:]))
                                e.did(v.tensor_tensor(shift[:], shift[:], shift_split[:, s], ALU.subtract))
                            e.end()
                            v.tensor_copy(shift_split[:, 2], shift[:]).then_inc(shift_ready, 1)

                    if has_att:
                        largest_scores(0)
                    if has_post:
                        q.go(v.tensor_copy(att_static[:], att[:, bass.ds(TP, HT)]))
                    if has_front:
                        layernorm(v, f, xn[:], X[:, bass.ds(TF, HT)], stF, wF, xn_ready)
                    if has_post:
                        k = product("attT")
                        v.tensor_copy(attT[:], ps[:, k]).then_inc(free[k], 1)
                    if has_front:
                        k = product("xT")
                        v.tensor_copy(xnT[:], ps[:, k]).then_inc(free[k], 1)
                    if has_post:
                        k = product("wo")
                        v.tensor_tensor(XP, ps[:, k].rearrange("p (t d) -> p t d", t=HT), XP, ALU.add).then_inc(free[k], 1)
                        was_read("wo")
                        q.did(v.tensor_tensor(XP, XP, bo0[:].unsqueeze(1).to_broadcast([P, HT, D]), ALU.add))
                    if has_front:
                        for u in range(HT):
                            k = product(f"m{u}")
                            v.tensor_tensor(qk[:, u], ps[:, k, 0:2 * D], bqkvg[:, 0:2 * D], ALU.add)
                            v.tensor_tensor(VG[:, TF + u], ps[:, k, 2 * D:W0], bqkvg[:, 2 * D:W0], ALU.add).then_inc(free[k], 1)
                    if has_post:
                        layernorm(v, q, x1n[:], XP, st, work, x1n_ready)
                    if has_front:
                        was_read("m3")
                        f.did(v.tensor_tensor(sq[:], qk[:], qk[:], ALU.mult))
                        f.did(v.tensor_reduce(rr[:, 1], sq[:].rearrange("p t (h d) -> p (t h) d", d=HD), AX_X, ALU.add))
                        f.did(v.tensor_scalar(rr[:, 0], rr[:, 1], 1.0 / HD, RMS0_EPS, ALU.mult, ALU.add))
                        rsqrt(v, f, rr[:, 3], rr[:, 0], rr[:, 1], rr[:, 2])
                        qk_heads = qk[:].rearrange("p t (h d) -> p (t h) d", d=HD)
                        f.did(v.tensor_tensor(qk_heads, qk_heads, rr[:, 3].unsqueeze(2).to_broadcast([P, HT * 2 * H0, HD]), ALU.mult))
                        v.tensor_tensor(qk[:, :, D:], qk[:, :, D:], kscale[:].unsqueeze(1).to_broadcast([P, HT, D]), ALU.mult).then_inc(qkn_ready, 1)
                    if has_post:
                        k = product("x1T")
                        v.tensor_copy(xn1T[:, bass.ds(TP * P, HN)], ps[:, k]).then_inc(free[k], 1)
                    if has_att:
                        output(0)
                    if has_front:
                        v.wait_ge(split_stored, 16 * (it + 2))
                        for a, job in ((0, "q"), (1, "k")):
                            k = product(job)
                            f.did(v.tensor_copy(split[:, 0, a], ps[:, k]))
                            v.tensor_tensor(rest[:, a], ps[:, k], split[:, 0, a], ALU.subtract).then_inc(free[k], 1)
                        was_read("q")
                        was_read("k")
                        f.did(v.tensor_copy(split[:, 1], rest[:]))
                        v.tensor_tensor(split[:, 2], rest[:], split[:, 1], ALU.subtract).then_inc(split_ready, 1)
                        v.wait_ge(gate_exp, it + 3)
                        f.did(v.tensor_scalar(gexp[:], gexp[:], 1.0, None, ALU.add))
                        f.go(v.reciprocal(G[:, bass.ds(TF, HT)], gexp[:]))
                        f.end()
                    if has_att:
                        largest_scores(1)
                        output(1)
                        output(2)
                    if has_post:
                        for job in "fig":
                            was_read(job)
                        CP = C2[:, bass.ds(hp * HN, HN)]
                        q.go(v.scalar_tensor_tensor(tg[:, 0], tg[:, 0], 1.0, CP, ALU.add, ALU.mult))
                        q.did(v.scalar_tensor_tensor(tg[:, 1], tg[:, 1], 1.0, tg[:, 2], ALU.add, ALU.mult))
                        v.scalar_tensor_tensor(CP, tg[:, 0], 0.5, tg[:, 1], ALU.mult, ALU.add).then_inc(c_ready, 1)
                        q.end()
                    if has_att:
                        output(3)

                phases(v, body)

            @block.scalar
            def _(act):
                act.wait_ge(s_const, 16 * CONST_LOADS)
                act.wait_ge(s_prep, 3)

                def body(name, b, hp, has_front, has_att, has_post):
                    it = 2 * b + hp

                    def gates():
                        k, n = banks.at(name, "m3", it)
                        act.wait_ge(free[k], n)
                        act.activation(gexp[:], VG[:, bass.ds((b + 1) * TB + hp * HT, HT), D:], ACT.Exp, scale=-1.0).then_inc(gate_exp, 1)

                    def tanh(n_gate, job):
                        k, n = banks.at(name, job, it)
                        act.wait_ge(full[k], n)
                        act.wait_ge(c_ready, it - 1)
                        act.activation(tg[:, n_gate], ps[:, k], ACT.Tanh, bias=bg3[:, n_gate:n_gate + 1],
                                       scale=(0.5 if n_gate < 2 else 1.0)).then_inc(free[k], 1)

                    for slot in range(SLOTS if has_att else 1):
                        if has_att:
                            for pair in range(2):
                                n = 2 * slot + pair
                                act.wait_ge(scores_ready, 2 * SLOTS * it + n + 1)
                                if pair == 0 and n >= PROBS:
                                    act.wait_ge(probs_used, SLOTS * it + (n - PROBS) // 2 + 1)
                                act.activation(prob[:, n % PROBS], S[:, n % 2], ACT.Exp).then_inc(probs_ready, 1)
                        if has_front and slot == (GATES_AT if has_att else 0):
                            gates()
                        for g, job in enumerate("fig"):
                            if has_post and slot == (TANH_AT[g] if has_att else 0):
                                tanh(g, job)

                phases(act, body)

            @block.tensor
            def _(pe):
                pe.wait_ge(s_const, 16 * CONST_LOADS)
                pe.wait_ge(s_prep, 5)
                shifted = pe.value_load(shift_flag[0:1, 0:1], min_val=0, max_val=1)

                def body(name, b, hp, has_front, has_att, has_post):
                    it = 2 * b + hp

                    def bank(job):
                        k, n = banks.at(name, job, it)
                        pe.wait_ge(free[k], n - 1)
                        return k

                    def transposed(job, src):
                        k = bank(job)
                        for t in range(HT):
                            mm = pe.transpose(ps[:, k, t * P:(t + 1) * P], src(t), ident)
                        mm.then_inc(full[k], 1)

                    def was_read(job):
                        k, n = banks.at(name, job, it)
                        pe.wait_ge(free[k], n)

                    def x_transpose():
                        pe.wait_ge(xn_ready, it + 3)
                        transposed("xT", lambda t: xn[:, t])

                    def project(u):
                        if u == 0:
                            was_read("xT")
                        k = bank(f"m{u}")
                        pe.matmul(ps[:, k, 0:W0], xnT[:, u * P:(u + 1) * P], wqkvg[:], start=True, stop=True).then_inc(full[k], 1)

                    def qk_transpose(a):
                        pe.wait_ge(qkn_ready, it + 3)
                        transposed("qk"[a], lambda t: qk[:, t, a * D:(a + 1) * D])

                    def att_transpose():
                        pe.wait_ge(post_steps, (it - 2) * POST_STEPS + 1)
                        transposed("attT", lambda t: att_static[:, t])

                    def project_out():
                        was_read("attT")
                        k = bank("wo")
                        for t in range(HT):
                            mm = pe.matmul(ps[:, k, t * P:(t + 1) * P], attT[:, t * P:(t + 1) * P], wo0[:], start=True, stop=True)
                        mm.then_inc(full[k], 1)

                    def x1_transpose():
                        pe.wait_ge(x1n_ready, it - 1)
                        transposed("x1T", lambda t: x1n[:, t])

                    def gate_x(g):
                        if g == 0:
                            was_read("x1T")
                            pe.wait_ge(c_ready, it - 2)
                        k = bank("fig"[g])
                        pe.matmul(ps[:, k], wg3[:, g], xn1T[:, bass.ds(((b - 1) * 2 + hp) * HN, HN)], start=True, stop=False)

                    def gate_c(g):
                        k, _ = banks.at(name, "fig"[g], it)
                        pe.matmul(ps[:, k], ug3[:, g], C2[:, bass.ds(hp * HN, HN)], start=False, stop=True).then_inc(full[k], 1)

                    def out_transpose(unit):
                        pe.wait_ge(o_copied, 4 * it + unit + 1)
                        qh = unit % 2
                        k = bank(f"oT{unit}")
                        for t in range(HT):
                            mm = pe.transpose(ps[:, k, t * P:(t + 1) * P], OT[:, qh, t * P:(t + 1) * P], ident)
                        mm.then_inc(full[k], 1)

                    pieces = []
                    if has_post:
                        pieces += [(0, att_transpose, ()), (3, project_out, ()), (9, x1_transpose, ()),
                                   (15, gate_x, (0,)), (16, gate_c, (0,)), (20, gate_x, (1,)), (21, gate_c, (1,)),
                                   (23, gate_x, (2,)), (24, gate_c, (2,))]
                    if has_front:
                        pieces += [(2, x_transpose, ())] + [(4 + u, project, (u,)) for u in range(HT)]
                        pieces += [(12, qk_transpose, (0,)), (13, qk_transpose, (1,))]
                    if has_att:
                        pieces += [(10, out_transpose, (0,)), (18, out_transpose, (1,)), (26, out_transpose, (2,))]
                    pieces.sort(key=lambda piece: piece[0])

                    def all_scores(i):
                        with pe.If(shifted != 0):
                            with pe.Fori(0, HG) as j:
                                with pe.Fori(0, TB // 2) as t:
                                    for u in range(2):
                                        n = j * TB + 2 * t + u
                                        pe.wait_ge(max_taken, (2 * it + i) * HG * TB + (2 * t + j * TB))
                                        if u == 0:
                                            pe.wait_ge(probs_ready, 2 * SLOTS * it + SLOTS * i)
                                        for half in range(2):
                                            mm = pe.matmul(S[:, u, half], Q_st[0:SHIFT_ROW, i, j, bass.ds((2 * t + u) * P, P)],
                                                           K_st[0:SHIFT_ROW, i, j, half * HN:(half + 1) * HN], start=True, stop=True)
                                        mm.then_inc(max_scores, 1)
                            pe.wait_ge(max_taken, (2 * it + i + 1) * HG * TB)
                            pe.transpose(ps[0:HG * TB, 0, 0:P], row_max[:], ident).then_inc(max_turned, 1)
                            pe.wait_ge(shift_loaded, 16 * (2 * it + i + 1))

                    def scores(n):
                        i, m = n // (2 * 2 * TB), n % (2 * 2 * TB)
                        qh, kt, pair = m // (2 * TB), (m // 2) % TB, m % 2
                        if m == 0:
                            pe.wait_ge(loaded[i], LOADS * (it + 1))
                            all_scores(i)
                        if n >= 2:
                            pe.wait_ge(probs_ready, 2 * SLOTS * it + n - 1)
                        for j in range(2):
                            mm = pe.matmul(S[:, n % 2, j], K_st[:, i, 2 * pair + j, kt * P:(kt + 1) * P],
                                           Q_st[:, i, 2 * pair + j, qh * HN:(qh + 1) * HN], start=True, stop=True)
                        mm.then_inc(scores_ready, 1)

                    def values(slot):
                        i, qh, kt = slot // (2 * TB), (slot // TB) % 2, slot % TB
                        if slot % (2 * TB) == 0:
                            pe.wait_ge(v_staged[i], it + 1)
                        if kt == 0 and slot >= 2 * TB:
                            pe.wait_ge(o_copied, 4 * it + slot // TB - 1)
                        pe.wait_ge(probs_ready, 2 * SLOTS * it + 2 * slot + 2)
                        for j in range(HG):
                            mm = pe.matmul(O[VW * j:VW * (j + 1), qh], V_st[:, i, kt, j], prob[:, (2 * slot + j // 2) % PROBS, j % 2],
                                           start=(kt == 0), stop=(kt == TB - 1))
                        mm.then_inc(probs_used, 1)

                    if has_att:
                        pe.wait_ge(probs_ready, 2 * SLOTS * it)
                        scores(0)
                        scores(1)
                    for slot in range(SLOTS if has_att else 1):
                        if has_att:
                            if slot < SLOTS - 1:
                                scores(2 * slot + 2)
                            if slot:
                                values(slot - 1)
                        while pieces and (pieces[0][0] <= slot or not has_att):
                            _, piece, args = pieces.pop(0)
                            piece(*args)
                        if has_att and slot < SLOTS - 1:
                            scores(2 * slot + 3)
                    if has_att:
                        values(SLOTS - 1)
                        out_transpose(3)

                phases(pe, body)

        with ExitStack() as part:
            def pb(name, shape, dt=F32):
                return part.enter_context(nc.sbuf_tensor(name, shape, dt))

            wh = pb("wh", [D, D])
            uh = pb("uh", [D, D])
            bh = pb("bh", [D, 1])
            wq1 = pb("wq1", [D, D])
            wk1 = pb("wk1", [D, D])
            wv1 = pb("wv1", [D, D])
            wo1 = pb("wo1", [D, D])
            fmq = pb("fmq", [D, 2 * D])
            fmk = pb("fmk", [D, 2 * D])
            fb = pb("fb", [D, 2])
            rmsw = pb("rmsw", [D, 1])
            wqf = pb("wqf", [D, 2 * D])
            wkf = pb("wkf", [D, 2 * D])
            wg = pb("wg", [D, E])
            w1 = pb("w1", [D, E, F])
            w2 = pb("w2", [P, E, FT, D])
            b1 = pb("b1", [P, E, FT])
            b2 = pb("b2", [E, D])
            hT = pb("hT", [D, HN])
            xn2 = pb("xn2", [P, HT, D])
            xn2T = pb("xn2T", [D, HN])
            Qf = pb("Qf", [P, G1, HN])
            Kf = pb("Kf", [P, G1, HN])
            Qbd = pb("Qbd", [P, G1, HG, HN])
            V1 = pb("V1", [P, HT, H1, VW])
            Kt = pb("Kt", [P, G1, HT, P])
            Am = pb("Am", [P, 2, G1, HG, P])
            state = pb("state", [P, 2, G1, P])
            oT1 = pb("oT1", [P, HT, G1, P])
            sq1 = pb("sq1", [P, HT, H1, DK])
            rr1 = pb("rr1", [P, 4, HT * H1])
            on = pb("on", [P, HT, D])
            onT = pb("onT", [D, HN])
            xn3 = pb("xn3", [P, HT, D])
            x3s = pb("x3s", [D, HN])
            sg = pb("sg", [P, HT, E])
            pairs = pb("pairs", [P, 2, HT * E, E])
            combT = pb("combT", [E, HN])
            comb = pb("comb", [P, 2, HT, E])
            hid = pb("hid", [P, 2, FT, HN])
            block = part.enter_context(nc.Block())

            def halves(eng, body):
                for phase, b0, count, parts in LATE_PHASES:
                    if count == 1:
                        for tag, hf, has_linear, has_experts in parts:
                            body(phase, b0, tag, hf, has_linear, has_experts)
                    else:
                        with eng.Fori(b0, b0 + count) as b:
                            for tag, hf, has_linear, has_experts in parts:
                                body(phase, b, tag, hf, has_linear, has_experts)

            def half_of(b, tag, hf, phase):
                return 2 * b + (2 if phase == "middle" and hf == 0 else hf)

            def wait_full(eng, phase, job, i):
                k, n = banks.at(phase, job, i)
                eng.wait_ge(full[k], n)
                return k

            def wait_free(eng, phase, job, i, before=0):
                k, n = banks.at(phase, job, i)
                eng.wait_ge(free[k], n - before)
                return k

            @block.sync
            def _(sp):
                loads = ((wh, w_h), (uh, u_h), (bh, b_h), (wq1, w_q1), (wk1, w_k1), (wv1, w_v1), (wo1, w_o1), (fmq, fm_q), (fmk, fm_k),
                         (rmsw, rms_w), (wg, w_g))
                assert len(loads) + 2 == LATE_LOADS
                for dst, src in loads:
                    sp.dma_start(dst[:], src).then_inc(w_loaded, 16)
                sp.dma_start(fb[:, 0:1], fb_q).then_inc(w_loaded, 16)
                sp.dma_start(fb[:, 1:2], fb_k).then_inc(w_loaded, 16)
                for dst, src in ((w1, w_1), (w2, w_2), (b1, b_1), (b2, b_2)):
                    sp.dma_start(dst[:], src).then_inc(we_loaded, 16)

                def store(phase, b, tag, hf, has_linear, has_experts):
                    if has_experts:
                        m = half_of(b, tag, hf, phase) - 1
                        wait_free(sp, phase, f"down{E - 1}{tag}", b)
                        sp.dma_start(out[bass.ds(m * HN, HN), :].rearrange("(t p) d -> p t d", p=P), X[:, bass.ds(m * HT, HT)]).then_inc(stored, 16)

                halves(sp, store)
                sp.wait_ge(stored, 16 * 2 * B)

            @block.vector
            def _(v):
                v.memset(Qbd[:], 0.0).then_inc(s_prep2, 1)
                v.memset(V1[:], 0.0).then_inc(s_prep2, 1)
                v.wait_ge(w_loaded, 16 * LATE_LOADS)
                v.tensor_scalar(uh[:], uh[:], 0.5, None, ALU.mult).then_inc(s_prep2, 1)
                v.tensor_scalar(wo1[:], wo1[:], rmsw[:], None, ALU.mult).then_inc(s_prep2, 1)
                v.tensor_tensor(fmq[:], fmq[:], signs, ALU.mult).then_inc(s_prep2, 1)
                v.tensor_tensor(fmk[:], fmk[:], signs, ALU.mult).then_inc(s_prep2, 1)
                v.tensor_tensor(fb[:], fb[:], sign_col.to_broadcast([D, 2]), ALU.mult).then_inc(s_prep2, 1)
                v.wait_ge(s_prep2, 7)
                v.tensor_scalar(fb[:, 0:1], fb[:, 0:1], -0.5 * math.log(DF), None, ALU.add).then_inc(s_prep2, 1)
                v.wait_ge(s_prep_pe, 2)
                v.tensor_copy(wqf[:], ps[:, 0, 0:2 * D]).then_inc(s_prep2, 1)
                v.tensor_copy(wkf[:], ps[:, 1, 0:2 * D]).then_inc(s_prep2, 1)

                def body(phase, b, tag, hf, has_linear, has_experts):
                    h = half_of(b, tag, hf, phase)
                    s = Steps(v, l1_steps, h * L1_STEPS, L1_STEPS)
                    m = Steps(v, moe_steps, (h - 1) * MOE_STEPS, MOE_STEPS)
                    X4 = X[:, bass.ds(h * HT, HT)] if has_linear else None
                    XE = X[:, bass.ds((h - 1) * HT, HT)] if has_experts else None

                    def product(job):
                        return wait_full(v, phase, job + tag, b)

                    def was_read(job):
                        wait_free(v, phase, job + tag, b)

                    if has_experts:
                        v.wait_ge(l1_steps, h * L1_STEPS)
                    for job in late_order(has_linear, has_experts):
                        if job == "hT":
                            k = product("hT")
                            v.tensor_tensor(X4, ps[:, k].rearrange("p (t d) -> p t d", t=HT), X4, ALU.add).then_inc(free[k], 1)
                            was_read("hT")
                            layernorm(v, s, xn2[:], X4, st, work, xn2_ready)
                        elif job == "x2T":
                            k = product("x2T")
                            v.tensor_copy(xn2T[:], ps[:, k]).then_inc(free[k], 1)
                        elif job == "kf1":
                            was_read("qf0")
                            was_read("qf1")
                            for j in range(HG):
                                rows = slice(DF * j, DF * (j + 1))
                                ins = v.tensor_copy(Qbd[rows, :, j], Qf[rows])
                            ins.then_inc(qbd_ready, 1)
                        elif job == "v":
                            k = product("v")
                            v.tensor_copy(V1[:, :, :, 0:DK], ps[:, k].rearrange("p (t h d) -> p t h d", t=HT, h=H1)).then_inc(free[k], 1)
                        elif job[0] == "A":
                            c, g = int(job[1]), int(job[2])
                            k = product(job)
                            v.tensor_tensor(Am[:, c % 2, g], ps[:, k].rearrange("p (j q) -> p j q", j=HG), causal.unsqueeze(1).to_broadcast([P, HG, P]),
                                            ALU.mult).then_inc(free[k], 1)
                        elif job[0] == "S":
                            c = int(job[1])
                            k = product(job)
                            v.tensor_tensor(state[:, (c + 1) % 2], ps[:, k, 0:G1 * P].rearrange("p (g v) -> p g v", g=G1),
                                            blocks.unsqueeze(1).to_broadcast([P, G1, P]), ALU.mult).then_inc(free[k], 1)
                        elif job == "on1":
                            v.wait_ge(squared1, 2 * h + 2)
                            s.did(v.tensor_reduce(rr1[:, 1], sq1[:].rearrange("p t h d -> p (t h) d"), AX_X, ALU.add))
                            s.did(v.tensor_scalar(rr1[:, 0], rr1[:, 1], 1.0 / DK, RMS1_EPS, ALU.mult, ALU.add))
                            rsqrt(v, s, rr1[:, 3], rr1[:, 0], rr1[:, 1], rr1[:, 2])
                            for a in range(2):
                                k = product(f"on{a}")
                                for c in range(2):
                                    ins = v.tensor_tensor(on[:, 2 * a + c].rearrange("p (h d) -> p h d", h=H1),
                                                          ps[:, k, 2 * c * P:2 * (c + 1) * P].rearrange("p (h d) -> p h d", h=H1)[:, :, 0:DK],
                                                          rr1[:, 3, (2 * a + c) * H1:(2 * a + c + 1) * H1].unsqueeze(2).to_broadcast([P, H1, DK]), ALU.mult)
                                ins.then_inc(free[k], 1)
                        elif job == "onT":
                            k = product("onT")
                            v.tensor_copy(onT[:], ps[:, k]).then_inc(free[k], 1)
                        elif job == "wo1":
                            k = product("wo1")
                            v.tensor_tensor(X4, ps[:, k].rearrange("p (t d) -> p t d", t=HT), X4, ALU.add).then_inc(free[k], 1)
                            was_read("wo1")
                            layernorm(v, s, xn3[:], X4, st, work, xn3_ready)
                        elif job == "x3T":
                            k = product("x3T")
                            s.did(v.tensor_copy(x3s[:], ps[:, k]))
                            v.tensor_copy(xn1T[:, bass.ds(h * HN, HN)], x3s[:]).then_inc(free[k], 1)
                        elif job == "gate":
                            was_read("gate")
                            s.did(v.tensor_scalar(sg[:], sg[:], 1.0, None, ALU.add))
                            s.did(v.reciprocal(sg[:], sg[:]))
                            for t in range(HT):
                                mine = sg[:, t].unsqueeze(2).to_broadcast([P, E, E])
                                other = sg[:, t].unsqueeze(1).to_broadcast([P, E, E])
                                s.go(v.tensor_tensor(pairs[:, 0, t * E:(t + 1) * E], other, mine, ALU.is_gt))
                                s.go(v.tensor_tensor(pairs[:, 1, t * E:(t + 1) * E], other, mine, ALU.is_equal))
                            s.wait()
                            p4 = pairs[:, 1].rearrange("p (t e) f -> p t e f", t=HT)
                            s.did(v.tensor_tensor(p4, p4, before.unsqueeze(1).to_broadcast([P, HT, E, E]), ALU.mult))
                            s.did(v.tensor_tensor(pairs[:, 0], pairs[:, 0], pairs[:, 1], ALU.add))
                            s.did(v.tensor_reduce(rr1[:, 0], pairs[:, 0], AX_X, ALU.add))
                            s.go(v.scalar_tensor_tensor(comb[:, hf].rearrange("p t e -> p (t e)"), rr1[:, 0], 2.0,
                                                        sg[:].rearrange("p t e -> p (t e)"), ALU.is_lt, ALU.mult))
                            s.end()
                        elif job == "cT":
                            k = product("cT")
                            v.tensor_copy(combT[:], ps[0:E, k]).then_inc(free[k], 1)
                        elif job == "b2":
                            k = product("b2")
                            v.tensor_tensor(XE, ps[:, k].rearrange("p (t d) -> p t d", t=HT), XE, ALU.add).then_inc(free[k], 1)
                        elif job[:4] == "down" and int(job[-1]) == HT - 1:
                            e = int(job[4])
                            k = product(f"down{e}")
                            if e:
                                m.wait()
                            was_read(f"down{e - 1}" if e else "b2")
                            for t in range(HT):
                                row = X[:, (h - 1) * HT + t]
                                ins = v.scalar_tensor_tensor(row, ps[:, k, t * D:(t + 1) * D], comb[:, 1 - hf, t, e:e + 1], row, ALU.mult, ALU.add)
                                if t < HT - 1:
                                    m.go(ins)
                            ins.then_inc(free[k], 1)
                            if e == E - 1:
                                was_read(f"down{e}")
                                m.end()

                halves(v, body)

            @block.scalar
            def _(act):
                act.wait_ge(s_prep2, 10)
                act.wait_ge(we_loaded, 64)

                def body(phase, b, tag, hf, has_linear, has_experts):
                    for job in late_order(has_linear, has_experts):
                        if job == "h":
                            k = wait_full(act, phase, job + tag, b)
                            act.activation(hT[:], ps[:, k], ACT.Tanh, bias=bh[:]).then_inc(free[k], 1)
                        elif job[1:2] == "f":
                            a, dst, g = (0, Qf, int(job[2])) if job[0] == "q" else (1, Kf, int(job[2]))
                            k = wait_full(act, phase, job + tag, b)
                            act.activation(dst[:, g], ps[:, k], ACT.Exp, bias=fb[:, a:a + 1]).then_inc(free[k], 1)
                        elif job[:2] == "kt":
                            k = wait_full(act, phase, job + tag, b)
                            act.activation(Kt[:, int(job[2])].rearrange("p c f -> p (c f)"), ps[:, k], ACT.Copy).then_inc(free[k], 1)
                        elif job in ("outer1", "outer3"):
                            a = int(job[-1]) // 2
                            k = wait_full(act, phase, f"O{a}{tag}", b)
                            act.activation(oT1[:, 2 * a:2 * a + 2].rearrange("p c g t -> p (c g t)"), ps[:, k], ACT.Copy).then_inc(free[k], 1)
                        elif job in ("on0", "on1"):
                            a = int(job[-1])
                            k = wait_full(act, phase, job + tag, b)
                            for c in range(2):
                                ins = act.activation(sq1[:, 2 * a + c], ps[:, k, 2 * c * P:2 * (c + 1) * P].rearrange("p (h d) -> p h d", h=H1)[:, :, 0:DK], ACT.Square)
                            ins.then_inc(squared1, 1)
                        elif job == "gate":
                            k = wait_full(act, phase, job + tag, b)
                            act.activation(sg[:].rearrange("p t e -> p (t e)"), ps[:, k, 0:HT * E], ACT.Exp, scale=-1.0).then_inc(free[k], 1)
                        elif job[:2] == "up":
                            e, f = int(job[2]), int(job[3])
                            k = wait_full(act, phase, job + tag, b)
                            if e >= 2 and f == 0:
                                wait_full(act, phase, f"down{e - 2}{tag}", b)
                            act.activation(hid[:, e % 2, f], ps[:, k], ACT.Gelu_apprx_tanh, bias=b1[:, e, f:f + 1]).then_inc(free[k], 1)

                halves(act, body)

            @block.tensor
            def _(pe):
                pe.wait_ge(s_prep2, 6)
                pe.matmul(ps[:, 0, 0:2 * D], wq1[:], fmq[:], start=True, stop=True).then_inc(s_prep_pe, 1)
                pe.matmul(ps[:, 1, 0:2 * D], wk1[:], fmk[:], start=True, stop=True).then_inc(s_prep_pe, 1)
                pe.wait_ge(s_prep2, 10)
                pe.wait_ge(we_loaded, 64)

                def body(phase, b, tag, hf, has_linear, has_experts):
                    h = half_of(b, tag, hf, phase)

                    def bank(job):
                        return wait_free(pe, phase, job + tag, b, 1)

                    def was_read(job):
                        wait_free(pe, phase, job + tag, b)

                    def transposed(job, src):
                        k = bank(job)
                        for t in range(HT):
                            mm = pe.transpose(ps[:, k, t * P:(t + 1) * P], src(t), ident)
                        mm.then_inc(full[k], 1)

                    def by_tile(job, src, w, width=D):
                        k = bank(job)
                        for t in range(HT):
                            mm = pe.matmul(ps[:, k, t * width:(t + 1) * width], src[:, t * P:(t + 1) * P], w[:], start=True, stop=True)
                        mm.then_inc(full[k], 1)

                    def outer(c):
                        first = hf == 0 and c == 0
                        k = banks.at(phase, f"O{c // 2}{tag}", b)[0]
                        if c % 2 == 0:
                            bank(f"O{c // 2}")
                        if c:
                            was_read(f"S{c - 1}")
                        was_read(f"A{c}1")
                        for g in range(G1):
                            cols = slice(((c % 2) * G1 + g) * P, ((c % 2) * G1 + g + 1) * P)
                            if not first:
                                pe.matmul(ps[:, k, cols], state[:, c % 2, g], Qf[:, g, c * P:(c + 1) * P], start=True, stop=False, skip_group_check=True)
                            for j in range(HG):
                                mm = pe.matmul(ps[VW * j:VW * (j + 1), k, cols], V1[:, c, HG * g + j], Am[:, c % 2, g, j], start=first, stop=True,
                                               skip_group_check=True)
                        if c % 2:
                            mm.then_inc(full[k], 1)

                    for job in late_order(has_linear, has_experts):
                        if job == "h":
                            k = bank("h")
                            pe.matmul(ps[:, k], wh[:], xn1T[:, bass.ds(h * HN, HN)], start=True, stop=False)
                            pe.matmul(ps[:, k], uh[:], C2[:, hf * HN:(hf + 1) * HN], start=False, stop=True).then_inc(full[k], 1)
                        elif job == "hT":
                            was_read("h")
                            transposed("hT", lambda t: hT[:, t * P:(t + 1) * P])
                        elif job == "x2T":
                            pe.wait_ge(xn2_ready, h + 1)
                            transposed("x2T", lambda t: xn2[:, t])
                        elif job[1:2] == "f":
                            if job == "qf0":
                                was_read("x2T")
                            k = bank(job)
                            g = int(job[2])
                            pe.matmul(ps[:, k], (wqf if job[0] == "q" else wkf)[:, g * P:(g + 1) * P], xn2T[:], start=True, stop=True).then_inc(full[k], 1)
                        elif job == "v":
                            by_tile("v", xn2T, wv1)
                        elif job[:2] == "kt":
                            g = int(job[2])
                            was_read(f"kf{g}")
                            transposed(job, lambda t: Kf[:, g, t * P:(t + 1) * P])
                        elif job[0] == "A":
                            c, g = int(job[1]), int(job[2])
                            if c == 0 and g == 0:
                                pe.wait_ge(qbd_ready, h + 1)
                            k = bank(job)
                            pe.matmul(ps[:, k], Kf[:, g, c * P:(c + 1) * P], Qbd[:, g, :, c * P:(c + 1) * P], start=True, stop=True).then_inc(full[k], 1)
                        elif job[:5] == "outer":
                            if job == "outer0":
                                was_read("v")
                                was_read("kt0")
                                was_read("kt1")
                            outer(int(job[5]))
                        elif job[0] == "S":
                            c = int(job[1])
                            k = bank(job)
                            for g in range(G1):
                                mm = pe.matmul(ps[:, k, g * P:(g + 1) * P], Kt[:, g, c], V1[:, c, HG * g:HG * (g + 1)].rearrange("p j v -> p (j v)"),
                                               start=(hf == 0 and c == 0 and g == 0), stop=True, skip_group_check=True)
                            mm.then_inc(full[k], 1)
                        elif job in ("on0", "on1"):
                            a = int(job[2])
                            was_read(f"O{a}")
                            k = bank(job)
                            for c in range(2):
                                for g in range(G1):
                                    mm = pe.transpose(ps[:, k, (2 * c + g) * P:(2 * c + g + 1) * P], oT1[:, 2 * a + c, g], ident)
                            mm.then_inc(full[k], 1)
                        elif job == "onT":
                            was_read("on0")
                            was_read("on1")
                            transposed("onT", lambda t: on[:, t])
                        elif job == "wo1":
                            was_read("onT")
                            by_tile("wo1", onT, wo1)
                        elif job == "x3T":
                            pe.wait_ge(xn3_ready, h + 1)
                            transposed("x3T", lambda t: xn3[:, t])
                        elif job == "gate":
                            was_read("x3T")
                            by_tile("gate", x3s, wg, E)
                        elif job == "cT":
                            pe.wait_ge(l1_steps, h * L1_STEPS)
                            k = bank("cT")
                            for t in range(HT):
                                mm = pe.transpose(ps[0:E, k, t * P:(t + 1) * P], comb[:, 1 - hf, t], ident)
                            mm.then_inc(full[k], 1)
                        elif job == "b2":
                            was_read("cT")
                            by_tile("b2", combT, b2)
                        elif job[:2] == "up":
                            e, f = int(job[2]), int(job[3])
                            k = bank(job)
                            pe.matmul(ps[:, k], w1[:, e, f * P:(f + 1) * P], xn1T[:, bass.ds((h - 1) * HN, HN)], start=True, stop=True).then_inc(full[k], 1)
                        elif job[:4] == "down":
                            e, t = int(job[4]), int(job[5])
                            k = banks.at(phase, f"down{e}{tag}", b)[0]
                            if t == 0:
                                bank(f"down{e}")
                                was_read(f"up{e}{FT - 1}")
                            for f in range(FT):
                                mm = pe.matmul(ps[:, k, t * D:(t + 1) * D], hid[:, e % 2, f, t * P:(t + 1) * P], w2[:, e, f], start=(f == 0), stop=(f == FT - 1))
                            if t == HT - 1:
                                mm.then_inc(full[k], 1)

                halves(pe, body)


def _layout(np, a):
    def diagonal(w):
        o = np.zeros((H1, DK, H1, 2, DK), w.dtype)
        for h in range(H1):
            for sign in range(2):
                o[h, :, h, sign, :] = w.T
        return o.reshape(D, 2 * D)

    wq, bq = a["L0_attn_Wq"], a["L0_attn_bq"]
    consts = np.zeros((P, NCONST), np.float32)
    consts[:, 0:P] = np.eye(P)
    consts[:, P:2 * P] = np.triu(np.ones((P, P)))
    consts[:, 2 * P:3 * P] = np.kron(np.eye(HG), np.ones((VW, VW)))
    consts[:, 3 * P:5 * P] = np.tile(np.repeat([1.0, -1.0], DK), 2 * HG)
    consts[:, 5 * P:5 * P + E * E] = np.tril(np.ones((E, E)), -1).reshape(E * E)
    consts[:, 5 * P + E * E] = np.tile(np.repeat([1.0, -1.0], DK), HG)
    return dict(
        x=a["L0_attn_x"].reshape(NT * P, D),
        w_qkvg=np.concatenate([wq[:, :D], a["L0_attn_Wk"], a["L0_attn_Wv"], wq[:, D:]], 1),
        b_qkvg=np.concatenate([bq[:D], a["L0_attn_bk"], a["L0_attn_bv"], bq[D:]]),
        qn_w=np.tile(a["L0_attn_qn_w"], H0), kn_w=np.tile(a["L0_attn_kn_w"], H0),
        w_o0=a["L0_attn_Wo"], b_o0=a["L0_attn_bo"],
        w_gates=np.stack([a["L0_ffn_w" + c].T for c in "fic"], 1),
        u_gates=np.stack([a["L0_ffn_u" + c].T for c in "fic"], 1),
        b_gates=np.stack([a["L0_ffn_b" + c] for c in "fic"], 1),
        w_h=a["L0_ffn_wo"].T, u_h=a["L0_ffn_uo"].T, b_h=a["L0_ffn_bo"].reshape(D, 1), c_in=a["L0_ffn_in_c"].reshape(D, 1),
        w_q1=a["L1_attn_Wq"], w_k1=a["L1_attn_Wk"], w_v1=a["L1_attn_Wv"].T, w_o1=a["L1_attn_Wo"].T,
        fm_q=diagonal(a["L1_attn_fmq_w"]), fm_k=diagonal(a["L1_attn_fmk_w"]),
        fb_q=np.tile(a["L1_attn_fmq_b"], H1).reshape(D, 1), fb_k=np.tile(a["L1_attn_fmk_b"], H1).reshape(D, 1),
        rms_w=np.tile(a["L1_attn_rms_w"], H1).reshape(D, 1),
        w_g=a["L1_ffn_Wg"], w_1=a["L1_ffn_W1"].transpose(1, 0, 2), b_1=a["L1_ffn_b1"].reshape(E, FT, P).transpose(2, 0, 1),
        w_2=a["L1_ffn_W2"].reshape(E, FT, P, D).transpose(2, 0, 1, 3), b_2=a["L1_ffn_b2"],
        consts=consts,
    )


def kernel(**inputs):
    import numpy as _np
    import concourse.bacc as _bacc
    from concourse import mybir as _mybir
    from concourse.bass_utils import run_bass_kernel_spmd as _run

    nc = _bacc.Bacc("TRN2", target_bir_lowering=False, num_devices=1)
    laid = _layout(_np, {k: _np.asarray(v) for k, v in inputs.items()})
    arrays, args = {}, {}
    for name, a in laid.items():
        a = _np.ascontiguousarray(a)
        arrays[f"in_{name}"] = a
        args[name] = nc.dram_tensor(f"in_{name}", a.shape, _mybir.dt.from_np(a.dtype), kind="ExternalInput").ap()
    out = nc.dram_tensor("out_rows", (NT * P, D), _mybir.dt.float32, kind="ExternalOutput").ap()
    build(nc, out=out, **args)
    r = _run(nc, [arrays], core_ids=[0])
    return r.results[0]["out_rows"].reshape(B, N, D)
```

```python
import math
from contextlib import ExitStack

import concourse.bass as bass
from concourse import mybir

F32 = mybir.dt.float32
BF16 = mybir.dt.bfloat16
I32 = mybir.dt.int32
F22 = mybir.dt.float32r
HIGH_BITS = -4096
ALU = mybir.AluOpType
ACT = mybir.ActivationFunctionType
AX_X = mybir.AxisListType.X
AX_XY = mybir.AxisListType.XY

P = 128
D = 128
B, N = 4, 1024
TB = N // P
NT = B * TB
HT = TB // 2
HN = N // 2
LN_EPS = 1e-5

H0, HD = 16, 8
HG = 4
NG = H0 // HG
VW = 32
SPLITS = 3
COMBOS = SPLITS * SPLITS
KROWS = 96
W0 = 3 * D + H0
RMS0_EPS = 1e-6
SLOTS = 2 * 2 * TB
SHIFT_ROW = COMBOS * HD
SHIFT_ABOVE = 40.0
PROBS = 8
LOADS = 16 * 2 * SPLITS

H1, DK = 8, 16
DF = 2 * DK
G1 = 2
RMS1_EPS = 1e-5

E, F = 8, 512
FT = F // P
NCONST = 5 * P + E * E + 1
RSQRT_MAGIC = float(0x5F3759DF)

AT = {"attT": 0, "xT": 3, "wo": 3, "m": 4, "x1T": 7, "oT": (12, 18, 26), "q": 12, "k": 14, "f": 16, "i": 21, "g": 22}
SIDE_BANK = {"attT": 1, "xT": 1, "wo": 0, "m0": 1, "m1": 0, "m2": 1, "m3": 0, "x1T": 1, "oT0": 0, "q": 1, "k": 0, "f": 1, "oT1": 0, "i": 1,
             "g": 0, "oT2": 0, "oT3": 0}
GATES_AT, TANH_AT = 9, (18, 23, 25)
EARLY = (28, 29)
BESIDE = ("outputs_copy", "norm", "att_copy", "x_copy", "residual", "norm1", "biases", "x1_copy", "head_norms", "output0", "splits",
          "output1", "output2", "recur", "output3")


def side_jobs(has_front, has_att, has_post):
    jobs = []
    if has_post:
        jobs += [(AT[job], job) for job in ("attT", "wo", "x1T", "f", "i", "g")]
        jobs += [(AT[job] + 1, job + "_state") for job in "fig"]
    if has_front:
        jobs += [(AT[job], job) for job in ("xT", "q", "k")] + [(AT["m"] + u, f"m{u}") for u in range(HT)]
    if has_att:
        jobs += [(AT["oT"][unit], f"oT{unit}") for unit in range(3)] + [(SLOTS, "oT3")]
    return sorted(jobs, key=lambda job: job[0])


class Steps:

    def __init__(self, eng, sem, base, per):
        self.eng, self.sem, self.base, self.per, self.n = eng, sem, base, per, 0

    def go(self, ins):
        self.n += 1
        ins.then_inc(self.sem, 1)

    def wait(self):
        self.eng.wait_ge(self.sem, self.base + self.n)

    def did(self, ins):
        self.go(ins)
        self.wait()

    def end(self):
        assert self.n == self.per, self.n


LATE = (("h", 1), ("hT", 13), ("x2T", 2), ("qf0", 0), ("qf1", 0), ("kf0", 0), ("kf1", 1), ("v", 0), ("kt0", 0), ("kt1", 6), ("A00", 2),
        ("A01", 2), ("A10", 3), ("A11", 0), ("O0", 1), ("outer0", 1), ("S0", 1), ("A20", 3), ("A21", 0), ("outer1", 0), ("S1", 0), ("A30",
        1), ("A31", 2), ("O1", 0), ("outer2", 1), ("S2", 1), ("on0", 0), ("outer3", 1), ("S3", 0), ("on1", 4), ("onT", 2), ("wo1", 10),
        ("x3T", 4), ("gate", 0))
LATE_PHASES = (("start", 0, 1, (("", 0, True, False),)),
               ("middle", 0, B - 1, (("'", 1, True, True), ("", 0, True, True))),
               ("last", B - 1, 1, (("'", 1, True, True),)),
               ("end", B, 1, (("", 0, False, True),)))


def late_order(has_linear, has_experts):
    experts = []
    if has_experts:
        def up(e):
            return [f"up{e}{f}" for f in range(FT)]

        experts = ["cT", "b2"] + up(0)
        for e in range(E):
            experts += (up(e + 1) if e + 1 < E else []) + [f"down{e}{t}" for t in range(HT)]
    order = []
    for job, fill in LATE if has_linear else ():
        order += [job] + experts[:fill]
        experts = experts[fill:]
    return order + experts


class Banks:

    def __init__(self, n):
        self.used, self.phases = [0] * n, {}

    def phase(self, name, first, count, jobs):
        base, place = list(self.used), {}
        for job, bank in jobs:
            self.used[bank] += 1
            place[job] = (bank, self.used[bank])
        per = [u - b for u, b in zip(self.used, base)]
        self.phases[name] = (first, per, place)
        self.used = [b + count * p for b, p in zip(base, per)]

    def at(self, name, job, i):
        first, per, place = self.phases[name]
        bank, n = place[job]
        return bank, (i - first) * per[bank] + n


RSQRT_STEPS = 11
LN_STEPS = 4 + 3 + 3 + 1 + RSQRT_STEPS


def rsqrt(v, s, out, x, t, half):
    s.did(v.tensor_scalar(half.bitcast(I32), x.bitcast(I32), 1, None, ALU.logical_shift_right))
    s.did(v.tensor_scalar(out.bitcast(I32), half.bitcast(I32), -1.0, RSQRT_MAGIC, ALU.mult, ALU.add))
    for _ in range(3):
        s.did(v.tensor_tensor(t, out, out, ALU.mult))
        s.did(v.scalar_tensor_tensor(t, t, -0.5, x, ALU.mult, ALU.mult))
        s.did(v.scalar_tensor_tensor(out, t, 1.5, out, ALU.add, ALU.mult))


def layernorm(v, s, out, x, st, w, ready):
    v.memset(w[:, 6], 0.0)
    for u in range(HT):
        s.go(v.bn_stats(st[:, u], x[:, u]))
    s.wait()
    s.go(v.tensor_tensor(w[:, 0], st[:, :, 1], st[:, :, 4], ALU.add))
    s.go(v.tensor_tensor(w[:, 1], st[:, :, 1], st[:, :, 4], ALU.subtract))
    s.go(v.tensor_tensor(w[:, 2], st[:, :, 2], st[:, :, 5], ALU.add))
    s.wait()
    s.go(v.tensor_scalar(w[:, 6], w[:, 0], 0.5, None, ALU.mult))
    s.go(v.scalar_tensor_tensor(w[:, 3], w[:, 1], 0.25, w[:, 1], ALU.mult, ALU.mult))
    s.go(v.tensor_scalar(w[:, 4], w[:, 2], 1.0 / D, LN_EPS, ALU.mult, ALU.add))
    s.wait()
    s.did(v.tensor_tensor(w[:, 0], w[:, 3], w[:, 4], ALU.add))
    rsqrt(v, s, w[:, 5], w[:, 0], w[:, 1], w[:, 2])
    for u in range(HT):
        ins = v.tensor_scalar(out[:, u], x[:, u], w[:, 6, u:u + 1], w[:, 5, u:u + 1], ALU.subtract, ALU.mult)
    ins.then_inc(ready, 1)


def build(nc, x, w_qkvg, b_qkvg, qn_w, kn_w, w_o0, b_o0, w_gates, u_gates, b_gates, w_h, u_h, b_h, c_in,
          w_q1, w_k1, w_v1, w_o1, fm_q, fm_k, fb_q, fb_k, rms_w, w_g, w_1, b_1, w_2, b_2, consts, out):
    with ExitStack() as ctx:
        def sb(name, shape, dt=F32):
            return ctx.enter_context(nc.sbuf_tensor(name, shape, dt))

        def sem(name):
            return ctx.enter_context(nc.semaphore(name))

        qk_dram = nc.dram_tensor("qk_splits", (B, SPLITS, 2, P, N), BF16, kind="Internal").ap()
        shift_dram = nc.dram_tensor("shift_splits", (SPLITS, HG * TB, P), BF16, kind="Internal").ap()
        X = sb("X", [P, NT, D])
        xn1T = sb("xn1T", [D, NT * P])
        C2 = sb("C2", [D, N])
        const_sb = sb("const_sb", [P, NCONST])
        ident = const_sb[:, 0:P]
        causal = const_sb[:, P:2 * P]
        blocks = const_sb[:, 2 * P:3 * P]
        signs = const_sb[:, 3 * P:5 * P]
        before = const_sb[:, 5 * P:5 * P + E * E].rearrange("p (e f) -> p e f", e=E)
        sign_col = const_sb[:, 5 * P + E * E:NCONST]
        work = sb("work", [P, 7, HT])
        st = sb("st", [P, HT, 6])

        wh = sb("wh", [D, D])
        uh = sb("uh", [D, D])
        bh = sb("bh", [D, 1])
        wq1 = sb("wq1", [D, D])
        wk1 = sb("wk1", [D, D])
        wv1 = sb("wv1", [D, D])
        wo1 = sb("wo1", [D, D])
        fmq = sb("fmq", [D, 2 * D])
        fmk = sb("fmk", [D, 2 * D])
        fb = sb("fb", [D, 2])
        rmsw = sb("rmsw", [D, 1])
        wqf = sb("wqf", [D, 2 * D])
        wkf = sb("wkf", [D, 2 * D])
        wg = sb("wg", [D, E])

        ps = ctx.enter_context(nc.psum_tensor("ps", [P, 8, 512], F32))
        S = ps[:, 0:4, :].rearrange("p (s j) q -> p s j q", s=2)
        O = ps[:, 4:6, :]
        SIDE = 6

        banks = Banks(8)
        full = [sem(f"bank{i}_full") for i in range(8)]
        free = [sem(f"bank{i}_free") for i in range(8)]

        PHASES = [("lead", -1, 0, 1, 0, 0), ("grow", 0, 1, 1, 1, 0), ("steady", 1, B - 1, 1, 1, 1),
                  ("shrink", B - 1, B, 0, 1, 1), ("tail", B, B + 1, 0, 0, 1)]
        banks.phase("lead", 0, 1, [("xT0", 6), ("xT1", 7)] + [(f"m{u}{hp}", u) for hp in range(2) for u in range(HT)] +
                    [("q0", 4), ("k0", 5), ("q1", 6), ("k1", 7)])
        for name, b0, b1, has_front, has_att, has_post in PHASES[1:-1]:
            jobs = [job for _, job in side_jobs(has_front, has_att, has_post) if job[1:] != "_state"]
            banks.phase(name, 2 * b0, 2 * (b1 - b0), [(job, SIDE + SIDE_BANK[job]) for job in jobs])
        banks.phase("tail", 0, 1, [(f"{job}{hp}", (4, 7)[hp]) for hp in range(2) for job in ("attT", "wo", "x1T")] +
                    [(f"{job}{hp}", 3 * hp + g) for hp in range(2) for g, job in enumerate("fig")])

        def place(name, job, it, hp):
            return banks.at(name, f"{job}{hp}", 0) if name in ("lead", "tail") else banks.at(name, job, it)

        late_banks = {"h": 0, "hT": 1, "x2T": 0, "qf0": 1, "qf1": 0, "kf0": 1, "kf1": 0, "v": 1, "kt0": 0, "kt1": 1, "A": 5, "O": 3, "S": 4,
                      "on0": 0, "on1": 1, "onT": 0, "wo1": 1, "x3T": 0, "gate": 1, "cT": 7, "b2": 7, "down": 7}

        def late_jobs(has_linear, has_experts, tag):
            for job in late_order(has_linear, has_experts):
                if job[:2] == "up":
                    yield job + tag, (2, 6)[int(job[3]) % 2]
                elif job[:4] == "down":
                    if job[5] == "0":
                        yield job[:5] + tag, late_banks["down"]
                elif job[0] == "A" and not has_experts:
                    yield job + tag, (5, 7)[int(job[2])]
                elif job[:5] != "outer":
                    yield job + tag, late_banks[job[0] if job[0] in "AOS" else job]

        for name, first, count, halves in LATE_PHASES:
            banks.phase(name, first, count, [pair for tag, hf, has_linear, has_experts in halves for pair in late_jobs(has_linear, has_experts, tag)])

        s_const = sem("s_const"); x_first = sem("x_first"); x_rest = sem("x_rest"); s_prep = sem("s_prep"); s_prep_pe = sem("s_prep_pe")
        s_zero = sem("s_zero"); s_pool = sem("s_pool")
        front_steps = sem("front_steps"); post_steps = sem("post_steps"); att_steps = sem("att_steps")
        xn_ready = sem("xn_ready"); qkn_ready = sem("qkn_ready"); x1n_ready = sem("x1n_ready")
        split_ready = sem("split_ready"); split_stored = sem("split_stored"); gate_exp = sem("gate_exp")
        loaded = [sem("loaded0"), sem("loaded1")]
        v_staged = [sem("v_staged0"), sem("v_staged1")]
        scores_ready = sem("scores_ready"); probs_ready = sem("probs_ready"); probs_used = sem("probs_used")
        o_copied = sem("o_copied"); c_ready = sem("c_ready")
        w_loaded = sem("w_loaded"); l1_steps = sem("l1_steps"); act1 = sem("act1")
        xn2_ready = sem("xn2_ready"); qbd_ready = sem("qbd_ready"); state_ready = sem("state_ready")
        on_ready = sem("on_ready"); xn3_ready = sem("xn3_ready"); state_sum = sem("state_sum")
        squared1 = sem("squared1"); x3_static = sem("x3_static")
        hid_ready = sem("hid_ready"); hid_used = sem("hid_used"); moe_steps = sem("moe_steps")
        combT_ready = sem("combT_ready"); stored = sem("stored")
        combT_ps = sem("combT_ps")

        FRONT_STEPS = LN_STEPS + 3 + RSQRT_STEPS + 1 + 3 + 2
        LEAD_STEPS = 2 * (FRONT_STEPS - 3)
        POST_STEPS = 1 + LN_STEPS + 1 + 2
        L1_STEPS = 2 * LN_STEPS + 2 + RSQRT_STEPS + 1 + 2 + 2 * HT + 4 + 2
        MOE_STEPS = 3 * E
        CONST_LOADS = 11
        LATE_LOADS = 13
        ones_loaded = sem("ones_loaded"); shift_ready = sem("shift_ready"); shift_loaded = sem("shift_loaded"); shift_stored = sem("shift_stored")
        max_scores = sem("max_scores"); max_taken = sem("max_taken"); max_turned = sem("max_turned"); shift_steps = sem("shift_steps")
        s_prep2 = sem("s_prep2"); we_loaded = sem("we_loaded"); w1_split = sem("w1_split"); w1_high = sem("w1_high"); late_zeros = sem("late_zeros")
        lead_squares = sem("lead_squares"); lead_splits = sem("lead_splits")

        with ExitStack() as part:
            def pb(name, shape, dt=F32):
                return part.enter_context(nc.sbuf_tensor(name, shape, dt))

            wqkvg = pb("wqkvg", [D, W0])
            bqkvg = pb("bqkvg", [P, W0])
            qnw = pb("qnw", [P, D])
            kscale = pb("kscale", [P, D])
            wo0 = pb("wo0", [D, D])
            bo0 = pb("bo0", [P, D])
            wg3 = pb("wg3", [D, 3, D])
            ug3 = pb("ug3", [D, 3, D])
            bg3 = pb("bg3", [D, 3])
            c0 = pb("c0", [D, 1])
            stF = pb("stF", [P, HT, 6])
            wF = pb("wF", [P, 7, HT])
            rr = pb("rr", [P, 4, 2 * H0 * HT])
            xn = pb("xn", [P, HT, D])
            xnT = pb("xnT", [D, HN])
            qk = pb("qk", [P, HT, 2 * D])
            sq = pb("sq", [P, HT, 2 * D])
            rest = pb("rest", [P, 2, HN])
            split = pb("split", [P, SPLITS, 2, HN], BF16)[:]
            VG = pb("VG", [P, NT, D + H0])
            G = pb("G", [P, NT, H0])
            gexp = pb("gexp", [P, 2, HT, H0])
            Q_st = pb("Q_st", [KROWS, 2, HG, N], BF16)
            K_st = pb("K_st", [KROWS, 2, HG, N], BF16)
            V_st = pb("V_st", [P, 2, TB, HG, VW])
            prob = pb("prob", [P, PROBS, 2, HN])
            OT = pb("OT", [P, 2, HN])
            rden = pb("rden", [P, 2, HG * HT])
            att = pb("att", [P, NT, D])
            att_static = pb("att_static", [P, HT, D])
            attT = pb("attT", [D, HN])
            x1n = pb("x1n", [P, HT, D])
            tg = pb("tg", [D, 3, HN])
            bound = pb("bound", [P, 1])
            shift_flag = pb("shift_flag", [1, 1], I32)
            row_max = pb("row_max", [P, HG * TB])
            shift = pb("shift", [HG * TB, P])
            shift_split = pb("shift_split", [HG * TB, SPLITS, P], BF16)
            block = part.enter_context(nc.Block())

            FRONT = dict(xn=xn[:], xnT=xnT[:], qk=qk[:], sq=sq[:], rest=rest[:], split=split, rr=rr[:], st=stF[:], w=wF[:], gexp=gexp[:, 0])
            POST = dict(att=att_static[:], attT=attT[:], x1n=x1n[:], st=st[:], w=work[:], tg=tg[:])
            wide = prob[:].rearrange("p n j q -> p (n j q)")

            def cut(at, shape, dt=F32):
                size = math.prod(shape) // (2 if dt == BF16 else 1)
                part = wide[:, at * HN:at * HN + size]
                if len(shape) == 1:
                    return part
                names = " ".join("abc"[:len(shape)])
                part = part.bitcast(dt) if dt != F32 else part
                return part.rearrange(f"p ({names}) -> p {names}", **{n: k for n, k in zip("abc", shape)})

            FRONT2 = dict(xn=cut(0, (HT, D)), xnT=cut(1, (HN,)), qk=cut(2, (HT, 2 * D)), sq=cut(4, (HT, 2 * D)), rest=cut(6, (2, HN)),
                          split=cut(8, (SPLITS, 2, HN), BF16), rr=cut(11, (4, 2 * H0 * HT)), st=st[:], w=work[:], gexp=gexp[:, 1])
            POST2 = dict(att=cut(0, (HT, D)), attT=cut(1, (HN,)), x1n=cut(2, (HT, D)), st=stF[:], w=wF[:], tg=cut(3, (3, HN)))

            def buffers(name, hp):
                return (FRONT2, POST2) if name in ("lead", "tail") and hp == 1 else (FRONT, POST)

            def phases(eng, body):
                for name, b0, b1, has_front, has_att, has_post in PHASES:
                    if name in ("lead", "tail"):
                        body(name, b0, None, has_front, has_att, has_post)
                    elif name == "shrink":
                        for hp in range(2):
                            body(name, b0, hp, has_front, has_att, has_post)
                    elif b1 - b0 == 1:
                        with eng.Fori(0, 2) as hp:
                            body(name, b0, hp, has_front, has_att, has_post)
                    else:
                        with eng.Fori(b0, b1) as b:
                            with eng.Fori(0, 2) as hp:
                                body(name, b, hp, has_front, has_att, has_post)

            @block.sync
            def _(sp):
                sp.dma_start(X[:, 0:TB], x[0:N].rearrange("(t p) d -> p t d", p=P)).then_inc(x_first, 16)
                loads = ((wqkvg, w_qkvg), (bqkvg, b_qkvg.partition_broadcast(P)), (qnw, qn_w.partition_broadcast(P)),
                         (kscale, kn_w.partition_broadcast(P)), (const_sb, consts), (wo0, w_o0), (bo0, b_o0.partition_broadcast(P)),
                         (wg3, w_gates), (ug3, u_gates), (bg3, b_gates), (c0, c_in))
                assert len(loads) == CONST_LOADS
                for dst, src in loads:
                    sp.dma_start(dst[:], src).then_inc(s_const, 16)
                sp.dma_start(X[:, TB:], x[N:].rearrange("(t p) d -> p t d", p=P)).then_inc(x_rest, 16)
                late_loads = ((wh, w_h), (uh, u_h), (bh, b_h), (wq1, w_q1), (wk1, w_k1), (wv1, w_v1), (wo1, w_o1), (fmq, fm_q), (fmk, fm_k),
                              (rmsw, rms_w), (wg, w_g))
                assert len(late_loads) + 2 == LATE_LOADS
                for dst, src in late_loads:
                    sp.dma_start(dst[:], src).then_inc(w_loaded, 16)
                sp.dma_start(fb[:, 0:1], fb_q).then_inc(w_loaded, 16)
                sp.dma_start(fb[:, 1:2], fb_k).then_inc(w_loaded, 16)

                def store_splits(b, hp, split=split):
                    sp.wait_ge(split_ready, 2 * b + hp + 1)
                    sp.dma_start(qk_dram[b, :, :, :, hp * HN:(hp + 1) * HN].rearrange("s a p t -> p (s a) t"),
                                 split.rearrange("p s a t -> p (s a) t")).then_inc(split_stored, 16)

                def load_group(b, hp, i, before_it=True):
                    if i == 0 and hp == 0:
                        sp.wait_ge(split_stored, 32 * (b + 1))
                    if before_it:
                        sp.wait_ge(scores_ready, 2 * SLOTS * (2 * b + hp - 1) + SLOTS * (i + 1))
                    heads = (2 * hp + i) * HG * HD
                    for c in range(SPLITS):
                        rows = slice(HD * SPLITS * c, HD * SPLITS * (c + 1))
                        q_rows = qk_dram[b, c, 0, heads:heads + HG * HD, :].rearrange("(d j) t -> d (j t)", d=HD)
                        k_rows = qk_dram[b, :, 1, heads:heads + HG * HD, :].rearrange("s (d j) t -> s d (j t)", d=HD)
                        sp.dma_start(Q_st[rows, i].rearrange("p j t -> p (j t)"), q_rows.unsqueeze(0).to_broadcast([SPLITS, HD, HG * N])).then_inc(loaded[i], 16)
                        sp.dma_start(K_st[rows, i].rearrange("p j t -> p (j t)"), k_rows).then_inc(loaded[i], 16)

                sp.wait_ge(s_zero, 3)
                sp.dma_start(K_st[SHIFT_ROW:SHIFT_ROW + SPLITS], Q_st[0:SPLITS]).then_inc(ones_loaded, 16)
                sp.wait_ge(ones_loaded, 16)
                store_splits(0, 0)
                store_splits(0, 1, FRONT2["split"])
                load_group(0, 0, 0, False)
                load_group(0, 0, 1, False)
                sp.wait_ge(s_prep, 5)
                shifted = sp.value_load(shift_flag[0:1, 0:1], min_val=0, max_val=1)

                def load_shift(it, i):
                    with sp.If(shifted != 0):
                        sp.wait_ge(shift_ready, 2 * it + i + 1)
                        sp.dma_start(shift_dram.rearrange("s r q -> r s q"), shift_split[:]).then_inc(shift_stored, 16)
                        sp.wait_ge(shift_stored, 16 * (2 * it + i + 1))
                        sp.dma_start(Q_st[SHIFT_ROW:SHIFT_ROW + SPLITS, i].rearrange("p j t -> p (j t)"),
                                     shift_dram.rearrange("s r q -> s (r q)")).then_inc(shift_loaded, 16)

                with sp.Fori(0, B - 1) as b:
                    for hp in range(2):
                        load_shift(2 * b + hp, 0)
                        store_splits(b + 1, hp)
                        load_shift(2 * b + hp, 1)
                        load_group(b + hp, 1 - hp, 0)
                        load_group(b + hp, 1 - hp, 1)
                load_shift(2 * B - 2, 0)
                load_shift(2 * B - 2, 1)
                load_group(B - 1, 1, 0)
                load_group(B - 1, 1, 1)
                load_shift(2 * B - 1, 0)
                load_shift(2 * B - 1, 1)

            @block.gpsimd
            def _(pool):
                pool.memset(Q_st[0:SPLITS], 1.0).then_inc(s_zero, 1)
                pool.memset(K_st[64:KROWS], 0.0).then_inc(s_zero, 1)
                pool.memset(Q_st[64:KROWS], 0.0).then_inc(s_zero, 1)
                pool.wait_ge(s_zero, 3)
                pool.memset(V_st[:], 0.0).then_inc(s_pool, 1)
                pool.wait_ge(s_pool, 1)
                pool.memset(V_st[:, :, :, :, HD:HD + 1], 1.0).then_inc(s_pool, 1)
                pool.wait_ge(s_pool, 2)

                def stage(b, hp, i, phase):
                    if i == 0 and hp == 0:
                        k, n = place(phase, "m3", 2 * b - 1, 1)
                        pool.wait_ge(free[k], n)
                    if phase != "lead":
                        pool.wait_ge(probs_used, SLOTS * (2 * b + hp - 1) + SLOTS // 2 * (i + 1))
                    heads = (2 * hp + i) * HG * HD
                    pool.tensor_copy(V_st[:, i, :, :, 0:HD],
                                     VG[:, bass.ds(b * TB, TB), heads:heads + HG * HD].rearrange("p k (j d) -> p k j d", d=HD)
                                     ).then_inc(v_staged[i], 1)

                stage(0, 0, 0, "lead")
                stage(0, 0, 1, "lead")
                for hp in range(2):
                    for i in range(2):
                        stage(hp, 1 - hp, i, "grow")
                with pool.Fori(1, B - 1) as b:
                    for hp in range(2):
                        for i in range(2):
                            stage(b + hp, 1 - hp, i, "steady")
                for i in range(2):
                    stage(B - 1, 1, i, "shrink")

            @block.vector
            def _(v):
                v.memset(row_max[:], 0.0).then_inc(max_taken, 1)
                shifted = None

                def prepare():
                    nonlocal shifted
                    v.wait_ge(s_const, 16 * CONST_LOADS)
                    v.scalar_tensor_tensor(kscale[:], qnw[:], float(HD) ** -0.5, kscale[:], ALU.mult, ALU.mult).then_inc(s_prep, 1)
                    v.tensor_scalar(ug3[:], ug3[:], 0.5, None, ALU.mult).then_inc(s_prep, 1)
                    v.tensor_scalar(bg3[:, 0:2], bg3[:, 0:2], 0.5, None, ALU.mult).then_inc(s_prep, 1)
                    v.tensor_scalar(C2[:], c0[:].to_broadcast([D, N]), 2.0, None, ALU.mult).then_inc(c_ready, 1)
                    v.wait_ge(s_prep, 3)
                    v.tensor_reduce(bound[:], kscale[:], AX_X, ALU.max, apply_absolute_value=True).then_inc(s_prep, 1)
                    v.wait_ge(s_prep, 4)
                    v.tensor_scalar(shift_flag[:], bound[0:1], float(HD), SHIFT_ABOVE, ALU.mult, ALU.is_gt).then_inc(s_prep, 1)
                    v.wait_ge(s_prep, 5)
                    shifted = v.value_load(shift_flag[0:1, 0:1], min_val=0, max_val=1)

                def prepare_late():
                    v.wait_ge(w_loaded, 16 * LATE_LOADS)
                    v.tensor_scalar(uh[:], uh[:], 0.5, None, ALU.mult).then_inc(s_prep2, 1)
                    v.tensor_scalar(wo1[:], wo1[:], rmsw[:], None, ALU.mult).then_inc(s_prep2, 1)
                    v.tensor_tensor(fmq[:], fmq[:], signs, ALU.mult).then_inc(s_prep2, 1)
                    v.tensor_tensor(fmk[:], fmk[:], signs, ALU.mult).then_inc(s_prep2, 1)
                    v.tensor_tensor(fb[:], fb[:], sign_col.to_broadcast([D, 2]), ALU.mult).then_inc(s_prep2, 1)
                    v.wait_ge(s_prep2, 5)
                    v.tensor_scalar(fb[:, 0:1], fb[:, 0:1], -0.5 * math.log(DF), None, ALU.add).then_inc(s_prep2, 1)
                    v.wait_ge(s_prep_pe, 2)
                    v.tensor_copy(wqf[:], ps[:, 0, 0:2 * D]).then_inc(s_prep2, 1)
                    v.tensor_copy(wkf[:], ps[:, 1, 0:2 * D]).then_inc(s_prep2, 1)

                class Half:

                    def __init__(self, name, b, hp, f, q):
                        self.name, self.hp, self.it, self.f, self.q = name, hp, 2 * b + hp, f, q
                        self.TF = (b + 1) * TB + hp * HT
                        self.TP = (b - 1) * TB + hp * HT
                        self.front, self.post = buffers(name, hp)

                    def product(self, job):
                        k, n = place(self.name, job, self.it, self.hp)
                        v.wait_ge(full[k], n)
                        return k

                    def was_read(self, job):
                        k, n = place(self.name, job, self.it, self.hp)
                        v.wait_ge(free[k], n)

                    def norm(self):
                        F = self.front
                        layernorm(v, self.f, F["xn"], X[:, bass.ds(self.TF, HT)], F["st"], F["w"], xn_ready)

                    def x_copy(self):
                        k = self.product("xT")
                        v.tensor_copy(self.front["xnT"], ps[:, k]).then_inc(free[k], 1)

                    def biases(self):
                        for u in range(HT):
                            k = self.product(f"m{u}")
                            v.tensor_tensor(self.front["qk"][:, u], ps[:, k, 0:2 * D], bqkvg[:, 0:2 * D], ALU.add)
                            v.tensor_tensor(VG[:, self.TF + u], ps[:, k, 2 * D:W0], bqkvg[:, 2 * D:W0], ALU.add).then_inc(free[k], 1)

                    def head_norms(self):
                        f, qk, sq, rr = self.f, self.front["qk"], self.front["sq"], self.front["rr"]
                        if self.name == "lead":
                            v.wait_ge(lead_squares, self.hp + 1)
                        else:
                            self.was_read("m3")
                            f.did(v.tensor_tensor(sq, qk, qk, ALU.mult))
                        f.did(v.tensor_reduce(rr[:, 1].rearrange("p (u j) -> p u j", j=HG), sq.rearrange("p t (g d j) -> p (t g) j d", d=HD, j=HG), AX_X, ALU.add))
                        f.did(v.tensor_scalar(rr[:, 0], rr[:, 1], 1.0 / HD, RMS0_EPS, ALU.mult, ALU.add))
                        rsqrt(v, f, rr[:, 3], rr[:, 0], rr[:, 1], rr[:, 2])
                        heads = qk.rearrange("p t (g d j) -> p (t g) d j", d=HD, j=HG)
                        f.did(v.tensor_tensor(heads, heads, rr[:, 3].rearrange("p (u j) -> p u j", j=HG).unsqueeze(2).to_broadcast([P, HT * 2 * NG, HD, HG]), ALU.mult))
                        v.tensor_tensor(qk[:, :, D:], qk[:, :, D:], kscale[:].unsqueeze(1).to_broadcast([P, HT, D]), ALU.mult).then_inc(qkn_ready, 1)

                    def splits(self):
                        f, split, rest = self.f, self.front["split"], self.front["rest"]
                        if self.name != "lead":
                            v.wait_ge(split_stored, 16 * (self.it + 2))
                        for a, job in ((0, "q"), (1, "k")):
                            k = self.product(job)
                            if self.name == "lead":
                                v.wait_ge(lead_splits, 2 * self.hp + a + 1)
                            else:
                                f.did(v.tensor_copy(split[:, 0, a], ps[:, k]))
                            v.tensor_tensor(rest[:, a], ps[:, k], split[:, 0, a], ALU.subtract).then_inc(free[k], 1)
                        self.was_read("q")
                        self.was_read("k")
                        f.did(v.tensor_copy(split[:, 1], rest))
                        v.tensor_tensor(split[:, 2], rest, split[:, 1], ALU.subtract).then_inc(split_ready, 1)

                    def gates(self):
                        f, gexp = self.f, self.front["gexp"]
                        v.wait_ge(gate_exp, self.it + 3)
                        f.did(v.tensor_scalar(gexp, gexp, 1.0, None, ALU.add))
                        f.go(v.reciprocal(G[:, bass.ds(self.TF, HT)], gexp))

                    def outputs_copy(self):
                        self.q.go(v.tensor_copy(self.post["att"], att[:, bass.ds(self.TP, HT)]))

                    def att_copy(self):
                        k = self.product("attT")
                        v.tensor_copy(self.post["attT"], ps[:, k]).then_inc(free[k], 1)

                    def residual(self):
                        XP = X[:, bass.ds(self.TP, HT)]
                        k = self.product("wo")
                        v.tensor_tensor(XP, ps[:, k].rearrange("p (t d) -> p t d", t=HT), XP, ALU.add).then_inc(free[k], 1)
                        self.was_read("wo")
                        self.q.did(v.tensor_tensor(XP, XP, bo0[:].unsqueeze(1).to_broadcast([P, HT, D]), ALU.add))

                    def norm1(self):
                        A = self.post
                        layernorm(v, self.q, A["x1n"], X[:, bass.ds(self.TP, HT)], A["st"], A["w"], x1n_ready)

                    def x1_copy(self):
                        k = self.product("x1T")
                        v.tensor_copy(xn1T[:, bass.ds(self.TP * P, HN)], ps[:, k]).then_inc(free[k], 1)

                    def recur(self):
                        tg = self.post["tg"]
                        for job in "fig":
                            self.was_read(job)
                        CP = C2[:, bass.ds(self.hp * HN, HN)]
                        self.q.go(v.scalar_tensor_tensor(tg[:, 0], tg[:, 0], 1.0, CP, ALU.add, ALU.mult))
                        self.q.did(v.scalar_tensor_tensor(tg[:, 1], tg[:, 1], 1.0, tg[:, 2], ALU.add, ALU.mult))
                        v.scalar_tensor_tensor(CP, tg[:, 0], 0.5, tg[:, 1], ALU.mult, ALU.add).then_inc(c_ready, 1)

                q = Steps(v, post_steps, (2 * B - 2) * POST_STEPS, 2 * POST_STEPS)
                last = [Half("tail", B, n, None, q) for n in range(2)]

                def body(name, b, hp, has_front, has_att, has_post):
                    if name == "lead":
                        f = Steps(v, front_steps, 0, LEAD_STEPS)
                        one, two = (Half(name, b, n, f, None) for n in range(2))
                        v.wait_ge(x_first, 16)
                        one.norm()
                        two.norm()
                        prepare()
                        one.biases()
                        one.head_norms()
                        two.biases()
                        two.head_norms()
                        one.splits()
                        two.splits()
                        one.gates()
                        two.gates()
                        f.end()
                        prepare_late()
                        v.wait_ge(x_rest, 16)
                        return
                    if name == "tail":
                        one, two = last
                        v.wait_ge(probs_used, 2 * B * SLOTS)
                        two.outputs_copy()
                        one.x1_copy()
                        two.att_copy()
                        two.residual()
                        two.norm1()
                        two.x1_copy()
                        one.recur()
                        two.recur()
                        one.q.end()
                        return
                    it = 2 * b + hp
                    f = Steps(v, front_steps, LEAD_STEPS + it * FRONT_STEPS, FRONT_STEPS)
                    q = Steps(v, post_steps, (it - 2) * POST_STEPS, POST_STEPS)
                    half = Half(name, b, hp, f, q)

                    def output(unit):
                        qh, g = unit % 2, 2 * hp + unit // 2
                        T4 = bass.ds(b * TB + HT * qh, HT)
                        v.wait_ge(probs_used, it * SLOTS + (unit + 1) * TB)
                        v.tensor_copy(OT[:, qh], O[:, qh]).then_inc(o_copied, 1)
                        k = half.product(f"oT{unit}")
                        oT = ps[:, k].rearrange("p (t j c) -> p t j c", t=HT, j=HG)
                        r = rden[:].rearrange("p a (t j) -> p a t j", t=HT)
                        a = Steps(v, att_steps, (4 * it + unit) * 2, 2)
                        a.did(v.reciprocal(r[:, 0], oT[:, :, :, HD]))
                        a.did(v.tensor_tensor(r[:, 1], r[:, 0], G[:, T4, bass.ds(g * HG, HG)], ALU.mult))
                        a.end()
                        v.tensor_tensor(att[:, T4, bass.ds(g * HG * HD, HG * HD)].rearrange("p t (j d) -> p t j d", d=HD),
                                        oT[:, :, :, 0:HD], r[:, 1].unsqueeze(3).to_broadcast([P, HT, HG, HD]), ALU.mult).then_inc(free[k], 1)

                    def largest_scores(i):
                        with v.If(shifted != 0):
                            with v.Fori(0, HG) as j:
                                with v.Fori(0, TB // 2) as t:
                                    for u in range(2):
                                        n = j * TB + 2 * t + u
                                        v.wait_ge(max_scores, (2 * it + i) * HG * TB + n + 1)
                                        v.tensor_reduce(row_max[:, bass.ds(n, 1)], S[:, u], AX_XY, ALU.max).then_inc(max_taken, 1)
                            v.wait_ge(max_turned, 2 * it + i + 1)
                            e = Steps(v, shift_steps, (2 * it + i) * 5, 5)
                            e.did(v.tensor_scalar(shift[:], ps[0:HG * TB, 0, 0:P], -1.0, None, ALU.mult))
                            for s in range(2):
                                e.did(v.tensor_copy(shift_split[:, s], shift[:]))
                                e.did(v.tensor_tensor(shift[:], shift[:], shift_split[:, s], ALU.subtract))
                            e.end()
                            v.tensor_copy(shift_split[:, 2], shift[:]).then_inc(shift_ready, 1)

                    front = {"norm": half.norm, "x_copy": half.x_copy, "biases": half.biases, "head_norms": half.head_norms, "splits": half.splits}
                    post = {"outputs_copy": half.outputs_copy, "att_copy": half.att_copy, "residual": half.residual, "norm1": half.norm1,
                            "x1_copy": half.x1_copy, "recur": half.recur}
                    if has_att:
                        largest_scores(0)
                    for stage in BESIDE:
                        if stage == "output3" and name == "shrink" and hp == 1:
                            half.was_read("oT2")
                            last[0].outputs_copy()
                            last[0].att_copy()
                            last[0].residual()
                            last[0].norm1()
                        if has_front and stage in front:
                            front[stage]()
                            if stage == "splits":
                                half.gates()
                        elif has_post and stage in post:
                            post[stage]()
                        elif has_att and stage[:6] == "output" and stage[6:].isdigit():
                            if stage == "output1":
                                largest_scores(1)
                            output(int(stage[6]))
                    if has_front:
                        f.end()
                    if has_post:
                        q.end()
                    if has_att:
                        half.was_read("oT3")

                phases(v, body)

            @block.scalar
            def _(act):
                act.wait_ge(s_const, 16 * CONST_LOADS)
                act.wait_ge(s_prep, 3)

                def body(name, b, hp, has_front, has_att, has_post):
                    def gates(hp):
                        k, n = place(name, "m3", 2 * b + hp, hp)
                        act.wait_ge(free[k], n)
                        act.activation(buffers(name, hp)[0]["gexp"], VG[:, bass.ds((b + 1) * TB + hp * HT, HT), D:], ACT.Exp, scale=-1.0).then_inc(gate_exp, 1)

                    def tanh(n_gate, job, hp):
                        k, n = place(name, job, 2 * b + hp, hp)
                        act.wait_ge(full[k], n)
                        if name != "tail":
                            act.wait_ge(c_ready, it - 1)
                        act.activation(buffers(name, hp)[1]["tg"][:, n_gate], ps[:, k], ACT.Tanh, bias=bg3[:, n_gate:n_gate + 1],
                                       scale=(0.5 if n_gate < 2 else 1.0)).then_inc(free[k], 1)

                    if name == "lead":
                        def copy(job, hp, to, sem):
                            k, n = place(name, job, 0, hp)
                            act.wait_ge(full[k], n)
                            act.activation(to, ps[:, k], ACT.Copy).then_inc(free[k] if sem is None else sem, 1)

                        copy("xT", 0, FRONT["xnT"], None)
                        copy("xT", 1, FRONT2["xnT"], None)
                        for n in range(2):
                            F = buffers(name, n)[0]
                            k, m = place(name, "m3", 0, n)
                            act.wait_ge(free[k], m)
                            act.activation(F["sq"], F["qk"], ACT.Square).then_inc(lead_squares, 1)
                            gates(n)
                        for n in range(2):
                            for a in range(2):
                                copy("qk"[a], n, buffers(name, n)[0]["split"][:, 0, a], lead_splits)
                        return
                    if name == "tail":
                        act.wait_ge(c_ready, 2 * B - 1)
                        for n in range(2):
                            for g, job in enumerate("fig"):
                                tanh(g, job, n)
                        return
                    it = 2 * b + hp
                    for slot in range(SLOTS):
                        if has_att:
                            for pair in range(2):
                                n = 2 * slot + pair
                                act.wait_ge(scores_ready, 2 * SLOTS * it + n + 1)
                                if pair == 0 and n >= PROBS:
                                    act.wait_ge(probs_used, SLOTS * it + (n - PROBS) // 2 + 1)
                                act.activation(prob[:, n % PROBS], S[:, n % 2], ACT.Exp).then_inc(probs_ready, 1)
                        if has_front and slot == GATES_AT:
                            gates(hp)
                        for g, job in enumerate("fig"):
                            if has_post and slot == TANH_AT[g]:
                                tanh(g, job, hp)

                phases(act, body)

            @block.tensor
            def _(pe):
                pe.wait_ge(s_const, 16 * CONST_LOADS)
                shifted = None

                def load_flag():
                    nonlocal shifted
                    pe.wait_ge(s_prep, 5)
                    shifted = pe.value_load(shift_flag[0:1, 0:1], min_val=0, max_val=1)

                class Half:

                    def __init__(self, name, b, hp):
                        self.name, self.b, self.hp, self.it = name, b, hp, 2 * b + hp
                        self.front, self.post = buffers(name, hp)

                    def bank(self, job):
                        k, n = place(self.name, job, self.it, self.hp)
                        if not (isinstance(n, int) and n == 1):
                            pe.wait_ge(free[k], n - 1)
                        return k

                    def transposed(self, job, src):
                        k = self.bank(job)
                        for t in range(HT):
                            mm = pe.transpose(ps[:, k, t * P:(t + 1) * P], src(t), ident)
                        mm.then_inc(full[k], 1)

                    def was_read(self, job):
                        k, n = place(self.name, job, self.it, self.hp)
                        pe.wait_ge(free[k], n)

                    def x_transpose(self):
                        pe.wait_ge(xn_ready, self.it + 3)
                        self.transposed("xT", lambda t: self.front["xn"][:, t])

                    def project(self, u):
                        if u == 0:
                            self.was_read("xT")
                        k = self.bank(f"m{u}")
                        pe.matmul(ps[:, k, 0:W0], self.front["xnT"][:, u * P:(u + 1) * P], wqkvg[:], start=True, stop=True).then_inc(full[k], 1)

                    def qk_transpose(self, a):
                        pe.wait_ge(qkn_ready, self.it + 3)
                        self.transposed("qk"[a], lambda t: self.front["qk"][:, t, a * D:(a + 1) * D])

                    def att_transpose(self):
                        if self.name == "tail":
                            pe.wait_ge(post_steps, (2 * B - 2) * POST_STEPS + 1 + self.hp * (LN_STEPS + 2))
                        else:
                            pe.wait_ge(post_steps, (self.it - 2) * POST_STEPS + 1)
                        self.transposed("attT", lambda t: self.post["att"][:, t])

                    def project_out(self):
                        self.was_read("attT")
                        k = self.bank("wo")
                        for t in range(HT):
                            mm = pe.matmul(ps[:, k, t * P:(t + 1) * P], self.post["attT"][:, t * P:(t + 1) * P], wo0[:], start=True, stop=True)
                        mm.then_inc(full[k], 1)

                    def x1_transpose(self):
                        pe.wait_ge(x1n_ready, self.it - 1)
                        self.transposed("x1T", lambda t: self.post["x1n"][:, t])

                    def gate_x(self, g):
                        if g == 0:
                            self.was_read("x1T")
                            pe.wait_ge(c_ready, 2 * B - 1 if self.name == "tail" else self.it - 1)
                        k = self.bank("fig"[g])
                        pe.matmul(ps[:, k], wg3[:, g], xn1T[:, bass.ds(((self.b - 1) * 2 + self.hp) * HN, HN)], start=True, stop=False)

                    def gate_c(self, g):
                        k, _ = place(self.name, "fig"[g], self.it, self.hp)
                        pe.matmul(ps[:, k], ug3[:, g], C2[:, bass.ds(self.hp * HN, HN)], start=False, stop=True).then_inc(full[k], 1)

                last = [Half("tail", B, n) for n in range(2)]

                def body(name, b, hp, has_front, has_att, has_post):
                    if name == "lead":
                        both = [Half(name, b, n) for n in range(2)]
                        for half in both:
                            half.x_transpose()
                        for half in both:
                            for u in range(HT):
                                half.project(u)
                        for half in both:
                            half.qk_transpose(0)
                            half.qk_transpose(1)
                        pe.wait_ge(s_prep2, 4)
                        pe.matmul(ps[:, 0, 0:2 * D], wq1[:], fmq[:], start=True, stop=True).then_inc(s_prep_pe, 1)
                        pe.matmul(ps[:, 1, 0:2 * D], wk1[:], fmk[:], start=True, stop=True).then_inc(s_prep_pe, 1)
                        pe.wait_ge(s_prep2, 8)
                        load_flag()
                        return
                    if name == "tail":
                        one, two = last
                        two.att_transpose()
                        one.gate_x(0)
                        two.project_out()
                        one.gate_c(0)
                        for g in (1, 2):
                            one.gate_x(g)
                            one.gate_c(g)
                        two.x1_transpose()
                        for g in range(3):
                            two.gate_x(g)
                            two.gate_c(g)
                        return
                    it = 2 * b + hp
                    half = Half(name, b, hp)
                    early = name == "shrink" and hp == 1

                    def out_transpose(unit):
                        pe.wait_ge(o_copied, 4 * it + unit + 1)
                        qh = unit % 2
                        k = half.bank(f"oT{unit}")
                        for t in range(HT):
                            mm = pe.transpose(ps[:, k, t * P:(t + 1) * P], OT[:, qh, t * P:(t + 1) * P], ident)
                        mm.then_inc(full[k], 1)

                    def side(job):
                        if job == "attT":
                            half.att_transpose()
                        elif job == "wo":
                            half.project_out()
                        elif job == "x1T":
                            half.x1_transpose()
                        elif job == "xT":
                            half.x_transpose()
                        elif job[0] == "m":
                            half.project(int(job[1]))
                        elif job in ("q", "k"):
                            half.qk_transpose("qk".index(job))
                        elif job[:2] == "oT":
                            out_transpose(int(job[2]))
                        elif job[1:] == "_state":
                            half.gate_c("fig".index(job[0]))
                        else:
                            half.gate_x("fig".index(job))

                    beside = side_jobs(has_front, has_att, has_post)

                    def all_scores(i):
                        with pe.If(shifted != 0):
                            with pe.Fori(0, HG) as j:
                                with pe.Fori(0, TB // 2) as t:
                                    for u in range(2):
                                        n = j * TB + 2 * t + u
                                        pe.wait_ge(max_taken, 1 + (2 * it + i) * HG * TB + (2 * t + j * TB))
                                        if u == 0 and i:
                                            pe.wait_ge(probs_ready, 2 * SLOTS * it + SLOTS * i)
                                        for half in range(2):
                                            mm = pe.matmul(S[:, u, half], Q_st[0:SHIFT_ROW, i, j, bass.ds((2 * t + u) * P, P)],
                                                           K_st[0:SHIFT_ROW, i, j, half * HN:(half + 1) * HN], start=True, stop=True)
                                        mm.then_inc(max_scores, 1)
                            pe.wait_ge(max_taken, 1 + (2 * it + i + 1) * HG * TB)
                            pe.transpose(ps[0:HG * TB, 0, 0:P], row_max[:], ident).then_inc(max_turned, 1)
                            pe.wait_ge(shift_loaded, 16 * (2 * it + i + 1))

                    def scores(n):
                        i, m = n // (2 * 2 * TB), n % (2 * 2 * TB)
                        qh, kt, pair = m // (2 * TB), (m // 2) % TB, m % 2
                        if m == 0:
                            pe.wait_ge(loaded[i], LOADS * (it + 1))
                            all_scores(i)
                        if n >= 2:
                            pe.wait_ge(probs_ready, 2 * SLOTS * it + n - 1)
                        for j in range(2):
                            mm = pe.matmul(S[:, n % 2, j], K_st[:, i, 2 * pair + j, kt * P:(kt + 1) * P],
                                           Q_st[:, i, 2 * pair + j, qh * HN:(qh + 1) * HN], start=True, stop=True)
                        mm.then_inc(scores_ready, 1)

                    def values(slot):
                        i, qh, kt = slot // (2 * TB), (slot // TB) % 2, slot % TB
                        if slot % (2 * TB) == 0:
                            pe.wait_ge(v_staged[i], it + 1)
                        if kt == 0 and slot >= 2 * TB:
                            pe.wait_ge(o_copied, 4 * it + slot // TB - 1)
                        pe.wait_ge(probs_ready, 2 * SLOTS * it + 2 * slot + 2)
                        for j in range(HG):
                            mm = pe.matmul(O[VW * j:VW * (j + 1), qh], V_st[:, i, kt, j], prob[:, (2 * slot + j // 2) % PROBS, j % 2],
                                           start=(kt == 0), stop=(kt == TB - 1))
                        mm.then_inc(probs_used, 1)

                    if has_att:
                        scores(0)
                        scores(1)
                    for slot in range(SLOTS):
                        if has_att:
                            if slot < SLOTS - 1:
                                scores(2 * slot + 2)
                            if slot:
                                values(slot - 1)
                        for at, job in beside:
                            if at == slot:
                                side(job)
                        if early and slot == EARLY[0]:
                            last[0].att_transpose()
                        if early and slot == EARLY[1]:
                            last[0].project_out()
                        if has_att and slot < SLOTS - 1:
                            scores(2 * slot + 3)
                    if has_att:
                        values(SLOTS - 1)
                        side("oT3")
                        if early:
                            last[0].x1_transpose()

                phases(pe, body)

        with ExitStack() as part:
            def pb(name, shape, dt=F32):
                return part.enter_context(nc.sbuf_tensor(name, shape, dt))

            w1 = pb("w1", [D, E, F])
            w2 = pb("w2", [P, E, FT, D])
            b1 = pb("b1", [P, E, FT])
            b2 = pb("b2", [E, D])
            hT = pb("hT", [D, HN])
            xn2 = pb("xn2", [P, HT, D])
            xn2T = pb("xn2T", [D, HN])
            Qf = pb("Qf", [P, G1, HN])
            Kf = pb("Kf", [P, G1, HN])
            Qbd = pb("Qbd", [P, G1, HG, HN])
            V1 = pb("V1", [P, HT, H1, VW])
            Kt = pb("Kt", [P, G1, HT, P])
            Am = pb("Am", [P, 2, G1, HG, P])
            state = pb("state", [P, 2, G1, P])
            oT1 = pb("oT1", [P, HT, G1, P])
            sq1 = pb("sq1", [P, HT, H1, DK])
            rr1 = pb("rr1", [P, 4, HT * H1])
            on = pb("on", [P, HT, D])
            onT = pb("onT", [D, HN])
            xn3 = pb("xn3", [P, HT, D])
            x3s = pb("x3s", [D, HN])
            sg = pb("sg", [P, HT, E])
            pairs = pb("pairs", [P, 2, HT * E, E])
            combT = pb("combT", [E, HN])
            comb = pb("comb", [P, 2, HT, E])
            w1_parts = pb("w1_parts", [D, 2, E, F], F22)
            x3_parts = pb("x3_parts", [D, 2, 2, HN], F22)
            high = pb("high", [P, HN])
            hid = pb("hid", [P, 2, FT, HN])
            w1_high_bits = hid[:].rearrange("p a f t -> p (a f t)").rearrange("p (e f) -> p e f", e=E)
            block = part.enter_context(nc.Block())

            def halves(eng, body):
                for phase, b0, count, parts in LATE_PHASES:
                    if count == 1:
                        for tag, hf, has_linear, has_experts in parts:
                            body(phase, b0, tag, hf, has_linear, has_experts)
                    else:
                        with eng.Fori(b0, b0 + count) as b:
                            for tag, hf, has_linear, has_experts in parts:
                                body(phase, b, tag, hf, has_linear, has_experts)

            def half_of(b, tag, hf, phase):
                return 2 * b + (2 if phase == "middle" and hf == 0 else hf)

            def wait_full(eng, phase, job, i):
                k, n = banks.at(phase, job, i)
                eng.wait_ge(full[k], n)
                return k

            def wait_free(eng, phase, job, i, before=0):
                k, n = banks.at(phase, job, i)
                if not (isinstance(n, int) and n == before):
                    eng.wait_ge(free[k], n - before)
                return k

            @block.sync
            def _(sp):
                for dst, src in ((w1[:], w_1), (w2[:], w_2), (b1[:], b_1), (b2[:], b_2)):
                    sp.dma_start(dst, src).then_inc(we_loaded, 16)

                def store(phase, b, tag, hf, has_linear, has_experts):
                    if has_experts:
                        m = half_of(b, tag, hf, phase) - 1
                        wait_free(sp, phase, f"down{E - 1}{tag}", b)
                        sp.dma_start(out[bass.ds(m * HN, HN), :].rearrange("(t p) d -> p t d", p=P), X[:, bass.ds(m * HT, HT)]).then_inc(stored, 16)

                halves(sp, store)
                sp.wait_ge(stored, 16 * 2 * B)

            @block.gpsimd
            def _(pool):
                pool.memset(Qbd[:], 0.0).then_inc(late_zeros, 1)
                pool.wait_ge(late_zeros, 1)
                pool.memset(V1[:], 0.0).then_inc(late_zeros, 1)
                pool.wait_ge(late_zeros, 2)
                for e in range(E):
                    pool.wait_ge(w1_high, e + 1)
                    pool.tensor_copy(w1_parts[:, 0, e], w1_high_bits[:, e]).then_inc(w1_split, 1)
                    pool.wait_ge(w1_split, 2 * e + 1)
                    pool.tensor_tensor(w1_parts[:, 1, e], w1[:, e], w1_high_bits[:, e], ALU.subtract).then_inc(w1_split, 1)
                    pool.wait_ge(w1_split, 2 * e + 2)

            @block.vector
            def _(v):
                def body(phase, b, tag, hf, has_linear, has_experts):
                    h = half_of(b, tag, hf, phase)
                    s = Steps(v, l1_steps, h * L1_STEPS, L1_STEPS)
                    m = Steps(v, moe_steps, (h - 1) * MOE_STEPS, MOE_STEPS)
                    X4 = X[:, bass.ds(h * HT, HT)] if has_linear else None
                    XE = X[:, bass.ds((h - 1) * HT, HT)] if has_experts else None

                    def product(job):
                        return wait_full(v, phase, job + tag, b)

                    def was_read(job):
                        wait_free(v, phase, job + tag, b)

                    if has_experts:
                        v.wait_ge(l1_steps, h * L1_STEPS)
                    for job in late_order(has_linear, has_experts):
                        if job == "hT":
                            k = product("hT")
                            v.tensor_tensor(X4, ps[:, k].rearrange("p (t d) -> p t d", t=HT), X4, ALU.add).then_inc(free[k], 1)
                            was_read("hT")
                            layernorm(v, s, xn2[:], X4, st, work, xn2_ready)
                        elif job == "x2T":
                            k = product("x2T")
                            v.tensor_copy(xn2T[:], ps[:, k]).then_inc(free[k], 1)
                        elif job == "kf1":
                            was_read("qf0")
                            was_read("qf1")
                            v.wait_ge(late_zeros, 2)
                            for j in range(HG):
                                rows = slice(DF * j, DF * (j + 1))
                                ins = v.tensor_copy(Qbd[rows, :, j], Qf[rows])
                            ins.then_inc(qbd_ready, 1)
                        elif job == "v":
                            k = product("v")
                            v.tensor_copy(V1[:, :, :, 0:DK], ps[:, k].rearrange("p (t h d) -> p t h d", t=HT, h=H1)).then_inc(free[k], 1)
                        elif job[0] == "A":
                            c, g = int(job[1]), int(job[2])
                            k = product(job)
                            v.tensor_tensor(Am[:, c % 2, g], ps[:, k].rearrange("p (j q) -> p j q", j=HG), causal.unsqueeze(1).to_broadcast([P, HG, P]),
                                            ALU.mult).then_inc(free[k], 1)
                            if phase == "start":
                                e = G1 * c + g
                                v.wait_ge(we_loaded, 64)
                                v.tensor_scalar(w1_high_bits[:, e].bitcast(I32), w1[:, e].bitcast(I32), HIGH_BITS, None, ALU.bitwise_and).then_inc(w1_high, 1)
                        elif job[0] == "S":
                            c = int(job[1])
                            k = product(job)
                            v.tensor_tensor(state[:, (c + 1) % 2], ps[:, k, 0:G1 * P].rearrange("p (g v) -> p g v", g=G1),
                                            blocks.unsqueeze(1).to_broadcast([P, G1, P]), ALU.mult).then_inc(free[k], 1)
                        elif job == "on1":
                            v.wait_ge(squared1, 2 * h + 2)
                            s.did(v.tensor_reduce(rr1[:, 1], sq1[:].rearrange("p t h d -> p (t h) d"), AX_X, ALU.add))
                            s.did(v.tensor_scalar(rr1[:, 0], rr1[:, 1], 1.0 / DK, RMS1_EPS, ALU.mult, ALU.add))
                            rsqrt(v, s, rr1[:, 3], rr1[:, 0], rr1[:, 1], rr1[:, 2])
                            for a in range(2):
                                k = product(f"on{a}")
                                for c in range(2):
                                    ins = v.tensor_tensor(on[:, 2 * a + c].rearrange("p (h d) -> p h d", h=H1),
                                                          ps[:, k, 2 * c * P:2 * (c + 1) * P].rearrange("p (h d) -> p h d", h=H1)[:, :, 0:DK],
                                                          rr1[:, 3, (2 * a + c) * H1:(2 * a + c + 1) * H1].unsqueeze(2).to_broadcast([P, H1, DK]), ALU.mult)
                                ins.then_inc(free[k], 1)
                        elif job == "onT":
                            k = product("onT")
                            v.tensor_copy(onT[:], ps[:, k]).then_inc(free[k], 1)
                        elif job == "wo1":
                            k = product("wo1")
                            v.tensor_tensor(X4, ps[:, k].rearrange("p (t d) -> p t d", t=HT), X4, ALU.add).then_inc(free[k], 1)
                            was_read("wo1")
                            layernorm(v, s, xn3[:], X4, st, work, xn3_ready)
                        elif job == "x3T":
                            k = product("x3T")
                            v.tensor_copy(x3s[:], ps[:, k]).then_inc(free[k], 1)
                            was_read("x3T")
                            s.did(v.tensor_scalar(high[:].bitcast(I32), x3s[:].bitcast(I32), HIGH_BITS, None, ALU.bitwise_and))
                            s.go(v.tensor_copy(x3_parts[:, hf, 0], high[:]))
                            s.did(v.tensor_tensor(x3_parts[:, hf, 1], x3s[:], high[:], ALU.subtract))
                        elif job == "gate":
                            was_read("gate")
                            s.did(v.tensor_scalar(sg[:], sg[:], 1.0, None, ALU.add))
                            s.did(v.reciprocal(sg[:], sg[:]))
                            for t in range(HT):
                                mine = sg[:, t].unsqueeze(2).to_broadcast([P, E, E])
                                other = sg[:, t].unsqueeze(1).to_broadcast([P, E, E])
                                s.go(v.tensor_tensor(pairs[:, 0, t * E:(t + 1) * E], other, mine, ALU.is_gt))
                                s.go(v.tensor_tensor(pairs[:, 1, t * E:(t + 1) * E], other, mine, ALU.is_equal))
                            s.wait()
                            p4 = pairs[:, 1].rearrange("p (t e) f -> p t e f", t=HT)
                            s.did(v.tensor_tensor(p4, p4, before.unsqueeze(1).to_broadcast([P, HT, E, E]), ALU.mult))
                            s.did(v.tensor_tensor(pairs[:, 0], pairs[:, 0], pairs[:, 1], ALU.add))
                            s.did(v.tensor_reduce(rr1[:, 0], pairs[:, 0], AX_X, ALU.add))
                            s.go(v.scalar_tensor_tensor(comb[:, hf].rearrange("p t e -> p (t e)"), rr1[:, 0], 2.0,
                                                        sg[:].rearrange("p t e -> p (t e)"), ALU.is_lt, ALU.mult))
                            s.end()
                        elif job == "cT":
                            k = product("cT")
                            v.tensor_copy(combT[:], ps[0:E, k]).then_inc(free[k], 1)
                        elif job == "b2":
                            k = product("b2")
                            v.tensor_tensor(XE, ps[:, k].rearrange("p (t d) -> p t d", t=HT), XE, ALU.add).then_inc(free[k], 1)
                        elif job[:4] == "down" and int(job[-1]) == HT - 1:
                            e = int(job[4])
                            k = product(f"down{e}")
                            if e:
                                m.wait()
                            was_read(f"down{e - 1}" if e else "b2")
                            for t in range(HT):
                                row = X[:, (h - 1) * HT + t]
                                ins = v.scalar_tensor_tensor(row, ps[:, k, t * D:(t + 1) * D], comb[:, 1 - hf, t, e:e + 1], row, ALU.mult, ALU.add)
                                if t < HT - 1:
                                    m.go(ins)
                            ins.then_inc(free[k], 1)
                            if e == E - 1:
                                was_read(f"down{e}")
                                m.end()

                halves(v, body)

            @block.scalar
            def _(act):
                act.wait_ge(s_prep2, 8)

                def body(phase, b, tag, hf, has_linear, has_experts):
                    for job in late_order(has_linear, has_experts):
                        if job == "h":
                            k = wait_full(act, phase, job + tag, b)
                            act.activation(hT[:], ps[:, k], ACT.Tanh, bias=bh[:]).then_inc(free[k], 1)
                        elif job[1:2] == "f":
                            a, dst, g = (0, Qf, int(job[2])) if job[0] == "q" else (1, Kf, int(job[2]))
                            k = wait_full(act, phase, job + tag, b)
                            act.activation(dst[:, g], ps[:, k], ACT.Exp, bias=fb[:, a:a + 1]).then_inc(free[k], 1)
                        elif job[:2] == "kt":
                            k = wait_full(act, phase, job + tag, b)
                            act.activation(Kt[:, int(job[2])].rearrange("p c f -> p (c f)"), ps[:, k], ACT.Copy).then_inc(free[k], 1)
                        elif job in ("outer1", "outer3"):
                            a = int(job[-1]) // 2
                            k = wait_full(act, phase, f"O{a}{tag}", b)
                            act.activation(oT1[:, 2 * a:2 * a + 2].rearrange("p c g t -> p (c g t)"), ps[:, k], ACT.Copy).then_inc(free[k], 1)
                        elif job in ("on0", "on1"):
                            a = int(job[-1])
                            k = wait_full(act, phase, job + tag, b)
                            for c in range(2):
                                ins = act.activation(sq1[:, 2 * a + c], ps[:, k, 2 * c * P:2 * (c + 1) * P].rearrange("p (h d) -> p h d", h=H1)[:, :, 0:DK], ACT.Square)
                            ins.then_inc(squared1, 1)
                        elif job == "gate":
                            k = wait_full(act, phase, job + tag, b)
                            act.activation(sg[:].rearrange("p t e -> p (t e)"), ps[:, k, 0:HT * E], ACT.Exp, scale=-1.0).then_inc(free[k], 1)
                        elif job[:2] == "up":
                            e, f = int(job[2]), int(job[3])
                            k = wait_full(act, phase, job + tag, b)
                            if e >= 2 and f == 0:
                                wait_full(act, phase, f"down{e - 2}{tag}", b)
                            if phase == "middle" and tag and e == 0 and f == 0:
                                act.wait_ge(we_loaded, 64)
                            act.activation(hid[:, e % 2, f], ps[:, k], ACT.Gelu_apprx_tanh, bias=b1[:, e, f:f + 1]).then_inc(free[k], 1)

                halves(act, body)

            @block.tensor
            def _(pe):
                pe.wait_ge(s_prep2, 8)

                def body(phase, b, tag, hf, has_linear, has_experts):
                    h = half_of(b, tag, hf, phase)

                    def bank(job):
                        return wait_free(pe, phase, job + tag, b, 1)

                    def was_read(job):
                        wait_free(pe, phase, job + tag, b)

                    def transposed(job, src):
                        k = bank(job)
                        for t in range(HT):
                            mm = pe.transpose(ps[:, k, t * P:(t + 1) * P], src(t), ident)
                        mm.then_inc(full[k], 1)

                    def by_tile(job, src, w, width=D):
                        k = bank(job)
                        for t in range(HT):
                            mm = pe.matmul(ps[:, k, t * width:(t + 1) * width], src[:, t * P:(t + 1) * P], w[:], start=True, stop=True)
                        mm.then_inc(full[k], 1)

                    def outer(c):
                        first = hf == 0 and c == 0
                        k = banks.at(phase, f"O{c // 2}{tag}", b)[0]
                        if c % 2 == 0:
                            bank(f"O{c // 2}")
                        if c:
                            was_read(f"S{c - 1}")
                        was_read(f"A{c}1")
                        for g in range(G1):
                            cols = slice(((c % 2) * G1 + g) * P, ((c % 2) * G1 + g + 1) * P)
                            if not first:
                                pe.matmul(ps[:, k, cols], state[:, c % 2, g], Qf[:, g, c * P:(c + 1) * P], start=True, stop=False, skip_group_check=True)
                            for j in range(HG):
                                mm = pe.matmul(ps[VW * j:VW * (j + 1), k, cols], V1[:, c, HG * g + j], Am[:, c % 2, g, j], start=first, stop=True,
                                               skip_group_check=True)
                        if c % 2:
                            mm.then_inc(full[k], 1)

                    for job in late_order(has_linear, has_experts):
                        if job == "h":
                            k = bank("h")
                            pe.matmul(ps[:, k], wh[:], xn1T[:, bass.ds(h * HN, HN)], start=True, stop=False)
                            pe.matmul(ps[:, k], uh[:], C2[:, hf * HN:(hf + 1) * HN], start=False, stop=True).then_inc(full[k], 1)
                        elif job == "hT":
                            was_read("h")
                            transposed("hT", lambda t: hT[:, t * P:(t + 1) * P])
                        elif job == "x2T":
                            pe.wait_ge(xn2_ready, h + 1)
                            transposed("x2T", lambda t: xn2[:, t])
                        elif job[1:2] == "f":
                            if job == "qf0":
                                was_read("x2T")
                            k = bank(job)
                            g = int(job[2])
                            pe.matmul(ps[:, k], (wqf if job[0] == "q" else wkf)[:, g * P:(g + 1) * P], xn2T[:], start=True, stop=True).then_inc(full[k], 1)
                        elif job == "v":
                            by_tile("v", xn2T, wv1)
                        elif job[:2] == "kt":
                            g = int(job[2])
                            was_read(f"kf{g}")
                            transposed(job, lambda t: Kf[:, g, t * P:(t + 1) * P])
                        elif job[0] == "A":
                            c, g = int(job[1]), int(job[2])
                            if c == 0 and g == 0:
                                pe.wait_ge(qbd_ready, h + 1)
                            k = bank(job)
                            pe.matmul(ps[:, k], Kf[:, g, c * P:(c + 1) * P], Qbd[:, g, :, c * P:(c + 1) * P], start=True, stop=True).then_inc(full[k], 1)
                        elif job[:5] == "outer":
                            if job == "outer0":
                                was_read("v")
                                was_read("kt0")
                                was_read("kt1")
                            outer(int(job[5]))
                        elif job[0] == "S":
                            c = int(job[1])
                            k = bank(job)
                            for g in range(G1):
                                mm = pe.matmul(ps[:, k, g * P:(g + 1) * P], Kt[:, g, c], V1[:, c, HG * g:HG * (g + 1)].rearrange("p j v -> p (j v)"),
                                               start=(hf == 0 and c == 0 and g == 0), stop=True, skip_group_check=True)
                            mm.then_inc(full[k], 1)
                        elif job in ("on0", "on1"):
                            a = int(job[2])
                            was_read(f"O{a}")
                            k = bank(job)
                            for c in range(2):
                                for g in range(G1):
                                    mm = pe.transpose(ps[:, k, (2 * c + g) * P:(2 * c + g + 1) * P], oT1[:, 2 * a + c, g], ident)
                            mm.then_inc(full[k], 1)
                        elif job == "onT":
                            was_read("on0")
                            was_read("on1")
                            transposed("onT", lambda t: on[:, t])
                        elif job == "wo1":
                            was_read("onT")
                            by_tile("wo1", onT, wo1)
                        elif job == "x3T":
                            pe.wait_ge(xn3_ready, h + 1)
                            transposed("x3T", lambda t: xn3[:, t])
                        elif job == "gate":
                            was_read("x3T")
                            by_tile("gate", x3s, wg, E)
                        elif job == "cT":
                            pe.wait_ge(l1_steps, h * L1_STEPS)
                            k = bank("cT")
                            for t in range(HT):
                                mm = pe.transpose(ps[0:E, k, t * P:(t + 1) * P], comb[:, 1 - hf, t], ident)
                            mm.then_inc(full[k], 1)
                        elif job == "b2":
                            was_read("cT")
                            if phase == "middle" and tag:
                                pe.wait_ge(we_loaded, 64)
                            by_tile("b2", combT, b2)
                        elif job[:2] == "up":
                            e, f = int(job[2]), int(job[3])
                            k = bank(job)
                            if phase == "middle" and tag == "'" and e == 0 and f == 0:
                                pe.wait_ge(w1_split, 2 * E)
                            for a, b_part in ((0, 0), (0, 1), (1, 0)):
                                mm = pe.matmul(ps[:, k], w1_parts[:, a, e, f * P:(f + 1) * P], x3_parts[:, 1 - hf, b_part],
                                               start=(a == 0 and b_part == 0), stop=(a == 1))
                            mm.then_inc(full[k], 1)
                        elif job[:4] == "down":
                            e, t = int(job[4]), int(job[5])
                            k = banks.at(phase, f"down{e}{tag}", b)[0]
                            if t == 0:
                                bank(f"down{e}")
                                was_read(f"up{e}{FT - 1}")
                            for f in range(FT):
                                mm = pe.matmul(ps[:, k, t * D:(t + 1) * D], hid[:, e % 2, f, t * P:(t + 1) * P], w2[:, e, f], start=(f == 0), stop=(f == FT - 1))
                            if t == HT - 1:
                                mm.then_inc(full[k], 1)

                halves(pe, body)


def _layout(np, a):
    def diagonal(w):
        o = np.zeros((H1, DK, H1, 2, DK), w.dtype)
        for h in range(H1):
            for sign in range(2):
                o[h, :, h, sign, :] = w.T
        return o.reshape(D, 2 * D)

    def interleaved(w):
        return w.reshape(-1, NG, HG, HD).swapaxes(2, 3).reshape(w.shape)

    wq, bq = a["L0_attn_Wq"], a["L0_attn_bq"]
    consts = np.zeros((P, NCONST), np.float32)
    consts[:, 0:P] = np.eye(P)
    consts[:, P:2 * P] = np.triu(np.ones((P, P)))
    consts[:, 2 * P:3 * P] = np.kron(np.eye(HG), np.ones((VW, VW)))
    consts[:, 3 * P:5 * P] = np.tile(np.repeat([1.0, -1.0], DK), 2 * HG)
    consts[:, 5 * P:5 * P + E * E] = np.tril(np.ones((E, E)), -1).reshape(E * E)
    consts[:, 5 * P + E * E] = np.tile(np.repeat([1.0, -1.0], DK), HG)
    return dict(
        x=a["L0_attn_x"].reshape(NT * P, D),
        w_qkvg=np.concatenate([interleaved(wq[:, :D]), interleaved(a["L0_attn_Wk"]), a["L0_attn_Wv"], wq[:, D:]], 1),
        b_qkvg=np.concatenate([interleaved(bq[:D]), interleaved(a["L0_attn_bk"]), a["L0_attn_bv"], bq[D:]]),
        qn_w=np.tile(np.repeat(a["L0_attn_qn_w"], HG), NG), kn_w=np.tile(np.repeat(a["L0_attn_kn_w"], HG), NG),
        w_o0=a["L0_attn_Wo"], b_o0=a["L0_attn_bo"],
        w_gates=np.stack([a["L0_ffn_w" + c].T for c in "fic"], 1),
        u_gates=np.stack([a["L0_ffn_u" + c].T for c in "fic"], 1),
        b_gates=np.stack([a["L0_ffn_b" + c] for c in "fic"], 1),
        w_h=a["L0_ffn_wo"].T, u_h=a["L0_ffn_uo"].T, b_h=a["L0_ffn_bo"].reshape(D, 1), c_in=a["L0_ffn_in_c"].reshape(D, 1),
        w_q1=a["L1_attn_Wq"], w_k1=a["L1_attn_Wk"], w_v1=a["L1_attn_Wv"].T, w_o1=a["L1_attn_Wo"].T,
        fm_q=diagonal(a["L1_attn_fmq_w"]), fm_k=diagonal(a["L1_attn_fmk_w"]),
        fb_q=np.tile(a["L1_attn_fmq_b"], H1).reshape(D, 1), fb_k=np.tile(a["L1_attn_fmk_b"], H1).reshape(D, 1),
        rms_w=np.tile(a["L1_attn_rms_w"], H1).reshape(D, 1),
        w_g=a["L1_ffn_Wg"], w_1=a["L1_ffn_W1"].transpose(1, 0, 2), b_1=a["L1_ffn_b1"].reshape(E, FT, P).transpose(2, 0, 1),
        w_2=a["L1_ffn_W2"].reshape(E, FT, P, D).transpose(2, 0, 1, 3), b_2=a["L1_ffn_b2"],
        consts=consts,
    )


def kernel(**inputs):
    import numpy as _np
    import concourse.bacc as _bacc
    from concourse import mybir as _mybir
    from concourse.bass_utils import run_bass_kernel_spmd as _run

    nc = _bacc.Bacc("TRN2", target_bir_lowering=False, num_devices=1)
    laid = _layout(_np, {k: _np.asarray(v) for k, v in inputs.items()})
    arrays, args = {}, {}
    for name, a in laid.items():
        a = _np.ascontiguousarray(a)
        arrays[f"in_{name}"] = a
        args[name] = nc.dram_tensor(f"in_{name}", a.shape, _mybir.dt.from_np(a.dtype), kind="ExternalInput").ap()
    out = nc.dram_tensor("out_rows", (NT * P, D), _mybir.dt.float32, kind="ExternalOutput").ap()
    build(nc, out=out, **args)
    r = _run(nc, [arrays], core_ids=[0])
    return r.results[0]["out_rows"].reshape(B, N, D)
```
